# Optimizing a Trainium2 kernel written in Bass

```python
import numpy as np
import jax
import jax.numpy as jnp

def _softmax(x, axis=-1):
    return jax.nn.softmax(x, axis=axis)

def _gelu(x):
    return jax.nn.gelu(x, approximate=True)

def _silu(x):
    return jax.nn.silu(x)

def _sigmoid(x):
    return jax.nn.sigmoid(x)

def _layernorm(x, axis=-1, eps=1e-05):
    m = jnp.mean(x, axis=axis, keepdims=True)
    v = jnp.var(x, axis=axis, keepdims=True)
    return (x - m) / jnp.sqrt(v + eps)

def _scatter_add(tgt, idx, src, axis=0):
    return tgt.at[idx].add(src)

def _segment_sum(src, seg, n):
    return jax.ops.segment_sum(src, seg, n)
kernel_name = 'mk_hybrid_d1_jaxref_r4_552907'

def setup_inputs(seed: int=0):
    np.random.seed(seed)
    _w = jnp.asarray

    def _L0_attn_a_setup():
        import jax, jax.numpy as jnp
        import numpy as np
        B, L, D = (2, 512, 256)
        H = 16
        DH = D // H
        FACTOR = 0.6
        U = max(1, min(L, int(FACTOR * L)))

        def _split_heads(x):
            b, l, d = x.shape
            return x.reshape(b, l, H, DH).transpose(0, 2, 1, 3)
        key = jax.random.key(seed)
        ks = jax.random.split(key, 9)
        s = 0.02
        return {'x': jax.random.normal(ks[0], (B, L, D), dtype=jnp.float32), 'Wq': jax.random.normal(ks[1], (D, D), dtype=jnp.float32) * s, 'bq': jnp.zeros((D,), dtype=jnp.float32), 'Wk': jax.random.normal(ks[2], (D, D), dtype=jnp.float32) * s, 'bk': jnp.zeros((D,), dtype=jnp.float32), 'Wv': jax.random.normal(ks[3], (D, D), dtype=jnp.float32) * s, 'bv': jnp.zeros((D,), dtype=jnp.float32), 'Wo': jax.random.normal(ks[4], (D, D), dtype=jnp.float32) * s, 'bo': jnp.zeros((D,), dtype=jnp.float32)}
    _L0_attn_a_in = _L0_attn_a_setup()

    def _L0_attn_b_setup():
        import jax, jax.numpy as jnp
        import numpy as np
        D_MODEL = 256
        N_HEADS = 16
        D_K = D_MODEL // N_HEADS
        D_HID = 4 * D_MODEL
        GATE_TEMP = 16.0
        RMS_EPS = 1e-06
        LN_EPS = 1e-05

        def _rmsnorm(x, scale):
            norm = jnp.sqrt(jnp.sum(x * x, axis=-1, keepdims=True))
            rms = norm / np.sqrt(x.shape[-1]).astype(np.float32)
            return x / (rms + RMS_EPS) * scale

        def _silu(x):
            return x * jax.nn.sigmoid(x)

        def _gla(x, wq, wk, wv, wg1, bg1, wg2, bg2, wog, bog, wo):
            xb = jnp.swapaxes(x, 0, 1)
            B, T, C = xb.shape
            H, dk = (N_HEADS, D_K)
            q = (xb @ wq.T).reshape(B, T, H, dk)
            k = (xb @ wk.T).reshape(B, T, H, dk)
            v = (xb @ wv.T).reshape(B, T, H, dk)
            gate_hidden = _silu(xb @ wg1.T + bg1)
            alpha = jax.nn.sigmoid((gate_hidden @ wg2.T + bg2) / GATE_TEMP).reshape(B, T, H, dk)
            qT, kT, vT, aT = (jnp.moveaxis(a, 1, 0) for a in (q, k, v, alpha))
            S0 = jnp.zeros((B, H, dk, dk), xb.dtype)

            def step(S, qkva):
                q_t, k_t, v_t, a_t = qkva
                S = a_t[..., None] * S + k_t[..., :, None] * v_t[..., None, :]
                o_t = jnp.einsum('bhk,bhkv->bhv', q_t, S)
                return (S, o_t)
            S_final, oT = jax.lax.scan(step, S0, (qT, kT, vT, aT))
            o = jnp.moveaxis(oT, 0, 1)
            mu = jnp.mean(o, axis=-1, keepdims=True)
            var = jnp.mean((o - mu) ** 2, axis=-1, keepdims=True)
            o = (o - mu) / jnp.sqrt(var + LN_EPS)
            o = o.reshape(B, T, H * dk)
            out_gate = _silu(xb @ wog.T + bog)
            out = o * out_gate @ wo.T
            return (jnp.swapaxes(out, 0, 1), S_final)

        def _reference_tuple_inner(x, scale1, scale2, wq, wk, wv, wg1, bg1, wg2, bg2, wog, bog, wo, w_gate, w_up, w_down):
            attn_out, new_cache = _gla(_rmsnorm(x, scale1), wq, wk, wv, wg1, bg1, wg2, bg2, wog, bog, wo)
            x = x + attn_out
            normed = _rmsnorm(x, scale2)
            ffn = _silu(normed @ w_gate.T) * (normed @ w_up.T) @ w_down.T
            x = x + ffn
            return (x, new_cache)
        key = jax.random.key(seed)
        ks = jax.random.split(key, 20)
        s = 0.02

        def w(k, shape):
            return jax.random.normal(k, shape, dtype=jnp.float32) * s
        inp = {'x': jax.random.normal(ks[0], (512, 4, D_MODEL), dtype=jnp.float32), 'scale1': jnp.ones((D_MODEL,), jnp.float32), 'scale2': jnp.ones((D_MODEL,), jnp.float32), 'wq': w(ks[1], (D_MODEL, D_MODEL)), 'wk': w(ks[2], (D_MODEL, D_MODEL)), 'wv': w(ks[3], (D_MODEL, D_MODEL)), 'wg1': w(ks[4], (16, D_MODEL)), 'bg1': jnp.zeros((16,), jnp.float32), 'wg2': w(ks[5], (D_MODEL, 16)), 'bg2': jnp.zeros((D_MODEL,), jnp.float32), 'wog': w(ks[6], (D_MODEL, D_MODEL)), 'bog': jnp.zeros((D_MODEL,), jnp.float32), 'wo': w(ks[7], (D_MODEL, D_MODEL)), 'w_gate': w(ks[8], (D_HID, D_MODEL)), 'w_up': w(ks[9], (D_HID, D_MODEL)), 'w_down': w(ks[10], (D_MODEL, D_HID))}
        return inp
    _L0_attn_b_in = _L0_attn_b_setup()

    def _L0_ffn_setup():
        import jax, jax.numpy as jnp
        import numpy as np
        IN_F, OUT_F, BLOCK, NBLK = (256, 1024, 64, 16)
        TOPK = NBLK // 4
        key = jax.random.key(seed)
        ks = jax.random.split(key, 7)
        s = 1.0 / np.sqrt(IN_F)
        s2 = 1.0 / np.sqrt(OUT_F)
        return {'x': jax.random.normal(ks[0], (4, 1024, IN_F), jnp.float32), 'router_w': jax.random.uniform(ks[1], (NBLK, IN_F), jnp.float32, -s, s), 'router_b': jax.random.uniform(ks[2], (NBLK,), jnp.float32, -s, s), 'w1': jax.random.uniform(ks[3], (OUT_F, IN_F), jnp.float32, -s, s), 'b1': jax.random.uniform(ks[4], (OUT_F,), jnp.float32, -s, s), 'w2': jax.random.uniform(ks[5], (IN_F, OUT_F), jnp.float32, -s2, s2), 'b2': jax.random.uniform(ks[6], (IN_F,), jnp.float32, -s2, s2)}
    _L0_ffn_in = _L0_ffn_setup()
    _d = {'L0_attn_a_x': _L0_attn_a_in['x'], 'L0_attn_a_Wq': _L0_attn_a_in['Wq'], 'L0_attn_a_bq': _L0_attn_a_in['bq'], 'L0_attn_a_Wk': _L0_attn_a_in['Wk'], 'L0_attn_a_bk': _L0_attn_a_in['bk'], 'L0_attn_a_Wv': _L0_attn_a_in['Wv'], 'L0_attn_a_bv': _L0_attn_a_in['bv'], 'L0_attn_a_Wo': _L0_attn_a_in['Wo'], 'L0_attn_a_bo': _L0_attn_a_in['bo'], 'L0_attn_b_scale1': _L0_attn_b_in['scale1'], 'L0_attn_b_scale2': _L0_attn_b_in['scale2'], 'L0_attn_b_wq': _L0_attn_b_in['wq'], 'L0_attn_b_wk': _L0_attn_b_in['wk'], 'L0_attn_b_wv': _L0_attn_b_in['wv'], 'L0_attn_b_wg1': _L0_attn_b_in['wg1'], 'L0_attn_b_bg1': _L0_attn_b_in['bg1'], 'L0_attn_b_wg2': _L0_attn_b_in['wg2'], 'L0_attn_b_bg2': _L0_attn_b_in['bg2'], 'L0_attn_b_wog': _L0_attn_b_in['wog'], 'L0_attn_b_bog': _L0_attn_b_in['bog'], 'L0_attn_b_wo': _L0_attn_b_in['wo'], 'L0_attn_b_w_gate': _L0_attn_b_in['w_gate'], 'L0_attn_b_w_up': _L0_attn_b_in['w_up'], 'L0_attn_b_w_down': _L0_attn_b_in['w_down'], 'L0_ffn_router_w': _L0_ffn_in['router_w'], 'L0_ffn_router_b': _L0_ffn_in['router_b'], 'L0_ffn_w1': _L0_ffn_in['w1'], 'L0_ffn_b1': _L0_ffn_in['b1'], 'L0_ffn_w2': _L0_ffn_in['w2'], 'L0_ffn_b2': _L0_ffn_in['b2']}
    _x0 = _d['L0_attn_a_x']
    _d['L0_attn_a_x'] = jax.random.normal(jax.random.fold_in(jax.random.key(seed), 1), (8, 512, 256), dtype=_x0.dtype)
    del _x0
    return _d

def reference(L0_attn_a_x, L0_attn_a_Wq, L0_attn_a_bq, L0_attn_a_Wk, L0_attn_a_bk, L0_attn_a_Wv, L0_attn_a_bv, L0_attn_a_Wo, L0_attn_a_bo, L0_attn_b_scale1, L0_attn_b_scale2, L0_attn_b_wq, L0_attn_b_wk, L0_attn_b_wv, L0_attn_b_wg1, L0_attn_b_bg1, L0_attn_b_wg2, L0_attn_b_bg2, L0_attn_b_wog, L0_attn_b_bog, L0_attn_b_wo, L0_attn_b_w_gate, L0_attn_b_w_up, L0_attn_b_w_down, L0_ffn_router_w, L0_ffn_router_b, L0_ffn_w1, L0_ffn_b1, L0_ffn_w2, L0_ffn_b2):

    def _L0_attn_a_ref(x, Wq, bq, Wk, bk, Wv, bv, Wo, bo):
        import jax, jax.numpy as jnp
        import numpy as np
        B, L, D = (2, 512, 256)
        H = 16
        DH = D // H
        FACTOR = 0.6
        U = max(1, min(L, int(FACTOR * L)))

        def _split_heads(x):
            b, l, d = x.shape
            return x.reshape(b, l, H, DH).transpose(0, 2, 1, 3)
        b, l, _ = x.shape
        scale = 1.0 / jnp.sqrt(jnp.asarray(DH, dtype=x.dtype))
        q = _split_heads(x @ Wq + bq)
        k = _split_heads(x @ Wk + bk)
        v = _split_heads(x @ Wv + bv)
        scores = jnp.einsum('bhqd,bhkd->bhqk', q, k) * scale
        sparsity = scores.max(axis=-1) - scores.mean(axis=-1)
        _, top_idx = jax.lax.top_k(sparsity, U)
        q_sel = jnp.take_along_axis(q, top_idx[..., None], axis=2)
        scores_sel = jnp.einsum('bhud,bhkd->bhuk', q_sel, k) * scale
        attn = jax.nn.softmax(scores_sel, axis=-1)
        out_sel = jnp.einsum('bhuk,bhkd->bhud', attn, v)
        bi = jnp.arange(b)[:, None, None]
        hi = jnp.arange(H)[None, :, None]
        out = jnp.zeros_like(q).at[bi, hi, top_idx].set(out_sel)
        out = out.transpose(0, 2, 1, 3).reshape(b, l, D)
        return out @ Wo + bo

    def _L0_attn_b_ref(x, scale1, scale2, wq, wk, wv, wg1, bg1, wg2, bg2, wog, bog, wo, w_gate, w_up, w_down):
        import jax, jax.numpy as jnp
        import numpy as np
        D_MODEL = 256
        N_HEADS = 16
        D_K = D_MODEL // N_HEADS
        D_HID = 4 * D_MODEL
        GATE_TEMP = 16.0
        RMS_EPS = 1e-06
        LN_EPS = 1e-05

        def _rmsnorm(x, scale):
            norm = jnp.sqrt(jnp.sum(x * x, axis=-1, keepdims=True))
            rms = norm / np.sqrt(x.shape[-1]).astype(np.float32)
            return x / (rms + RMS_EPS) * scale

        def _silu(x):
            return x * jax.nn.sigmoid(x)

        def _gla(x, wq, wk, wv, wg1, bg1, wg2, bg2, wog, bog, wo):
            xb = jnp.swapaxes(x, 0, 1)
            B, T, C = xb.shape
            H, dk = (N_HEADS, D_K)
            q = (xb @ wq.T).reshape(B, T, H, dk)
            k = (xb @ wk.T).reshape(B, T, H, dk)
            v = (xb @ wv.T).reshape(B, T, H, dk)
            gate_hidden = _silu(xb @ wg1.T + bg1)
            alpha = jax.nn.sigmoid((gate_hidden @ wg2.T + bg2) / GATE_TEMP).reshape(B, T, H, dk)
            qT, kT, vT, aT = (jnp.moveaxis(a, 1, 0) for a in (q, k, v, alpha))
            S0 = jnp.zeros((B, H, dk, dk), xb.dtype)

            def step(S, qkva):
                q_t, k_t, v_t, a_t = qkva
                S = a_t[..., None] * S + k_t[..., :, None] * v_t[..., None, :]
                o_t = jnp.einsum('bhk,bhkv->bhv', q_t, S)
                return (S, o_t)
            S_final, oT = jax.lax.scan(step, S0, (qT, kT, vT, aT))
            o = jnp.moveaxis(oT, 0, 1)
            mu = jnp.mean(o, axis=-1, keepdims=True)
            var = jnp.mean((o - mu) ** 2, axis=-1, keepdims=True)
            o = (o - mu) / jnp.sqrt(var + LN_EPS)
            o = o.reshape(B, T, H * dk)
            out_gate = _silu(xb @ wog.T + bog)
            out = o * out_gate @ wo.T
            return (jnp.swapaxes(out, 0, 1), S_final)

        def _reference_tuple_inner(x, scale1, scale2, wq, wk, wv, wg1, bg1, wg2, bg2, wog, bog, wo, w_gate, w_up, w_down):
            attn_out, new_cache = _gla(_rmsnorm(x, scale1), wq, wk, wv, wg1, bg1, wg2, bg2, wog, bog, wo)
            x = x + attn_out
            normed = _rmsnorm(x, scale2)
            ffn = _silu(normed @ w_gate.T) * (normed @ w_up.T) @ w_down.T
            x = x + ffn
            return (x, new_cache)
        return _reference_tuple_inner(x, scale1, scale2, wq, wk, wv, wg1, bg1, wg2, bg2, wog, bog, wo, w_gate, w_up, w_down)[0]

    def _L0_ffn_ref(x, router_w, router_b, w1, b1, w2, b2):
        import jax, jax.numpy as jnp
        import numpy as np
        IN_F, OUT_F, BLOCK, NBLK = (256, 1024, 64, 16)
        TOPK = NBLK // 4
        x_shape = x.shape
        xf = x.reshape(-1, IN_F)
        n = xf.shape[0]
        prob = jax.nn.softmax(xf @ router_w.T + router_b, axis=-1)
        _, idx = jax.lax.top_k(prob, TOPK)
        mask = jnp.zeros((n, NBLK), bool).at[jnp.arange(n)[:, None], idx].set(True)
        w1b = w1.reshape(NBLK, BLOCK, IN_F)
        b1b = b1.reshape(NBLK, BLOCK)
        h = jnp.einsum('nd,ibd->nib', xf, w1b) + b1b
        h = jnp.where(mask[:, :, None], h, jnp.zeros((), h.dtype))
        h = jax.nn.relu(h)
        w2b = w2.reshape(IN_F, NBLK, BLOCK)
        y = jnp.einsum('nib,dib->nd', jnp.where(mask[:, :, None], h, 0.0), w2b) + b2
        return y.reshape(x_shape)
    x = L0_attn_a_x
    x = x + _L0_attn_a_ref(_layernorm(x, axis=-1), L0_attn_a_Wq, L0_attn_a_bq, L0_attn_a_Wk, L0_attn_a_bk, L0_attn_a_Wv, L0_attn_a_bv, L0_attn_a_Wo, L0_attn_a_bo)
    x = x + _L0_ffn_ref(_layernorm(x, axis=-1), L0_ffn_router_w, L0_ffn_router_b, L0_ffn_w1, L0_ffn_b1, L0_ffn_w2, L0_ffn_b2)
    x = x + _L0_attn_b_ref(_layernorm(x, axis=-1), L0_attn_b_scale1, L0_attn_b_scale2, L0_attn_b_wq, L0_attn_b_wk, L0_attn_b_wv, L0_attn_b_wg1, L0_attn_b_bg1, L0_attn_b_wg2, L0_attn_b_bg2, L0_attn_b_wog, L0_attn_b_bog, L0_attn_b_wo, L0_attn_b_w_gate, L0_attn_b_w_up, L0_attn_b_w_down)
    x = x + _L0_ffn_ref(_layernorm(x, axis=-1), L0_ffn_router_w, L0_ffn_router_b, L0_ffn_w1, L0_ffn_b1, L0_ffn_w2, L0_ffn_b2)
    return x

_drawn_inputs = setup_inputs


def setup_inputs(seed=0):
    import zlib

    import numpy as np

    out = dict(_drawn_inputs(seed))
    spreads = {'L0_attn_a_bq': (0.0, 0.356),
     'L0_attn_a_bk': (0.0, 2.0),
     'L0_attn_a_bv': (0.0, 0.1),
     'L0_attn_a_bo': (0.0, 0.1),
     'L0_attn_b_scale1': (1.0, 0.6),
     'L0_attn_b_scale2': (1.0, 0.6),
     'L0_attn_b_bg1': (0.0, 2.0),
     'L0_attn_b_bg2': (0.0, 2.0),
     'L0_attn_b_bog': (0.0, 0.772)}
    factors = {'L0_attn_a_Wk': 3.14,
     'L0_attn_a_Wv': 6.974,
     'L0_attn_b_wg1': 59.454,
     'L0_attn_b_wg2': 51.196,
     'L0_attn_b_w_gate': 2.972,
     'L0_attn_b_w_up': 2.969,
     'L0_attn_b_w_down': 2.964,
     'L0_ffn_b1': 4.953}
    for name, (base, spread) in spreads.items():
        noise = np.random.default_rng([zlib.crc32(name.encode()), seed]).standard_normal(out[name].shape)
        drawn = base * np.exp(spread * noise) if base else spread * noise
        out[name] = jnp.asarray(drawn.astype(out[name].dtype))
    for name, factor in factors.items():
        out[name] = (out[name] * factor).astype(out[name].dtype)
    return out
```

```python
from contextlib import ExitStack, contextmanager

import concourse.bass as bass
from concourse import mybir

ALU = mybir.AluOpType
ACT = mybir.ActivationFunctionType
AX_X = mybir.AxisListType.X
F32 = mybir.dt.float32
F32R = mybir.dt.float32r
BF16 = mybir.dt.bfloat16

P = 128
B, L, D = 8, 512, 256
H, DH = 16, 16
NC = D // P
NT = L // P
HU = P // DH
NPAIR = HU // 2
NMS = NPAIR * NT
HG = 4
OR = DH + 1
KEEP = max(1, min(L, int(0.6 * L)))
DROP = L - KEEP
ROUNDS = -(-DROP // 8)
PADS = ROUNDS * 8 - DROP
BIG = 3.0e38
GONE = -3.2e38
LN_EPS = 1e-5
QS = 0.25
PASSES = ((0, 0), (0, 1), (1, 0))
VZ_STRIDE = 1160
PT_BUFS = 4
DVE_LINKS = 18
DVE_LINKS_B = 69

TASKS = [["V", "X0", "X1", "Q", "K", "O0", "mean", "mx", "O1"],
         ["V", "Q", "K", "O0", "mean", "mx", "O1"]]
TASKS_FIRST = ["X0", "X1", "Q0", "K0", "mean0", "Q1", "K1", "mean1", "V", "mx"]
AT = {"V": 1, "X0": 3, "X1": 4, "Q": 6, "K": 7, "O0": 8, "mean": 9, "mx": 13, "O1": 15}
SCORES_AT = [1, 1, 2, 1, 1, 2, 1, 1, 2, 1, 1, 2, 0, 0, 0, 0]
assert sum(SCORES_AT) == NMS


def tasks_of(b_last, g):
    if not b_last:
        return TASKS[g]
    return [t for t in TASKS[g] if t in (("V", "O0", "mx", "O1") if g == 0 else ("O0", "O1"))]


def per_batch(kinds):
    return sum(t in kinds for g in (0, 1) for t in TASKS[g])


def constant_wait(eng, const):
    eng.wait_ge(const["ready"], const["count"])


class Link:

    def __init__(self, eng, sem, const):
        self.eng, self.sem, self.const, self.base, self.n = eng, sem, const, 0, 0

    def __call__(self, ins, alone=False):
        ins.then_inc(self.sem, 1)
        self.n += 1
        self.eng.wait_ge(self.sem, self.base + self.n)
        if alone:
            tiny = self.const["tiny"]
            self.eng.tensor_copy(tiny[:, 1:2], tiny[:, 0:1])

    def enter(self, i, per):
        self.start, self.per = self.n + self.base, per
        self.base, self.n = self.start + per * i, 0

    def leave(self, times):
        assert self.n == self.per, (self.n, self.per)
        self.base, self.n = self.start + self.per * times, 0


def attention(nc, ctx, dram, sb, ps, sem, const):
    x_in = sb("x_in", [P, NT, D], F32)
    xn = sb("xn", [P, NT, D], F32)
    xT = sb("xT", [P, NC, L], F32)
    xT_hi = sb("xT_hi", [P, NC, L], F32R)
    xT_lo = sb("xT_lo", [P, NC, L], F32R)
    xT_parts = (xT_hi, xT_lo)
    q_st = [sb(f"q_st{i}", [P, NPAIR, L], F32R) for i in range(2)]
    k_st = [sb(f"k_st{i}", [P, NPAIR, L], F32R) for i in range(2)]
    qk_hi = [sb(n, [P, L], F32R) for n in ("q_hi", "k_hi")]
    qk_lo = [sb(n, [P, L], F32R) for n in ("q_lo", "k_lo")]
    vz = [sb(f"vz{i}", [P, NT, VZ_STRIDE], F32) for i in range(2)]
    pT = [sb(f"pT{i}", [P, 2, L], F32) for i in range(PT_BUFS)]
    oT = [sb(f"oT{i}", [P, L], F32) for i in range(2)]
    mx = sb("mx", [P, NT, HU], F32)
    ksum = sb("ksum", [P, 2], F32)
    kmean = sb("kmean", [P, HU], F32)
    kmean_w = [sb(f"kmean_w{i}", [P, P], F32R) for i in range(2)]
    mean_sb = [sb(f"mean{i}", [HU, L], F32) for i in range(2)]
    m_hi = sb("m_hi", [HU, L], F32R)
    m_lo = sb("m_lo", [HU, L], F32R)
    sp_u = sb("sp_u", [HU, L], F32)
    spars = sb("spars", [P, L], F32)
    race = sb("race", [P, PADS + L], F32)
    top8 = sb("top8", [P, 8], F32)
    sel = sb("sel", [P, L], F32)
    selT = sb("selT", [P, NT, P], F32)
    oa = sb("oa", [P, B * NT, D], F32)
    rden = sb("rden", [P, NT, HG], F32)
    stat = sb("stat", [P, NT, 6], F32)
    mv = sb("mv", [P, NT, 2], F32)
    ve = sb("ve", [P, NT], F32)
    rstd = sb("rstd", [P, NT], F32)
    stage = sb("stage_a", [P, NC, D], F32)
    w_q = [sb(f"wq_a{i}", [P, NC, D], F32R) for i in range(2)]
    w_k = [sb(f"wk_a{i}", [P, NC, D], F32R) for i in range(2)]
    w_o = [sb(f"wo_a{i}", [P, NC, D], F32R) for i in range(2)]
    w_v = sb("wv_a", [P, NC, D], F32)
    bq = sb("bq", [P, NC], F32)
    bk = sb("bk", [P, NC], F32)
    bkL = sb("bkL", [P, NC], F32)
    bv_all = sb("bv_all", [P, D], F32)
    bo_all = sb("bo_all", [P, D], F32)
    head_of = sb("head_of", [P, HU], F32)
    ident, minus_half = const["ident"], const["minus_half"]

    bank = [ps[:, k, :] for k in range(8)]
    o_bank, misc = bank[6], bank[7]

    w_in, w_ready = sem("w_in"), sem("w_ready")
    stage_in, stage_free = sem("stage_in"), sem("stage_free")
    x_loaded, xn_ready = sem("x_loaded"), sem("xn_ready")
    var_ready, rstd_ready = sem("var_ready"), sem("rstd_ready")
    xT_ready, xT_split = sem("xT_ready"), sem("xT_split")
    hi_ready, lo_ready = sem("hi_ready"), sem("lo_ready")
    st_in = [sem(f"st_in{j}") for j in range(NPAIR)]
    kmean_ready, mean_ready = sem("kmean_ready"), sem("mean_ready")
    v_ready = sem("v_ready")
    s_done, max_done = sem("s_done"), sem("max_done")
    sT_done, exp_done, pT_free = sem("sT_done"), sem("exp_done"), sem("pT_free")
    oT_ready = sem("oT_ready")
    task_done, task_free = sem("task_done"), sem("task_free")
    m_ready, m_in, sp_in = sem("m_ready"), sem("m_in"), sem("sp_in")
    sp_out = sem("sp_out")
    sel_ready, selT_done, selT_ready = sem("sel_ready"), sem("selT_done"), sem("selT_ready")
    init_done = sem("init_done")
    dve_link = sem("dve_link")
    NPRO = len(TASKS_FIRST)
    NTASK = sum(map(len, TASKS))

    def task_no(b, last, g, kind):
        names = [(g_, t) for g_ in (0, 1) for t in tasks_of(last, g_)]
        return NPRO + NTASK * b + names.index((g, kind))

    def sp(eng):
        ld = lambda out, in_, s: eng.dma_start(out, in_).then_inc(s, 16)
        ld(x_in[:, :, :], dram["x"][0].rearrange("(t p) c -> p t c", p=P), x_loaded)
        for n, name in enumerate(("Wq", "Wk", "Wo")):
            if n:
                eng.wait_ge(stage_free, n)
            ld(stage[:, :, :], dram[name].rearrange("(c p) n -> p c n", p=P), stage_in)
        ld(w_v[:, :, :], dram["Wv"].rearrange("(c p) n -> p c n", p=P), w_in)
        ld(bv_all[:, :], dram["bv"].partition_broadcast(P), w_in)
        ld(bo_all[:, :], dram["bo"].partition_broadcast(P), w_in)

        def stack(w, j, buf):
            for parts, dst in (((qk_hi[0], qk_hi[0], qk_lo[0]), q_st[buf]),
                               ((qk_hi[1], qk_lo[1], qk_hi[1]), k_st[buf])):
                for r, src in enumerate(parts):
                    for e in range(2):
                        ld(dst[64 * e + DH * r:64 * e + DH * r + DH, j, :].bitcast(F32),
                           src[(2 * j + e) * DH:(2 * j + e + 1) * DH, :].bitcast(F32), st_in[j])

        def m_rows(w, buf):
            eng.wait_ge(m_ready, w + 1)
            for e in range(2):
                for r, src in enumerate((m_hi, m_lo)):
                    at = 64 * e + 3 * DH + r
                    ld(q_st[buf][at:at + 1, :, :].bitcast(F32), src[e::2, :].bitcast(F32), m_in)
            ld(dram["spars"][bass.ds(w * HU, HU), :], sp_u[:, :], sp_out)

        eng.wait_ge(init_done, 5)
        for w in range(2):
            eng.wait_ge(lo_ready, 2 * w + 2)
            for j in range(NPAIR):
                stack(w, j, w)
        m_rows(0, 0)

        def step(b, g, last):
            u = 2 * b + g
            if not last:
                if g == 0:
                    eng.wait_ge(xn_ready, b + 1)
                    ld(x_in[:, :, :], dram["x_tiles"][:, bass.ts(b + 1, NT), :], x_loaded)
                eng.wait_ge(lo_ready, 2 * (u + 2) + 2)
                for j in range(NPAIR - 1):
                    eng.wait_ge(sT_done, NMS * u + NT * (j + 1))
                    stack(u + 2, j, g)
            if not (last and g == 1):
                m_rows(u + 1, 1 - g)
            if not last:
                eng.wait_ge(sT_done, NMS * u + NMS)
                stack(u + 2, NPAIR - 1, g)

        with eng.Fori(0, B - 1) as b:
            step(b, 0, False)
            step(b, 1, False)
        step(B - 1, 0, True)
        step(B - 1, 1, True)
        eng.wait_ge(sp_out, 16 * 2 * B)
        ld(spars[:, :], dram["spars"][:, :], sp_in)

    def pool(eng):
        g = nc.gpsimd
        g.memset(head_of[:, :], 1.0).then_inc(init_done, 1)
        eng.wait_ge(init_done, 3)
        g.affine_select(out=head_of[:, :], in_=head_of[:, :], compare_op=ALU.is_ge, fill=0.0,
                        base=0, pattern=[[-DH, HU]], channel_multiplier=1).then_inc(init_done, 1)
        eng.wait_ge(init_done, 4)
        g.affine_select(out=head_of[:, :], in_=head_of[:, :], compare_op=ALU.is_ge, fill=0.0,
                        base=DH - 1, pattern=[[DH, HU]], channel_multiplier=-1).then_inc(init_done, 1)

        def power(i):
            eng.wait_ge(var_ready, i + 1)
            g.tensor_tensor(rstd[:, :], ve[:, :], minus_half[:, 0:NT], ALU.pow).then_inc(rstd_ready, 1)

        power(0)
        with eng.Fori(0, B - 1) as b:
            power(b + 1)

    def dve(eng):
        v = nc.vector
        link = Link(eng, dve_link, const)
        for buf in range(2):
            v.memset(q_st[buf][:, :, :].bitcast(F32), 0.0)
            v.memset(k_st[buf][:, :, :].bitcast(F32), 1.0)
            v.memset(kmean_w[buf][:, :].bitcast(F32), 0.0)
            link(v.memset(vz[buf][:, :, :], 0.0))
        v.memset(rden[:, :, :], 1.0).then_inc(pT_free, PT_BUFS)
        v.memset(mean_sb[0][:, :], 0.0).then_inc(exp_done, 1)
        v.memset(mean_sb[1][:, :], 0.0).then_inc(oT_ready, 1)
        v.memset(sp_u[:, :], 0.0).then_inc(task_free, 1)
        for buf in range(2):
            for gr in range(HU // HG):
                at = gr * HG * P + DH
                last = v.memset(vz[buf][:, :, at:at + HG * (P + OR)]
                                .rearrange("p t (h c) -> p t h c", c=P + OR)[:, :, :, 0:1], 1.0)
        last.then_inc(init_done, 1)
        v.memset(race[:, 0:PADS], BIG).then_inc(init_done, 1)

        for n, (w, s) in enumerate(((w_q, QS), (w_k, 1.0), (w_o, 1.0))):
            eng.wait_ge(stage_in, 16 * (n + 1))
            link(v.tensor_scalar(w[0][:, :, :], stage[:, :, :], s, None, ALU.mult))
            v.scalar_tensor_tensor(w[1][:, :, :], stage[:, :, :], s, w[0][:, :, :].bitcast(F32),
                                   ALU.mult, ALU.subtract).then_inc(stage_free, 1)
        eng.wait_ge(w_in, 16 * 5)
        link(v.tensor_scalar(bq[:, :], bq[:, :], QS, None, ALU.mult))
        v.tensor_scalar(bkL[:, :], bk[:, :], float(L), None, ALU.mult).then_inc(w_ready, 1)

        def layer_norm(i):
            eng.wait_ge(x_loaded, 16 * (i + 1))
            for t in range(NT):
                last = v.bn_stats(stat[:, t, :], x_in[:, t, :])
            link(last, alone=True)
            for t in range(NT):
                last = v.bn_aggr(mv[:, t, :], stat[:, t, :])
            link(last)
            v.tensor_scalar(ve[:, :], mv[:, :, 1], LN_EPS, None, ALU.add).then_inc(var_ready, 1)

        def normalise(i):
            eng.wait_ge(rstd_ready, i + 1)
            for t in range(NT):
                last = v.tensor_scalar(xn[:, t, :], x_in[:, t, :], mv[:, t, 0:1], rstd[:, t:t + 1],
                                       ALU.subtract, ALU.mult)
            last.then_inc(xn_ready, 1)

        def split_x(no, i):
            c = no
            eng.wait_ge(xT_ready, i + 1)
            link(v.tensor_copy(xT_hi[:, c, :], xT[:, c, :]))
            v.tensor_tensor(xT_lo[:, c, :], xT[:, c, :], xT_hi[:, c, :].bitcast(F32),
                            ALU.subtract).then_inc(xT_split, 1)

        def low(which, w, g):
            bias = (bq, bk)[which]
            eng.wait_ge(hi_ready, 2 * w + which + 1)
            v.scalar_tensor_tensor(qk_lo[which][:, :], misc[:, :], bias[:, g:g + 1],
                                   qk_hi[which][:, :].bitcast(F32), ALU.add,
                                   ALU.subtract).then_inc(lo_ready, 1)
            if which == 0:
                return
            link(v.tensor_reduce(ksum[:, 0:1], misc[:, :], AX_X, ALU.add))
            link(v.tensor_tensor(ksum[:, 1:2], ksum[:, 0:1], bkL[:, g:g + 1], ALU.add))
            link(v.tensor_scalar(kmean[:, :], head_of[:, :], ksum[:, 1:2], 1.0 / L, ALU.mult, ALU.mult))
            link(v.tensor_copy(kmean_w[0][:, 0:HU], kmean[:, :]))
            v.tensor_tensor(kmean_w[1][:, 0:HU], kmean[:, :], kmean_w[0][:, 0:HU].bitcast(F32),
                            ALU.subtract).then_inc(kmean_ready, 1)

        def values(g, no):
            eng.wait_ge(task_done, no + 1)
            for gr in range(HU // HG):
                at = gr * HG * P
                out = vz[g][:, :, at:at + HG * (P + OR)].rearrange(
                    "p t (h c) -> p t h c", c=P + OR)[:, :, :, 0:DH]
                cols = slice(gr * HG * DH, (gr + 1) * HG * DH)
                src = misc[:, :].rearrange("p (t c) -> p t c", t=NT)[:, :, cols].rearrange(
                    "p t (h d) -> p t h d", d=DH)
                bias = bv_all[:, g * P:(g + 1) * P][:, cols].rearrange("p (h d) -> p h d", d=DH)
                last = v.tensor_tensor(out, src, bias.unsqueeze(1).to_broadcast([P, NT, HG, DH]), ALU.add)
            return last

        def score_max(n, i):
            j, qt = divmod(i, NT)
            eng.wait_ge(s_done, n + 1)
            v.tensor_reduce(mx[:, qt, 2 * j:2 * j + 2], ps[:, 0:2, :], AX_X, ALU.max).then_inc(max_done, 1)

        def maxima(w, no, par):
            eng.wait_ge(task_done, no + 1)
            if not (isinstance(w, int) and w == 0):
                eng.wait_ge(m_in, 64 * w)
                eng.wait_ge(sp_out, 16 * w)
            link(v.tensor_scalar(m_hi[:, :], misc[0:HU, :], -1.0, None, ALU.mult))
            v.scalar_tensor_tensor(m_lo[:, :], misc[0:HU, :], -1.0, m_hi[:, :].bitcast(F32),
                                   ALU.mult, ALU.subtract)
            eng.wait_ge(mean_ready, w + 1)
            v.tensor_tensor(sp_u[:, :], misc[0:HU, :], mean_sb[par][:, :],
                            ALU.subtract).then_inc(m_ready, 1)

        def outputs(b, g, gr, no):
            eng.wait_ge(task_done, no + 1)
            src = misc[:, 0:NT * HG * OR].rearrange("p (t h c) -> p t h c", t=NT, h=HG)
            link(v.reciprocal(rden[:, :, :], src[:, :, :, DH]))
            at = g * P + gr * HG * DH
            out = oa[:, bass.ts(b, NT), at:at + HG * DH].rearrange("p t (h d) -> p t h d", h=HG)
            v.tensor_tensor(out, src[:, :, :, 0:DH],
                            rden[:, :, :].unsqueeze(3).to_broadcast([P, NT, HG, DH]),
                            ALU.mult).then_inc(task_free, 1)

        layer_norm(0)
        normalise(0)
        eng.wait_ge(init_done, 5)
        split_x(0, 0)
        split_x(1, 1)
        for w in range(2):
            low(0, w, w)
            low(1, w, w)
        values(0, TASKS_FIRST.index("V")).then_inc(v_ready, 1)
        for i in range(NMS):
            score_max(i, i)
        maxima(0, TASKS_FIRST.index("mx"), 0)

        def step(b, g, last):
            u = 2 * b + g
            n = 0
            todo = tasks_of(last, g)
            for m in range(NMS):
                scores = 0 if last and g == 1 else SCORES_AT[m]
                if scores:
                    score_max(NMS * (u + 1) + n, n)
                if not last and g == 0 and m == 0:
                    layer_norm(b + 1)
                if not last and g == 0 and m == 1:
                    normalise(b + 1)
                for t in todo:
                    if AT[t] != m:
                        continue
                    no = task_no(b, last, g, t)
                    if t == "V":
                        values(1 - g, no).then_inc(v_ready, 1)
                    elif t[0] == "X":
                        split_x(int(t[1]), 2 * (b + 1) + int(t[1]))
                    elif t in "QK":
                        low("QK".index(t), u + 2, g)
                    elif t[0] == "O":
                        outputs(b, g, int(t[1]), no)
                    elif t == "mx":
                        maxima(u + 1, no, 1 - g)
                if scores == 2:
                    score_max(NMS * (u + 1) + n + 1, n + 1)
                n += scores

        with eng.Fori(0, B - 1) as b:
            link.enter(b, DVE_LINKS)
            step(b, 0, False)
            step(b, 1, False)
            link.leave(B - 1)
        step(B - 1, 0, True)
        step(B - 1, 1, True)

        eng.wait_ge(sp_in, 16)
        link(v.tensor_scalar(race[:, PADS:], spars[:, ::-1], -1.0, None, ALU.mult))
        for _ in range(ROUNDS):
            link(v.max(top8[:, :], race[:, :]))
            link(v.match_replace(race[:, :], top8[:, :], race[:, :], GONE))
        v.tensor_scalar(sel[:, :], race[:, PADS:][:, ::-1], GONE, None,
                        ALU.not_equal).then_inc(sel_ready, 1)
        eng.wait_ge(selT_done, 1)
        v.tensor_copy(selT[:, :, :], bank[0][:, :].rearrange("p (t r) -> p t r", t=NT)).then_inc(selT_ready, 1)
        return link

    def act(eng):
        a = nc.scalar
        a.dma_start(bq[:, :], dram["bq"]).then_inc(w_in, 16)
        a.dma_start(bk[:, :], dram["bk"]).then_inc(w_in, 16)

        def x_out(c, no):
            eng.wait_ge(task_done, no + 1)
            a.activation(xT[:, c, :], misc[:, :], ACT.Copy).then_inc(xT_ready, 1)

        def high(which, w, g, no):
            bias = (bq, bk)[which]
            eng.wait_ge(task_done, no + 1)
            if which == 0 and not (isinstance(w, int) and w == 0):
                for j in range(NPAIR):
                    eng.wait_ge(st_in[j], 16 * 12 * w)
            a.activation(qk_hi[which][:, :], misc[:, :], ACT.Identity,
                         bias=bias[:, g:g + 1]).then_inc(hi_ready, 1)

        def mean_out(par, no):
            eng.wait_ge(task_done, no + 1)
            a.activation(mean_sb[par][:, :], misc[0:HU, :], ACT.Copy).then_inc(mean_ready, 1)

        def o_out(u, gr):
            eng.wait_ge(pT_free, PT_BUFS + NMS * u + NMS // 2 * (gr + 1))
            a.activation(oT[gr][:, :], o_bank[:, :], ACT.Copy).then_inc(oT_ready, 1)

        def exps(u, m):
            n = NMS * u + m
            eng.wait_ge(sT_done, n + 1)
            eng.wait_ge(pT_free, n + 1)
            a.activation(pT[m % PT_BUFS][:, :, :], ps[:, 2 + 2 * (m % 2):4 + 2 * (m % 2), :],
                         ACT.Exp).then_inc(exp_done, 1)

        eng.wait_ge(w_ready, 1)
        x_out(0, 0)
        x_out(1, 1)
        for w in range(2):
            high(0, w, w, TASKS_FIRST.index(f"Q{w}"))
            high(1, w, w, TASKS_FIRST.index(f"K{w}"))
            mean_out(w, TASKS_FIRST.index(f"mean{w}"))

        def step(b, g, last):
            u = 2 * b + g
            todo = tasks_of(last, g)
            for m in range(NMS):
                exps(u, m)
                for t in todo:
                    if AT[t] != m:
                        continue
                    no = task_no(b, last, g, t)
                    if t[0] == "X":
                        x_out(int(t[1]), no)
                    elif t in "QK":
                        high("QK".index(t), u + 2, g, no)
                    elif t == "mean":
                        mean_out(g, no)
                    elif t[0] == "O":
                        o_out(u, int(t[1]))

        with eng.Fori(0, B - 1) as b:
            step(b, 0, False)
            step(b, 1, False)
        step(B - 1, 0, True)
        step(B - 1, 1, True)

    def pe(eng):
        t_ = nc.tensor

        def x_task(c):
            for t in range(NT):
                last = t_.transpose(misc[:, t * P:(t + 1) * P], xn[:, t, c * P:(c + 1) * P], ident[:, :])
            last.then_inc(task_done, 1)

        def qk_task(which, g):
            w = (w_q, w_k)[which]
            n = 0
            for c in range(NC):
                for i, k in PASSES:
                    last = t_.matmul(misc[:, :], w[i][:, c, g * P:(g + 1) * P], xT_parts[k][:, c, :],
                                     start=n == 0, stop=n == NC * len(PASSES) - 1)
                    n += 1
            last.then_inc(task_done, 1)

        def v_task(g):
            for t in range(NT):
                for c in range(NC):
                    last = t_.matmul(misc[:, t * P:(t + 1) * P], xT[:, c, t * P:(t + 1) * P],
                                     w_v[:, c, g * P:(g + 1) * P], start=c == 0, stop=c == NC - 1)
            last.then_inc(task_done, 1)

        def mean_task():
            for n, (i, k) in enumerate(PASSES):
                last = t_.matmul(misc[:, :], kmean_w[i][:, :], (qk_hi[0], qk_lo[0])[k][:, :],
                                 start=n == 0, stop=n == len(PASSES) - 1)
            last.then_inc(task_done, 1)

        def mx_task():
            for t in range(NT):
                last = t_.transpose(misc[0:HU, t * P:(t + 1) * P], mx[:, t, :], ident[:, :])
            last.then_inc(task_done, 1)

        def o_task(gr):
            n = HG * OR
            for t in range(NT):
                last = t_.transpose(misc[:, t * n:(t + 1) * n], oT[gr][0:n, t * P:(t + 1) * P],
                                    ident[0:n, 0:n])
            last.then_inc(task_done, 1)

        def scores(n, i, buf):
            j, qt = divmod(i, NT)
            if not (isinstance(n, int) and n == 0):
                eng.wait_ge(max_done, n)
            for e in range(2):
                last = t_.matmul(bank[e][:, :],
                                 q_st[buf][64 * e:64 * e + 3 * DH, j, qt * P:(qt + 1) * P],
                                 k_st[buf][64 * e:64 * e + 3 * DH, j, :], start=True, stop=True)
            last.then_inc(s_done, 1)

        def scores_T(m, buf):
            j, kt = divmod(m, NT)
            for e in range(2):
                last = t_.matmul(bank[2 + 2 * (m % 2) + e][:, :],
                                 k_st[buf][64 * e:64 * e + 64, j, kt * P:(kt + 1) * P],
                                 q_st[buf][64 * e:64 * e + 64, j, :], start=True, stop=True)
            last.then_inc(sT_done, 1)

        def products(m, g):
            j, kt = divmod(m, NT)
            half = NMS // 2
            for e in range(2):
                h = 2 * j + e
                last = t_.matmul(o_bank[:, :], vz[g][:, kt, h * P:(h + 1) * P], pT[m % PT_BUFS][:, e, :],
                                 start=m % half == 0 and e == 0, stop=m % half == half - 1 and e == 1)
            last.then_inc(pT_free, 1)

        eng.wait_ge(init_done, 5)
        eng.wait_ge(const["ready"], const["count"])
        eng.wait_ge(w_ready, 1)
        eng.wait_ge(stage_free, 3)
        eng.wait_ge(xn_ready, 1)
        x_task(0)
        eng.wait_ge(xT_ready, 1)
        x_task(1)
        eng.wait_ge(xT_ready, 2)
        eng.wait_ge(xT_split, 2)
        for w in range(2):
            if w:
                eng.wait_ge(mean_ready, w)
            qk_task(0, w)
            eng.wait_ge(lo_ready, 2 * w + 1)
            qk_task(1, w)
            eng.wait_ge(kmean_ready, w + 1)
            mean_task()
        eng.wait_ge(mean_ready, 2)
        v_task(0)
        for i in range(NMS):
            if i % NT == 0:
                eng.wait_ge(st_in[i // NT], 16 * 12)
            scores(i, i, 0)
        eng.wait_ge(max_done, NMS)
        eng.wait_ge(v_ready, 1)
        mx_task()
        eng.wait_ge(m_in, 64)
        scores_T(0, 0)

        def step(b, g, last):
            u = 2 * b + g
            n = 0
            todo = tasks_of(last, g)
            for m in range(NMS):
                count = 0 if last and g == 1 else SCORES_AT[m]
                for k in range(count):
                    if k == 1:
                        continue
                    if n % NT == 0:
                        eng.wait_ge(st_in[n // NT], 16 * 12 * (u + 2))
                    scores(NMS * (u + 1) + n, n, 1 - g)
                if m < NMS - 1:
                    eng.wait_ge(exp_done, NMS * u + m + 1)
                    scores_T(m + 1, g)
                elif not (last and g == 1):
                    eng.wait_ge(exp_done, NMS * u + m + 1)
                    eng.wait_ge(m_in, 64 * (u + 2))
                    scores_T(0, 1 - g)
                if m != NMS - 1:
                    for t in todo:
                        if AT[t] == m:
                            task(b, last, g, t)
                eng.wait_ge(exp_done, NMS * u + m + 2)
                if m == 0:
                    eng.wait_ge(v_ready, u + 1)
                if m % (NMS // 2) == 0:
                    eng.wait_ge(oT_ready, 2 * u + m // (NMS // 2) + 1)
                products(m, g)
                if m == NMS - 1:
                    task(b, last, g, "O1")
                if count == 2:
                    if (n + 1) % NT == 0:
                        eng.wait_ge(st_in[(n + 1) // NT], 16 * 12 * (u + 2))
                    scores(NMS * (u + 1) + n + 1, n + 1, 1 - g)
                n += count

        def task(b, last, g, t):
            u = 2 * b + g
            todo = tasks_of(last, g)
            at = todo.index(t)
            prev = todo[at - 1] if at else "O1"
            if prev[0] == "O":
                eng.wait_ge(task_free, 2 * u + (2 if at else 1))
            elif prev == "V":
                eng.wait_ge(v_ready, u + 2)
            elif prev == "X0":
                eng.wait_ge(xT_ready, 2 * (b + 1) + 1)
            elif prev == "X1":
                eng.wait_ge(xT_ready, 2 * (b + 1) + 2)
            elif prev == "Q":
                eng.wait_ge(lo_ready, 2 * (u + 2) + 1)
            elif prev == "K":
                eng.wait_ge(kmean_ready, u + 3)
            elif prev == "mean":
                eng.wait_ge(mean_ready, u + 3)
            elif prev == "mx":
                eng.wait_ge(m_ready, u + 2)
            if t == "V":
                v_task(1 - g)
            elif t[0] == "X":
                if t == "X0":
                    eng.wait_ge(xn_ready, b + 2)
                x_task(int(t[1]))
            elif t in "QK":
                eng.wait_ge(xT_split, 2 * (b + 2))
                qk_task("QK".index(t), g)
            elif t == "mean":
                eng.wait_ge(kmean_ready, u + 3)
                mean_task()
            elif t == "mx":
                eng.wait_ge(max_done, NMS * (u + 2))
                mx_task()
            else:
                gr = int(t[1])
                eng.wait_ge(oT_ready, 2 * u + gr + 2)
                o_task(gr)

        eng.wait_ge(m_ready, 1)
        with eng.Fori(0, B - 1) as b:
            step(b, 0, False)
            step(b, 1, False)
        step(B - 1, 0, True)
        step(B - 1, 1, True)
        eng.wait_ge(sel_ready, 1)
        for t in range(NT):
            last = t_.transpose(bank[0][:, t * P:(t + 1) * P], sel[:, t * P:(t + 1) * P], ident[:, :])
        last.then_inc(selT_done, 1)

    return locals()


def project(nc, dram, sb, ps, sem, const, A):
    xi = [A["x_in"], sb("x_in2", [P, NT, D], F32)]
    om = [A["xn"], sb("xn2", [P, NT, D], F32)]
    hi = [A["xT_hi"], sb("xT_hi2", [P, NC, L], F32R)]
    lo = [A["xT_lo"], sb("xT_lo2", [P, NC, L], F32R)]
    oa, selT, bo_all, w_o, ident = A["oa"], A["selT"], A["bo_all"], A["w_o"], const["ident"]
    x_in, x_biased = sem("p_x_in"), sem("p_x_biased")
    masked, tr_done, hi_ready, lo_ready = sem("p_masked"), sem("p_tr_done"), sem("p_hi"), sem("p_lo")
    prod_done, x1_ready, x1_out = sem("p_prod"), sem("p_x1_ready"), sem("p_x1_out")

    def sp(eng):
        with eng.Fori(0, B // 2) as i:
            eng.wait_ge(x1_out, 32 * (i + 1))
            for p in range(2):
                eng.dma_start(xi[p][:, :, :], dram["x_tiles"][:, bass.ts(2 * i + p, NT), :]).then_inc(x_in, 16)
            for p in range(2):
                eng.wait_ge(x1_ready, 2 * i + p + 1)
                eng.dma_start(dram["x1_tiles"][:, bass.ts(2 * i + p, NT), :], xi[p][:, :, :]).then_inc(x1_out, 16)
        eng.wait_ge(x1_out, 32 + 16 * B)

    def pool(eng):
        with eng.Fori(0, B // 2) as i:
            for p in range(2):
                eng.wait_ge(x_in, 32 * (i + 1))
                nc.gpsimd.tensor_tensor(xi[p][:, :, :], xi[p][:, :, :],
                                        bo_all[:, :].unsqueeze(1).to_broadcast([P, NT, D]),
                                        ALU.add).then_inc(x_biased, 1)

    def dve(eng):
        v = nc.vector
        v.memset(const["tiny"][:, 0:1], 0.0).then_inc(x1_out, 32)
        with eng.Fori(0, B // 2) as i:
            for p in range(2):
                b = 2 * i + p
                v.tensor_tensor(om[p][:, :, :].rearrange("p t (h d) -> p t h d", h=H),
                                oa[:, bass.ts(b, NT), :].rearrange("p t (h d) -> p t h d", h=H),
                                selT[:, :, bass.ts(b, H)].unsqueeze(3).to_broadcast([P, NT, H, DH]),
                                ALU.mult).then_inc(masked, 1)
            for p in range(2):
                b = 2 * i + p
                for c in range(NC):
                    eng.wait_ge(hi_ready, NC * b + c + 1)
                    v.tensor_tensor(lo[p][:, c, :], ps[:, 2 * p + c, :], hi[p][:, c, :].bitcast(F32),
                                    ALU.subtract).then_inc(lo_ready, 1)
            for p in range(2):
                b = 2 * i + p
                eng.wait_ge(x_biased, b + 1)
                eng.wait_ge(prod_done, b + 1)
                for k in range(2):
                    rows = xi[p][:, 2 * k:2 * k + 2, :]
                    last = v.tensor_tensor(rows, ps[:, 4 + 2 * p + k, :].rearrange("p (t c) -> p t c", t=2),
                                           rows, ALU.add)
                last.then_inc(x1_ready, 1)

    def act(eng):
        with eng.Fori(0, B // 2) as i:
            for p in range(2):
                for c in range(NC):
                    eng.wait_ge(tr_done, NC * (2 * i + p) + c + 1)
                    nc.scalar.activation(hi[p][:, c, :], ps[:, 2 * p + c, :], ACT.Copy).then_inc(hi_ready, 1)

    def pe(eng):
        t_ = nc.tensor
        eng.wait_ge(A["selT_ready"], 1)
        with eng.Fori(0, B // 2) as i:
            for p in range(2):
                eng.wait_ge(masked, 2 * i + p + 1)
                for c in range(NC):
                    for t in range(NT):
                        last = t_.transpose(ps[:, 2 * p + c, t * P:(t + 1) * P],
                                            om[p][:, t, c * P:(c + 1) * P], ident[:, :])
                    last.then_inc(tr_done, 1)
            for p in range(2):
                eng.wait_ge(lo_ready, NC * (2 * i + p + 1))
                for t in range(NT):
                    n = 0
                    for c in range(NC):
                        for a, w in PASSES:
                            last = t_.matmul(ps[:, 4 + 2 * p + t // 2, (t % 2) * D:(t % 2 + 1) * D],
                                             (hi, lo)[a][p][:, c, t * P:(t + 1) * P], w_o[w][:, c, :],
                                             start=n == 0, stop=n == NC * len(PASSES) - 1)
                            n += 1
                last.then_inc(prod_done, 1)

    return locals()


PB = L // 8
NBLK = L // PB
T8 = B
NE, TOPK = 16, 4
HID = 1024
NM = HID // P
OFF = 2.0 ** 100
UNDER = -103.0
RMS_EPS = 1e-6
GATE_TEMP = 16.0
NOUT = 9


def block_part(nc, dram, sb, alias, ps, sem, const):
    ident, minus_half, plus_half = const["ident"], const["minus_half"], const["plus_half"]
    def two(name, shape):
        return [sb(f"{name}{i}", shape, F32R) for i in range(2)]

    w1, w2 = two("w1", [P, NC, HID]), two("w2", [P, NM, D])
    w_gate, w_up, w_down = two("w_gate", [P, NC, HID]), two("w_up", [P, NC, HID]), two("w_down", [P, NM, D])
    w_q, w_k, w_v, w_og, w_o = (two(n, [P, NC, D]) for n in ("wq_b", "wk_b", "wv_b", "wog_b", "wo_b"))
    w_r, w_g1, w_g2 = two("w_r", [P, NC, P]), two("w_g1", [P, NC, P]), two("w_g2", [P, D])
    b1, bg2, s1, s2 = sb("b1", [P, NM], F32), sb("bg2", [P, NC], F32), sb("s1", [P, NC], F32), sb("s2", [P, NC], F32)
    rb, bg1 = sb("rb", [NE, 1], F32), sb("bg1", [NE, 1], F32)
    b2_all, bog_all = sb("b2_all", [P, D], F32), sb("bog_all", [P, D], F32)
    expand = sb("expand", [P, HID], BF16)
    head_sum = sb("head_sum", [P, P], F32)
    x = sb("x", [P, NT, D], F32)
    y = sb("y", [P, NT, D], F32)
    tok = sb("tok", [P, NT, D], F32)
    og = sb("og", [P, NT, D], F32)
    oT = sb("oT_b", [P, NC, L], F32)
    sq = oT
    sq_rows = sq[:, :, :].rearrange("p a (b c) -> p (a b) c", c=D)
    xT = two("xT_b", [P, NC, L])
    hf = [sb(f"hf{i}", [P, L], F32) for i in range(2)]
    prod = hf
    hp = [sb(f"hp{i}", [P, L], F32) for i in range(2)]
    logT = sb("logT", [NE, L], F32)
    gT = two("gT", [P, L])
    maskT = sb("maskT", [P, L], BF16)
    lg, lg_out = sb("lg", [P, NT, TOPK + NE], F32), sb("lg_out", [P, NT, TOPK + NE], F32)
    top8 = sb("top8_b", [P, NT, 8], F32)
    lmax = sb("lmax", [P, NT], F32)
    mask = sb("mask", [P, NT, NE], F32)
    stat, mv, ve, rstd = sb("stat_b", [P, NT, 6], F32), sb("mv_b", [P, NT, 2], F32), sb("ve_b", [P, NT], F32), sb("rstd_b", [P, NT], F32)
    mu, var, rs = (sb(n, [P, NT * H], F32) for n in ("mu", "var", "rs"))
    stage = [sb(f"stage_b{i}", [P, HID], F32) for i in range(2)]
    with alias() as sb_x:
        h = [sb_x(f"h{i}", [P, NM, L], F32R) for i in range(2)]
    with alias() as sb_x:
        qT, kT, vT, aT = (sb_x(n, [P, NC, L], F32) for n in ("qT", "kT", "vT", "aT"))
        pr = [sb_x(f"pr{i}", [P, L], F32) for i in range(2)]
        w = sb_x("w", [P, L], F32)

    def site(name, *kinds):
        return {k: sem(f"{name}_{k}") for k in kinds}

    tr_kinds = ("src", "tr", "hi", "lo")
    ffn_kinds = ("var", "rstd", "biased", "rt", "lt", "lg", "mk", "mt", "mtb", "up", "relu", "hl", "dn", "out") + tr_kinds
    F = [site("ffn0", *ffn_kinds), site("ffn1", *ffn_kinds)]
    Z = site("z", "var", "rstd", "ss", "rn", "ghs", "out", "cv", "og", "ogb", "ogs", *tr_kinds)
    R = site("rec", "kd", "pr", "hs", "w")
    O = site("o", "os", "ot", "var", "rs", "wo", *tr_kinds)
    G = site("g", "pd", "xy", "ss", "rn", "gate", "silu", "up", "hl", "dn", "out", *tr_kinds)
    x_in, x_out = sem("b_x_in"), sem("b_x_out")
    stage_in = [sem(f"b_stage_in{k}") for k in range(2)]
    stage_hi, stage_lo = sem("b_stage_hi"), sem("b_stage_lo")
    small_in, b_init = sem("b_small_in"), sem("b_init")
    b_cleared = sem("b_cleared")
    dve_link = sem("b_dve_link")

    pieces = []
    for name, ws in (("w1", w1), ("w_gate", w_gate), ("w_up", w_up)):
        for c in range(NC):
            pieces.append((dram[name][c * P:(c + 1) * P, :], HID, [t[:, c, :] for t in ws]))
    for name, ws in (("w2", w2), ("w_down", w_down)):
        for k in range(2):
            rows = dram[name][k * NM // 2 * P:(k + 1) * NM // 2 * P, :].rearrange("(m p) n -> p m n", p=P)
            pieces.append((rows, HID, [t[:, k * NM // 2:(k + 1) * NM // 2, :] for t in ws]))
    for name, ws in (("wq", w_q), ("wk", w_k), ("wv", w_v), ("wog", w_og), ("wo", w_o)):
        pieces.append((dram[name].rearrange("(c p) n -> p c n", p=P), NC * D, [t[:, :, :] for t in ws]))
    for name, ws in (("rw", w_r), ("wg1", w_g1)):
        pieces.append((dram[name].rearrange("(c p) n -> p c n", p=P), NC * NE, [t[:, :, 0:NE] for t in ws]))
    pieces.append((dram["wg2"], D, [t[0:NE, :] for t in w_g2]))

    def staged(n):
        src, cols, ws = pieces[n]
        rows = ws[0].shape[0]
        v = stage[n % 2][0:rows, 0:cols]
        if len(ws[0].shape) == 3:
            v = v.rearrange("p (m n) -> p m n", m=ws[0].shape[1])
        return v

    small = [(b1[:, :], "b1"), (bg2[:, :], "bg2"), (s1[:, :], "s1"), (s2[:, :], "s2"), (rb[:, :], "rb"), (bg1[:, :], "bg1")]
    NSMALL = len(small) + 2

    def sp(eng):
        def ld(out, in_, s):
            eng.dma_start(out, in_).then_inc(s, 16)

        eng.wait_ge(*const["a_done"])
        for n, (src, _, _) in enumerate(pieces):
            if n >= 2:
                eng.wait_ge(stage_lo, n - 1)
            ld(staged(n), src, stage_in[n % 2])
            if n == 1:
                for out, name in small:
                    ld(out, dram[name], small_in)
                ld(b2_all[:, :], dram["b2"].partition_broadcast(P), small_in)
                ld(bog_all[:, :], dram["bog"].partition_broadcast(P), small_in)
        with eng.Fori(0, NBLK) as i:
            eng.wait_ge(x_out, 32 * (i + 1))
            for e in range(2):
                ld(x[e * PB:(e + 1) * PB, :, :], dram["x1_blocks"][e, bass.ts(i, PB), :, :], x_in)
            eng.wait_ge(F[1]["out"], i + 1)
            for e in range(2):
                ld(dram["out_blocks"][e, bass.ts(i, PB), :, :], x[e * PB:(e + 1) * PB, :, :], x_out)
        eng.wait_ge(x_out, 32 * (NBLK + 1))

    def pool(eng):
        g = nc.gpsimd
        eng.wait_ge(*const["a_done"])
        g.memset(expand[:, :], OFF).then_inc(b_init, 1)
        g.memset(head_sum[:, :], 1.0).then_inc(b_init, 1)
        n = 2
        hs3 = head_sum[:, :].rearrange("p (h d) -> p h d", h=HU)
        for out, base, pattern, mult in (
                (expand[:, :], 0, [[1, HID]], -HID // NE), (expand[:, :], HID // NE - 1, [[-1, HID]], HID // NE),
                (hs3, 0, [[-DH, HU], [0, DH]], 1), (hs3, DH - 1, [[DH, HU], [0, DH]], -1)):
            eng.wait_ge(b_init, n)
            g.affine_select(out=out, in_=out, compare_op=ALU.is_ge, fill=0.0, base=base, pattern=pattern,
                            channel_multiplier=mult).then_inc(b_init, 1)
            n += 1
        for n, (_, _, ws) in enumerate(pieces):
            eng.wait_ge(stage_hi, n + 1)
            g.tensor_tensor(ws[1], staged(n), ws[0].bitcast(F32), ALU.subtract).then_inc(stage_lo, 1)

        def power(src, dst, half, wait, done, i):
            eng.wait_ge(wait, i + 1)
            g.tensor_tensor(dst, src, half, ALU.pow).then_inc(done, 1)

        def ffn(i, S):
            power(ve[:, :], rstd[:, :], minus_half[:, 0:NT], S["var"], S["rstd"], i)
            eng.wait_ge(S["src"], i + 1)
            g.tensor_tensor(x[:, :, :], x[:, :, :], b2_all[:, :].unsqueeze(1).to_broadcast([P, NT, D]),
                            ALU.add).then_inc(S["biased"], 1)

        with eng.Fori(0, NBLK) as i:
            ffn(i, F[0])
            power(ve[:, :], rstd[:, :], minus_half[:, 0:NT], Z["var"], Z["rstd"], i)
            power(ve[:, :], rstd[:, :], plus_half[:, 0:NT], Z["ss"], Z["rn"], i)
            eng.wait_ge(Z["cv"], NOUT * (i + 1))
            for t in range(1, T8):
                for c in range(NC):
                    eng.wait_ge(R["pr"], 2 * T8 * i + 2 * (t - 1) + c + 1)
                    keys = kT[:, c, 0:PB * t].rearrange("p (s n) -> p s n", s=t)
                    decay = aT[:, c, PB * t:PB * (t + 1)].unsqueeze(1).to_broadcast([P, t, PB])
                    g.tensor_tensor(keys, keys, decay, ALU.mult).then_inc(R["kd"], 1)
            power(var[:, :], rs[:, :], minus_half[:, :], O["var"], O["rs"], i)
            power(ve[:, :], rstd[:, :], plus_half[:, 0:NT], G["ss"], G["rn"], i)
            g.tensor_tensor(x[:, :, :], x[:, :, :], y[:, :, :], ALU.add).then_inc(G["xy"], 1)
            ffn(i, F[1])

    def dve(eng):
        v = nc.vector
        link = Link(eng, dve_link, const)
        eng.wait_ge(*const["a_done"])
        for t in (*w_r, *w_g1):
            v.memset(t[:, :, :].bitcast(F32), 0.0)
        for t in (*w_g2, *gT):
            v.memset(t[:, :].bitcast(F32), 0.0)
        v.memset(maskT[:, :], 0.0).then_inc(x_out, 32)
        v.memset(lg[:, :, 0:TOPK], BIG).then_inc(b_cleared, 1)
        eng.wait_ge(small_in, 16 * NSMALL)
        link(v.tensor_scalar(bg2[:, :], bg2[:, :], 1.0 / GATE_TEMP, None, ALU.mult))

        def layer_norm(i, out, S, done):
            for t in range(NT):
                last = v.bn_stats(stat[:, t, :], x[:, t, :])
            link(last, alone=True)
            for t in range(NT):
                last = v.bn_aggr(mv[:, t, :], stat[:, t, :])
            link(last)
            v.tensor_scalar(ve[:, :], mv[:, :, 1], LN_EPS, None, ALU.add).then_inc(S["var"], 1)
            eng.wait_ge(S["rstd"], i + 1)
            for t in range(NT):
                last = v.tensor_scalar(out[:, t, :], x[:, t, :], mv[:, t, 0:1], rstd[:, t:t + 1],
                                       ALU.subtract, ALU.mult)
            done(last)

        def rms_norm(i, S):
            link(v.tensor_tensor(sq_rows, y[:, :, :], y[:, :, :], ALU.mult))
            v.tensor_reduce(ve[:, :], sq_rows, AX_X, ALU.add).then_inc(S["ss"], 1)
            eng.wait_ge(S["rn"], i + 1)
            link(v.tensor_scalar(ve[:, :], rstd[:, :], float(D) ** -0.5, RMS_EPS, ALU.mult, ALU.add))
            link(v.reciprocal(mu[:, 0:NT], ve[:, :]))
            for t in range(NT):
                last = v.tensor_scalar(tok[:, t, :], y[:, t, :], mu[:, t:t + 1], None, ALU.mult)
            last.then_inc(S["src"], 1)

        def low(i, S, scale=None):
            for c in range(NC):
                eng.wait_ge(S["hi"], NC * i + c + 1)
                v.scalar_tensor_tensor(xT[1][:, c, :], ps[:, c, :], 1.0 if scale is None else scale[:, c:c + 1],
                                       xT[0][:, c, :].bitcast(F32), ALU.mult, ALU.subtract).then_inc(S["lo"], 1)

        def split_h(m, src, S):
            link(v.tensor_copy(h[0][:, m, :], src))
            v.tensor_tensor(h[1][:, m, :], src, h[0][:, m, :].bitcast(F32), ALU.subtract).then_inc(S["hl"], 1)

        def add_down(i, S, bank, out):
            for k in range(2):
                eng.wait_ge(S["dn"], 2 * i + k + 1)
                rows = out[:, 2 * k:2 * k + 2, :]
                last = v.tensor_tensor(rows, ps[:, bank + k, :].rearrange("p (t c) -> p t c", t=2), rows, ALU.add)
            return last

        def ffn(i, S):
            layer_norm(i, tok, S, lambda last: last.then_inc(S["src"], 1))
            low(i, S)
            eng.wait_ge(S["lg"], i + 1)
            logits = ps[:, 3, 0:NT * NE].rearrange("p (t e) -> p t e", t=NT)
            link(v.tensor_reduce(lmax[:, :], logits, AX_X, ALU.max))
            link(v.tensor_tensor(lg[:, :, TOPK:], logits, lmax[:, :].unsqueeze(2).to_broadcast([P, NT, NE]),
                                 ALU.subtract))
            link(v.tensor_scalar(lg[:, :, TOPK:], lg[:, :, TOPK:], UNDER, None, ALU.max), alone=True)
            for t in range(NT):
                last = v.max(top8[:, t, :], lg[:, t, :])
            link(last, alone=True)
            for t in range(NT):
                last = v.match_replace(lg_out[:, t, :], top8[:, t, :], lg[:, t, :], GONE)
            link(last)
            v.tensor_scalar(mask[:, :, :], lg_out[:, :, TOPK:], GONE, 1.0, ALU.is_equal,
                            ALU.subtract).then_inc(S["mk"], 1)
            for m in range(NM):
                eng.wait_ge(S["relu"], NM * i + m + 1)
                split_h(m, hf[m % 2][:, :], S)
            eng.wait_ge(S["biased"], i + 1)
            add_down(i, S, 2, x).then_inc(S["out"], 1)
            eng.wait_ge(S["out"], i + 1)

        def recurrence(i):
            def product(s):
                t, c = divmod(s, NC)
                if t:
                    eng.wait_ge(R["kd"], 2 * (T8 - 1) * i + s - 1)
                if s >= 2:
                    eng.wait_ge(R["hs"], 2 * T8 * i + s - 1)
                shape = [P, t + 1, PB]
                v.tensor_tensor(pr[c][:, 0:PB * (t + 1)].rearrange("p (s n) -> p s n", n=PB),
                                kT[:, c, 0:PB * (t + 1)].rearrange("p (s n) -> p s n", n=PB),
                                qT[:, c, PB * t:PB * (t + 1)].unsqueeze(1).to_broadcast(shape),
                                ALU.mult).then_inc(R["pr"], 1)

            product(0)
            for s in range(2 * T8):
                if s + 1 < 2 * T8:
                    product(s + 1)
                t, c = divmod(s, NC)
                eng.wait_ge(R["hs"], 2 * T8 * i + s + 1)
                out = oT[:, c, PB * t:PB * (t + 1)]
                if t == 0:
                    v.tensor_tensor(out, ps[:, c, 0:PB], vT[:, c, 0:PB], ALU.mult).then_inc(R["w"], 1)
                    continue
                v.tensor_tensor(w[:, 0:PB * (t + 1)], ps[:, c, 0:PB * (t + 1)], vT[:, c, 0:PB * (t + 1)],
                                ALU.mult).then_inc(R["w"], 1)
                eng.wait_ge(R["w"], 2 * T8 * i + s + 1)
                last = v.tensor_reduce(out, w[:, 0:PB * (t + 1)].rearrange("p (s n) -> p n s", n=PB), AX_X, ALU.add)
                if s < 2 * T8 - 1:
                    link(last)
            last.then_inc(O["os"], 1)

        eng.wait_ge(b_init, 6)
        eng.wait_ge(b_cleared, 1)
        with eng.Fori(0, NBLK) as i:
            link.enter(i, DVE_LINKS_B)
            eng.wait_ge(x_in, 32 * (i + 1))
            ffn(i, F[0])
            layer_norm(i, y, Z, link)
            rms_norm(i, Z)
            low(i, Z, s1)
            eng.wait_ge(Z["cv"], NOUT * i + 1)
            g_in = hf[0][0:NE, :]
            link(v.tensor_copy(gT[0][0:NE, :], g_in))
            v.tensor_tensor(gT[1][0:NE, :], g_in, gT[0][0:NE, :].bitcast(F32), ALU.subtract).then_inc(Z["ghs"], 1)
            for k in range(2):
                eng.wait_ge(Z["og"], 2 * i + k + 1)
                last = v.tensor_tensor(og[:, 2 * k:2 * k + 2, :], ps[:, 2 + k, :].rearrange("p (t c) -> p t c", t=2),
                                       bog_all[:, :].unsqueeze(1).to_broadcast([P, 2, D]), ALU.add)
            last.then_inc(Z["ogb"], 1)
            eng.wait_ge(Z["cv"], NOUT * (i + 1))
            recurrence(i)
            for k in range(2):
                eng.wait_ge(O["ot"], 2 * i + k + 1)
                last = v.tensor_reduce(mu[:, 2 * k * H:2 * (k + 1) * H], ps[:, 2 + k, :].rearrange("p (g d) -> p g d", d=DH),
                                       AX_X, ALU.add)
            link(last)
            link(v.tensor_scalar(mu[:, :], mu[:, :], 1.0 / DH, None, ALU.mult))
            tokh = tok[:, :, :].rearrange("p t (h d) -> p (t h) d", d=DH)
            for k in range(2):
                part = slice(2 * k * H, 2 * (k + 1) * H)
                last = v.tensor_tensor(tokh[:, part, :], ps[:, 2 + k, :].rearrange("p (g d) -> p g d", d=DH),
                                       mu[:, part].unsqueeze(2).to_broadcast([P, 2 * H, DH]), ALU.subtract)
            link(last)
            sqh = sq_rows.rearrange("p t (h d) -> p (t h) d", d=DH)
            link(v.tensor_tensor(sqh, tokh, tokh, ALU.mult))
            link(v.tensor_reduce(var[:, :], sqh, AX_X, ALU.add))
            v.tensor_scalar(var[:, :], var[:, :], 1.0 / DH, LN_EPS, ALU.mult, ALU.add).then_inc(O["var"], 1)
            eng.wait_ge(O["rs"], i + 1)
            link(v.tensor_tensor(tokh, tokh, rs[:, :].unsqueeze(2).to_broadcast([P, NT * H, DH]), ALU.mult))
            eng.wait_ge(Z["ogs"], i + 1)
            v.tensor_tensor(tok[:, :, :], tok[:, :, :], og[:, :, :], ALU.mult).then_inc(O["src"], 1)
            low(i, O)
            for k in range(2):
                eng.wait_ge(O["wo"], 2 * i + k + 1)
                rows = y[:, 2 * k:2 * k + 2, :]
                last = v.tensor_tensor(rows, ps[:, 4 + k, :].rearrange("p (t c) -> p t c", t=2), rows, ALU.add)
            link(last)
            rms_norm(i, G)
            low(i, G, s2)
            for m in range(NM):
                eng.wait_ge(G["silu"], NM * i + m + 1)
                eng.wait_ge(G["up"], NM * i + m + 1)
                if m >= 2:
                    eng.wait_ge(G["hl"], NM * i + m - 1)
                v.tensor_tensor(hp[m % 2][:, :], ps[:, 6 + m % 2, :], hf[m % 2][:, :], ALU.mult).then_inc(G["pd"], 1)
                eng.wait_ge(G["pd"], NM * i + m + 1)
                split_h(m, hp[m % 2][:, :], G)
            eng.wait_ge(G["xy"], i + 1)
            link(add_down(i, G, 2, x))
            ffn(i, F[1])
            link.leave(NBLK)

    def act(eng):
        a = nc.scalar
        eng.wait_ge(*const["a_done"])
        eng.wait_ge(b_cleared, 1)
        for n, (_, _, ws) in enumerate(pieces):
            eng.wait_ge(stage_in[n % 2], 16 * (n // 2 + 1))
            a.activation(ws[0], staged(n), ACT.Copy).then_inc(stage_hi, 1)

        def high(i, S, scale=None):
            for c in range(NC):
                eng.wait_ge(S["tr"], NC * i + c + 1)
                if scale is None:
                    a.activation(xT[0][:, c, :], ps[:, c, :], ACT.Copy).then_inc(S["hi"], 1)
                else:
                    a.activation(xT[0][:, c, :], ps[:, c, :], ACT.Identity, scale=scale[:, c:c + 1]).then_inc(S["hi"], 1)

        def ffn(i, S):
            high(i, S)
            eng.wait_ge(S["rt"], i + 1)
            a.activation(logT[:, :], ps[0:NE, 2, :], ACT.Identity, bias=rb[:, :]).then_inc(S["lt"], 1)
            eng.wait_ge(S["mt"], i + 1)
            a.activation(maskT[0:NE, :], ps[0:NE, 2, :], ACT.Copy).then_inc(S["mtb"], 1)
            for m in range(NM):
                eng.wait_ge(S["up"], NM * i + m + 1)
                if m >= 2:
                    eng.wait_ge(S["hl"], NM * i + m - 1)
                a.activation(hf[m % 2][:, :], ps[:, 4 + m % 4, :], ACT.Relu, bias=b1[:, m:m + 1]).then_inc(S["relu"], 1)

        def projections(i, ns):
            for n in ns:
                eng.wait_ge(Z["out"], NOUT * i + n + 1)
                src = ps[:, 4 + n % 4, :]
                if n == 0:
                    ins = a.activation(hf[0][0:NE, :], src[0:NE, :], ACT.Silu, bias=bg1[:, :])
                elif n < 7:
                    c, k = divmod(n - 1, 3)
                    ins = a.activation((kT, qT, vT)[k][:, c, :], src, ACT.Copy)
                else:
                    ins = a.activation(aT[:, n - 7, :], src, ACT.Sigmoid, bias=bg2[:, n - 7:n - 6], scale=1.0 / GATE_TEMP)
                ins.then_inc(Z["cv"], 1)

        eng.wait_ge(b_init, 6)
        eng.wait_ge(b_cleared, 1)
        eng.wait_ge(small_in, 16 * NSMALL)
        with eng.Fori(0, NBLK) as i:
            ffn(i, F[0])
            high(i, Z, s1)
            projections(i, range(0, 4))
            eng.wait_ge(Z["ogb"], i + 1)
            a.activation(og[:, :, :], og[:, :, :], ACT.Silu).then_inc(Z["ogs"], 1)
            projections(i, range(4, NOUT))
            high(i, O)
            high(i, G, s2)
            for m in range(NM):
                eng.wait_ge(G["gate"], NM * i + m + 1)
                if m >= 2:
                    eng.wait_ge(G["pd"], NM * i + m - 1)
                a.activation(hf[m % 2][:, :], ps[:, 4 + m % 2, :], ACT.Silu).then_inc(G["silu"], 1)
            ffn(i, F[1])

    def pe(eng):
        t_ = nc.tensor

        def transposed(i, S):
            eng.wait_ge(S["src"], i + 1)
            for c in range(NC):
                for t in range(NT):
                    last = t_.transpose(ps[:, c, t * P:(t + 1) * P], tok[:, t, c * P:(c + 1) * P], ident[:, :])
                last.then_inc(S["tr"], 1)
            eng.wait_ge(S["lo"], NC * (i + 1))

        def channels(bank, ws, m, close=True):
            n = 0
            for c in range(NC):
                for a, k in PASSES:
                    last = t_.matmul(ps[:, bank, :], ws[a][:, c, m * P:(m + 1) * P], xT[k][:, c, :],
                                     start=n == 0, stop=close and n == NC * len(PASSES) - 1)
                    n += 1
            return last

        def rows(bank, ws, done):
            for t in range(NT):
                n = 0
                for c in range(NC):
                    for a, k in PASSES:
                        last = t_.matmul(ps[:, bank + t // 2, (t % 2) * D:(t % 2 + 1) * D],
                                         xT[a][:, c, t * P:(t + 1) * P], ws[k][:, c, :],
                                         start=n == 0, stop=n == NC * len(PASSES) - 1)
                        n += 1
                if t % 2:
                    last.then_inc(done, 1)

        def down(i, ws, S):
            eng.wait_ge(S["hl"], NM * (i + 1))
            for t in range(NT):
                n = 0
                for m in range(NM):
                    for a, k in PASSES:
                        last = t_.matmul(ps[:, 2 + t // 2, (t % 2) * D:(t % 2 + 1) * D],
                                         h[a][:, m, t * P:(t + 1) * P], ws[k][:, m, :],
                                         start=n == 0, stop=n == NM * len(PASSES) - 1)
                        n += 1
                if t % 2:
                    last.then_inc(S["dn"], 1)

        def ffn(i, S):
            transposed(i, S)
            channels(2, w_r, 0).then_inc(S["rt"], 1)
            channels(4, w1, 0, close=False)
            constant_wait(eng, const)
            eng.wait_ge(S["lt"], i + 1)
            for t in range(NT):
                last = t_.transpose(ps[:, 3, t * NE:(t + 1) * NE], logT[:, t * P:(t + 1) * P], ident[0:NE, 0:NE])
            last.then_inc(S["lg"], 1)
            for m in range(1, 4):
                channels(4 + m, w1, m, close=False)
            eng.wait_ge(S["mk"], i + 1)
            for t in range(NT):
                last = t_.transpose(ps[0:NE, 2, t * P:(t + 1) * P], mask[:, t, :], ident[:, :])
            last.then_inc(S["mt"], 1)
            eng.wait_ge(S["mtb"], i + 1)
            for m in range(NM):
                if m >= 4:
                    eng.wait_ge(S["relu"], NM * i + m - 3)
                    channels(4 + m % 4, w1, m, close=False)
                t_.matmul(ps[:, 4 + m % 4, :], expand[:, m * P:(m + 1) * P], maskT[:, :],
                          start=False, stop=True).then_inc(S["up"], 1)
            down(i, w2, S)

        eng.wait_ge(b_init, 6)
        eng.wait_ge(b_cleared, 1)
        eng.wait_ge(stage_lo, len(pieces))
        with eng.Fori(0, NBLK) as i:
            ffn(i, F[0])
            transposed(i, Z)
            outs = [(w_g1, 0)] + [(ws, c) for c in range(NC) for ws in (w_k, w_q, w_v)]
            for n, (ws, c) in enumerate(outs):
                if n >= 4:
                    eng.wait_ge(Z["cv"], NOUT * i + n - 3)
                channels(4 + n % 4, ws, c).then_inc(Z["out"], 1)
                if n == 3:
                    rows(2, w_og, Z["og"])
            eng.wait_ge(Z["ghs"], i + 1)
            for c in range(NC):
                n = len(outs) + c
                eng.wait_ge(Z["cv"], NOUT * i + n - 3)
                for k, (a, b) in enumerate(PASSES):
                    last = t_.matmul(ps[:, 4 + n % 4, :], w_g2[a][:, c * P:(c + 1) * P], gT[b][:, :],
                                     start=k == 0, stop=k == len(PASSES) - 1)
                last.then_inc(Z["out"], 1)
            for s in range(2 * T8):
                t, c = divmod(s, NC)
                eng.wait_ge(R["pr"], 2 * T8 * i + s + 1)
                if s >= 2:
                    eng.wait_ge(R["w"], 2 * T8 * i + s - 1)
                t_.matmul(ps[:, c, 0:PB * (t + 1)], head_sum[:, :], pr[c][:, 0:PB * (t + 1)],
                          start=True, stop=True).then_inc(R["hs"], 1)
            eng.wait_ge(O["os"], i + 1)
            for t in range(NT):
                for c in range(NC):
                    at = (t % 2) * D + c * P
                    last = t_.transpose(ps[:, 2 + t // 2, at:at + P], oT[:, c, t * P:(t + 1) * P], ident[:, :])
                if t % 2:
                    last.then_inc(O["ot"], 1)
            transposed(i, O)
            rows(4, w_o, O["wo"])
            transposed(i, G)
            for m in range(NM):
                if m >= 2:
                    eng.wait_ge(G["silu"], NM * i + m - 1)
                channels(4 + m % 2, w_gate, m).then_inc(G["gate"], 1)
                if m >= 2:
                    eng.wait_ge(G["pd"], NM * i + m - 1)
                channels(6 + m % 2, w_up, m).then_inc(G["up"], 1)
            down(i, w_down, G)
            ffn(i, F[1])

    return locals()


def build(nc, dram):
    ctx = ExitStack()
    with ctx:
        sb = lambda name, shape, dt: ctx.enter_context(nc.sbuf_tensor(name, shape, dt))
        sem = lambda name: ctx.enter_context(nc.semaphore(name))
        ps = ctx.enter_context(nc.psum_tensor("ps", [P, 8, 512], F32))
        ident = sb("ident", [P, P], F32)
        minus_half = sb("minus_half", [P, NT * H], F32)
        plus_half = sb("plus_half", [P, NT], F32)
        const_ready = sem("const_ready")
        tiny = sb("tiny", [P, 2], F32)
        const = {"ident": ident, "minus_half": minus_half, "plus_half": plus_half, "ready": const_ready, "count": 5, "tiny": tiny}
        arena = ExitStack()
        sb_a = lambda name, shape, dt: arena.enter_context(nc.sbuf_tensor(name, shape, dt))
        with arena:
            A = attention(nc, ctx, dram, sb_a, ps, sem, const)
            A2 = project(nc, dram, sb_a, ps, sem, const, A)
        const["a_done"] = (A2["x1_out"], 32 + 16 * B)
        second = lambda name, shape, dt: ctx.enter_context(nc.sbuf_tensor(name, shape, dt))

        @contextmanager
        def alias():
            with ExitStack() as own:
                yield lambda name, shape, dt: own.enter_context(nc.sbuf_tensor(name, shape, dt))

        BB = block_part(nc, dram, second, alias, ps, sem, const)
        block = ctx.enter_context(nc.Block())

        @block.sync
        def _(eng):
            A["sp"](eng)
            A2["sp"](eng)
            BB["sp"](eng)

        @block.gpsimd
        def _(eng):
            nc.gpsimd.memset(ident[:, :], 0.0).then_inc(const_ready, 1)
            nc.gpsimd.memset(minus_half[:, :], -0.5).then_inc(const_ready, 1)
            nc.gpsimd.memset(plus_half[:, :], 0.5).then_inc(const_ready, 1)
            nc.gpsimd.memset(tiny[:, :], 0.0).then_inc(const_ready, 1)
            eng.wait_ge(const_ready, 4)
            nc.gpsimd.affine_select(out=ident[:, :], in_=ident[:, :], compare_op=ALU.not_equal, fill=1.0,
                                    base=0, pattern=[[-1, P]], channel_multiplier=1).then_inc(const_ready, 1)
            A["pool"](eng)
            A2["pool"](eng)
            BB["pool"](eng)

        @block.vector
        def _(eng):
            eng.wait_ge(const_ready, const["count"])
            A["dve"](eng)
            eng.wait_ge(A["selT_ready"], 1)
            A2["dve"](eng)
            BB["dve"](eng)

        @block.scalar
        def _(eng):
            A["act"](eng)
            A2["act"](eng)
            BB["act"](eng)

        @block.tensor
        def _(eng):
            A["pe"](eng)
            A2["pe"](eng)
            BB["pe"](eng)



_NAMES = {"x": "L0_attn_a_x", "Wq": "L0_attn_a_Wq", "Wk": "L0_attn_a_Wk", "Wv": "L0_attn_a_Wv", "Wo": "L0_attn_a_Wo",
          "bq": "L0_attn_a_bq", "bk": "L0_attn_a_bk", "bv": "L0_attn_a_bv", "bo": "L0_attn_a_bo",
          "w1": "L0_ffn_w1", "w2": "L0_ffn_w2", "rw": "L0_ffn_router_w", "b1": "L0_ffn_b1", "b2": "L0_ffn_b2",
          "rb": "L0_ffn_router_b", "wq": "L0_attn_b_wq", "wk": "L0_attn_b_wk", "wv": "L0_attn_b_wv",
          "wog": "L0_attn_b_wog", "wo": "L0_attn_b_wo", "wg1": "L0_attn_b_wg1", "wg2": "L0_attn_b_wg2",
          "bg1": "L0_attn_b_bg1", "bg2": "L0_attn_b_bg2", "bog": "L0_attn_b_bog", "s1": "L0_attn_b_scale1",
          "s2": "L0_attn_b_scale2", "w_gate": "L0_attn_b_w_gate", "w_up": "L0_attn_b_w_up", "w_down": "L0_attn_b_w_down"}
_TRANSPOSED = ("w1", "w2", "rw", "wq", "wk", "wv", "wog", "wo", "wg1", "wg2", "w_gate", "w_up", "w_down")
_COLUMNS = ("bq", "bk", "b1", "bg2", "s1", "s2")
_ONE_COLUMN = ("rb", "bg1")


def kernel(**inputs):
    import numpy as _np
    import concourse.bacc as _bacc
    from concourse import mybir as _mybir
    from concourse.bass_utils import run_bass_kernel_spmd as _run

    nc = _bacc.Bacc("TRN2", target_bir_lowering=False, num_devices=1)
    arrays, dram = {}, {}
    for key, name in _NAMES.items():
        a = _np.asarray(inputs[name])
        if key in _TRANSPOSED:
            a = a.T
        elif key in _COLUMNS:
            a = a.reshape(-1, P).T
        elif key in _ONE_COLUMN:
            a = a.reshape(-1, 1)
        a = _np.ascontiguousarray(a)
        arrays[f"in_{key}_dram"] = a
        dram[key] = nc.dram_tensor(f"in_{key}_dram", a.shape, _mybir.dt.from_np(a.dtype), kind="ExternalInput").ap()
    out = nc.dram_tensor("out_dram", (B, L, D), F32, kind="ExternalOutput").ap()
    x1 = nc.dram_tensor("x1_dram", (B, L, D), F32).ap()
    dram["spars"] = nc.dram_tensor("spars_dram", (B * H, L), F32).ap()
    dram["x_tiles"] = dram["x"].rearrange("b (t p) c -> p (b t) c", p=P)
    dram["x1_tiles"] = x1.rearrange("b (t p) c -> p (b t) c", p=P)
    dram["x1_blocks"] = x1.rearrange("(t e) l c -> e l t c", e=2)
    dram["out_blocks"] = out.rearrange("(t e) l c -> e l t c", e=2)
    build(nc, dram)
    r = _run(nc, [arrays], core_ids=[0])
    return r.results[0]["out_dram"]
```

```python
from contextlib import ExitStack

import concourse.bass as bass
from concourse import mybir

ALU = mybir.AluOpType
ACT = mybir.ActivationFunctionType
AX_X = mybir.AxisListType.X
F32 = mybir.dt.float32
F32R = mybir.dt.float32r
BF16 = mybir.dt.bfloat16

P = 128
B, L, D = 8, 512, 256
H, DH = 16, 16
NC = D // P
NT = L // P
HU = P // DH
NPAIR = HU // 2
NMS = NPAIR * NT
HG = 4
OR = DH + 1
KEEP = max(1, min(L, int(0.6 * L)))
DROP = L - KEEP
ROUNDS = -(-DROP // 8)
PADS = ROUNDS * 8 - DROP
BIG = 3.0e38
GONE = -3.2e38
LN_EPS = 1e-5
QS = 0.25
PASSES = ((0, 0), (0, 1), (1, 0))
VZ_STRIDE = 1160
PT_BUFS = 4
DVE_LINKS = 18
DVE_LINKS_B = 50

TASKS = [["V", "X0", "X1", "Q", "K", "O0", "mean", "mx", "O1"],
         ["V", "Q", "K", "O0", "mean", "mx", "O1"]]
TASKS_FIRST = ["X0", "X1", "Q0", "K0", "mean0", "Q1", "K1", "mean1", "V", "mx"]
AT = {"V": 1, "X0": 3, "X1": 4, "Q": 6, "K": 7, "O0": 8, "mean": 9, "mx": 13, "O1": 15}
SCORES_AT = [1, 1, 2, 1, 1, 2, 1, 1, 2, 1, 1, 2, 0, 0, 0, 0]
assert sum(SCORES_AT) == NMS


def tasks_of(b_last, g):
    if not b_last:
        return TASKS[g]
    return [t for t in TASKS[g] if t in (("V", "O0", "mx", "O1") if g == 0 else ("O0", "O1"))]


def per_batch(kinds):
    return sum(t in kinds for g in (0, 1) for t in TASKS[g])


def constant_wait(eng, const):
    eng.wait_ge(const["ready"], const["count"])


class Link:

    def __init__(self, eng, sem, const):
        self.eng, self.sem, self.const, self.base, self.n = eng, sem, const, 0, 0

    def __call__(self, ins, alone=False):
        ins.then_inc(self.sem, 1)
        self.n += 1
        self.eng.wait_ge(self.sem, self.base + self.n)
        if alone:
            tiny = self.const["tiny"]
            self.eng.tensor_copy(tiny[:, 1:2], tiny[:, 0:1])

    def enter(self, i, per):
        self.start, self.per = self.n + self.base, per
        self.base, self.n = self.start + per * i, 0

    def leave(self, times):
        assert self.n == self.per, (self.n, self.per)
        self.base, self.n = self.start + self.per * times, 0


def attention(nc, ctx, dram, sb, ps, sem, const):
    x_in = sb("x_in", [P, NT, D], F32)
    xn = sb("xn", [P, NT, D], F32)
    xT = sb("xT", [P, NC, L], F32)
    xT_hi = sb("xT_hi", [P, NC, L], F32R)
    xT_lo = sb("xT_lo", [P, NC, L], F32R)
    xT_parts = (xT_hi, xT_lo)
    q_st = [sb(f"q_st{i}", [P, NPAIR, L], F32R) for i in range(2)]
    k_st = [sb(f"k_st{i}", [P, NPAIR, L], F32R) for i in range(2)]
    qk_hi = [sb(n, [P, L], F32R) for n in ("q_hi", "k_hi")]
    qk_lo = [sb(n, [P, L], F32R) for n in ("q_lo", "k_lo")]
    vz = [sb(f"vz{i}", [P, NT, VZ_STRIDE], F32) for i in range(2)]
    pT = [sb(f"pT{i}", [P, 2, L], F32) for i in range(PT_BUFS)]
    oT = [sb(f"oT{i}", [P, L], F32) for i in range(2)]
    mx = sb("mx", [P, NT, HU], F32)
    ksum = sb("ksum", [P, 2], F32)
    kmean = sb("kmean", [P, HU], F32)
    kmean_w = [sb(f"kmean_w{i}", [P, P], F32R) for i in range(2)]
    mean_sb = [sb(f"mean{i}", [HU, L], F32) for i in range(2)]
    m_hi = sb("m_hi", [HU, L], F32R)
    m_lo = sb("m_lo", [HU, L], F32R)
    sp_u = sb("sp_u", [HU, L], F32)
    spars = sb("spars", [P, L], F32)
    race = sb("race", [P, PADS + L], F32)
    top8 = sb("top8", [P, 8], F32)
    sel = sb("sel", [P, L], F32)
    selT = sb("selT", [P, NT, P], F32)
    oa = sb("oa", [P, B * NT, D], F32)
    rden = sb("rden", [P, NT, HG], F32)
    stat = sb("stat", [P, NT, 6], F32)
    mv = sb("mv", [P, NT, 2], F32)
    ve = sb("ve", [P, NT], F32)
    rstd = sb("rstd", [P, NT], F32)
    stage = sb("stage_a", [P, NC, D], F32)
    w_q = [sb(f"wq_a{i}", [P, NC, D], F32R) for i in range(2)]
    w_k = [sb(f"wk_a{i}", [P, NC, D], F32R) for i in range(2)]
    w_o = [sb(f"wo_a{i}", [P, NC, D], F32R) for i in range(2)]
    w_v = sb("wv_a", [P, NC, D], F32)
    bq = sb("bq", [P, NC], F32)
    bk = sb("bk", [P, NC], F32)
    bkL = sb("bkL", [P, NC], F32)
    bv_all = sb("bv_all", [P, D], F32)
    bo_all = sb("bo_all", [P, D], F32)
    head_of = sb("head_of", [P, HU], F32)
    ident, minus_half = const["ident"], const["minus_half"]

    bank = [ps[:, k, :] for k in range(8)]
    o_bank, misc = bank[6], bank[7]

    w_in, w_ready = sem("w_in"), sem("w_ready")
    stage_in, stage_free = sem("stage_in"), sem("stage_free")
    x_loaded, x_next, xn_ready = sem("x_loaded"), sem("x_next"), sem("xn_ready")
    var_ready, rstd_ready = sem("var_ready"), sem("rstd_ready")
    xT_ready, xT_split = sem("xT_ready"), sem("xT_split")
    hi_ready, lo_ready = sem("hi_ready"), sem("lo_ready")
    st_in = [sem(f"st_in{j}") for j in range(NPAIR)]
    kmean_ready, mean_ready = sem("kmean_ready"), sem("mean_ready")
    v_ready = sem("v_ready")
    s_done, max_done = sem("s_done"), sem("max_done")
    sT_done, exp_done, pT_free = sem("sT_done"), sem("exp_done"), sem("pT_free")
    oT_ready = sem("oT_ready")
    task_done, task_free = sem("task_done"), sem("task_free")
    m_ready, m_in, sp_in = sem("m_ready"), sem("m_in"), sem("sp_in")
    sp_out = sem("sp_out")
    sel_ready, selT_done, selT_ready = sem("sel_ready"), sem("selT_done"), sem("selT_ready")
    init_done = sem("init_done")
    dve_link = sem("dve_link")
    NPRO = len(TASKS_FIRST)
    NTASK = sum(map(len, TASKS))

    def task_no(b, last, g, kind):
        names = [(g_, t) for g_ in (0, 1) for t in tasks_of(last, g_)]
        return NPRO + NTASK * b + names.index((g, kind))

    def sp(eng):
        ld = lambda out, in_, s: eng.dma_start(out, in_).then_inc(s, 16)
        ld(x_in[:, :, :], dram["x"][0].rearrange("(t p) c -> p t c", p=P), x_loaded)
        for n, name in enumerate(("Wq", "Wk", "Wo")):
            if n:
                eng.wait_ge(stage_free, n)
            ld(stage[:, :, :], dram[name].rearrange("(c p) n -> p c n", p=P), stage_in)
        ld(w_v[:, :, :], dram["Wv"].rearrange("(c p) n -> p c n", p=P), w_in)
        ld(bv_all[:, :], dram["bv"].partition_broadcast(P), w_in)
        ld(bo_all[:, :], dram["bo"].partition_broadcast(P), w_in)

        def stack(w, j, buf):
            for parts, dst in (((qk_hi[0], qk_hi[0], qk_lo[0]), q_st[buf]),
                               ((qk_hi[1], qk_lo[1], qk_hi[1]), k_st[buf])):
                for r, src in enumerate(parts):
                    for e in range(2):
                        ld(dst[64 * e + DH * r:64 * e + DH * r + DH, j, :].bitcast(F32),
                           src[(2 * j + e) * DH:(2 * j + e + 1) * DH, :].bitcast(F32), st_in[j])

        def m_rows(w, buf):
            eng.wait_ge(m_ready, w + 1)
            for e in range(2):
                for r, src in enumerate((m_hi, m_lo)):
                    at = 64 * e + 3 * DH + r
                    ld(q_st[buf][at:at + 1, :, :].bitcast(F32), src[e::2, :].bitcast(F32), m_in)
            ld(dram["spars"][bass.ds(w * HU, HU), :], sp_u[:, :], sp_out)

        eng.wait_ge(init_done, 5)
        for w in range(2):
            eng.wait_ge(lo_ready, 2 * w + 2)
            for j in range(NPAIR):
                stack(w, j, w)
        m_rows(0, 0)

        def step(b, g, last):
            u = 2 * b + g
            if not last:
                eng.wait_ge(lo_ready, 2 * (u + 2) + 2)
                for j in range(NPAIR // 2):
                    eng.wait_ge(sT_done, NMS * u + NT * (j + 1))
                    stack(u + 2, j, g)
            if not (last and g == 1):
                m_rows(u + 1, 1 - g)
            if not last:
                for j in range(NPAIR // 2, NPAIR):
                    eng.wait_ge(sT_done, NMS * u + NT * (j + 1))
                    stack(u + 2, j, g)

        with eng.Fori(0, B - 1) as b:
            step(b, 0, False)
            step(b, 1, False)
        step(B - 1, 0, True)
        step(B - 1, 1, True)
        eng.wait_ge(sp_out, 16 * 2 * B)
        ld(spars[:, :], dram["spars"][:, :], sp_in)

    def pool(eng):
        g = nc.gpsimd
        g.memset(head_of[:, :], 1.0).then_inc(init_done, 1)
        eng.wait_ge(init_done, 3)
        g.affine_select(out=head_of[:, :], in_=head_of[:, :], compare_op=ALU.is_ge, fill=0.0,
                        base=0, pattern=[[-DH, HU]], channel_multiplier=1).then_inc(init_done, 1)
        eng.wait_ge(init_done, 4)
        g.affine_select(out=head_of[:, :], in_=head_of[:, :], compare_op=ALU.is_ge, fill=0.0,
                        base=DH - 1, pattern=[[DH, HU]], channel_multiplier=-1).then_inc(init_done, 1)

        def power(i):
            eng.wait_ge(var_ready, i + 1)
            g.tensor_tensor(rstd[:, :], ve[:, :], minus_half[:, 0:NT], ALU.pow).then_inc(rstd_ready, 1)

        power(0)
        with eng.Fori(0, B - 1) as b:
            eng.wait_ge(xn_ready, b + 1)
            g.dma_start(x_in[:, :, :], dram["x_tiles"][:, bass.ts(b + 1, NT), :]).then_inc(x_next, 16)
            power(b + 1)

    def dve(eng):
        v = nc.vector
        link = Link(eng, dve_link, const)
        for buf in range(2):
            v.memset(q_st[buf][:, :, :].bitcast(F32), 0.0)
            v.memset(k_st[buf][:, :, :].bitcast(F32), 1.0)
            v.memset(kmean_w[buf][:, :].bitcast(F32), 0.0)
            link(v.memset(vz[buf][:, :, :], 0.0))
        v.memset(rden[:, :, :], 1.0).then_inc(pT_free, PT_BUFS)
        v.memset(mean_sb[0][:, :], 0.0).then_inc(exp_done, 1)
        v.memset(mean_sb[1][:, :], 0.0).then_inc(oT_ready, 1)
        v.memset(sp_u[:, :], 0.0).then_inc(task_free, 1)
        for buf in range(2):
            for gr in range(HU // HG):
                at = gr * HG * P + DH
                last = v.memset(vz[buf][:, :, at:at + HG * (P + OR)]
                                .rearrange("p t (h c) -> p t h c", c=P + OR)[:, :, :, 0:1], 1.0)
        last.then_inc(init_done, 1)
        v.memset(race[:, 0:PADS], BIG).then_inc(init_done, 1)

        for n, (w, s) in enumerate(((w_q, QS), (w_k, 1.0), (w_o, 1.0))):
            eng.wait_ge(stage_in, 16 * (n + 1))
            link(v.tensor_scalar(w[0][:, :, :], stage[:, :, :], s, None, ALU.mult))
            v.scalar_tensor_tensor(w[1][:, :, :], stage[:, :, :], s, w[0][:, :, :].bitcast(F32),
                                   ALU.mult, ALU.subtract).then_inc(stage_free, 1)
        eng.wait_ge(w_in, 16 * 5)
        link(v.tensor_scalar(bq[:, :], bq[:, :], QS, None, ALU.mult))
        v.tensor_scalar(bkL[:, :], bk[:, :], float(L), None, ALU.mult).then_inc(w_ready, 1)

        def layer_norm(i):
            if isinstance(i, int):
                eng.wait_ge(x_loaded, 16)
            else:
                eng.wait_ge(x_next, 16 * i)
            for t in range(NT):
                last = v.bn_stats(stat[:, t, :], x_in[:, t, :])
            link(last, alone=True)
            for t in range(NT):
                last = v.bn_aggr(mv[:, t, :], stat[:, t, :])
            link(last)
            v.tensor_scalar(ve[:, :], mv[:, :, 1], LN_EPS, None, ALU.add).then_inc(var_ready, 1)

        def normalise(i):
            eng.wait_ge(rstd_ready, i + 1)
            for t in range(NT):
                last = v.tensor_scalar(xn[:, t, :], x_in[:, t, :], mv[:, t, 0:1], rstd[:, t:t + 1],
                                       ALU.subtract, ALU.mult)
            last.then_inc(xn_ready, 1)

        def split_x(no, i):
            c = no
            eng.wait_ge(xT_ready, i + 1)
            link(v.tensor_copy(xT_hi[:, c, :], xT[:, c, :]))
            v.tensor_tensor(xT_lo[:, c, :], xT[:, c, :], xT_hi[:, c, :].bitcast(F32),
                            ALU.subtract).then_inc(xT_split, 1)

        def low(which, w, g):
            bias = (bq, bk)[which]
            eng.wait_ge(hi_ready, 2 * w + which + 1)
            v.scalar_tensor_tensor(qk_lo[which][:, :], misc[:, :], bias[:, g:g + 1],
                                   qk_hi[which][:, :].bitcast(F32), ALU.add,
                                   ALU.subtract).then_inc(lo_ready, 1)
            if which == 0:
                return
            link(v.tensor_reduce(ksum[:, 0:1], misc[:, :], AX_X, ALU.add))
            link(v.tensor_tensor(ksum[:, 1:2], ksum[:, 0:1], bkL[:, g:g + 1], ALU.add))
            link(v.tensor_scalar(kmean[:, :], head_of[:, :], ksum[:, 1:2], 1.0 / L, ALU.mult, ALU.mult))
            link(v.tensor_copy(kmean_w[0][:, 0:HU], kmean[:, :]))
            v.tensor_tensor(kmean_w[1][:, 0:HU], kmean[:, :], kmean_w[0][:, 0:HU].bitcast(F32),
                            ALU.subtract).then_inc(kmean_ready, 1)

        def values(g, no):
            eng.wait_ge(task_done, no + 1)
            for gr in range(HU // HG):
                at = gr * HG * P
                out = vz[g][:, :, at:at + HG * (P + OR)].rearrange(
                    "p t (h c) -> p t h c", c=P + OR)[:, :, :, 0:DH]
                cols = slice(gr * HG * DH, (gr + 1) * HG * DH)
                src = misc[:, :].rearrange("p (t c) -> p t c", t=NT)[:, :, cols].rearrange(
                    "p t (h d) -> p t h d", d=DH)
                bias = bv_all[:, g * P:(g + 1) * P][:, cols].rearrange("p (h d) -> p h d", d=DH)
                last = v.tensor_tensor(out, src, bias.unsqueeze(1).to_broadcast([P, NT, HG, DH]), ALU.add)
            return last

        def score_max(n, i):
            j, qt = divmod(i, NT)
            eng.wait_ge(s_done, n + 1)
            v.tensor_reduce(mx[:, qt, 2 * j:2 * j + 2], ps[:, 0:2, :], AX_X, ALU.max).then_inc(max_done, 1)

        def maxima(w, no, par):
            eng.wait_ge(task_done, no + 1)
            if not (isinstance(w, int) and w == 0):
                eng.wait_ge(m_in, 64 * w)
                eng.wait_ge(sp_out, 16 * w)
            link(v.tensor_scalar(m_hi[:, :], misc[0:HU, :], -1.0, None, ALU.mult))
            v.scalar_tensor_tensor(m_lo[:, :], misc[0:HU, :], -1.0, m_hi[:, :].bitcast(F32),
                                   ALU.mult, ALU.subtract)
            eng.wait_ge(mean_ready, w + 1)
            v.tensor_tensor(sp_u[:, :], misc[0:HU, :], mean_sb[par][:, :],
                            ALU.subtract).then_inc(m_ready, 1)

        def outputs(b, g, gr, no):
            eng.wait_ge(task_done, no + 1)
            src = misc[:, 0:NT * HG * OR].rearrange("p (t h c) -> p t h c", t=NT, h=HG)
            link(v.reciprocal(rden[:, :, :], src[:, :, :, DH]))
            at = g * P + gr * HG * DH
            out = oa[:, bass.ts(b, NT), at:at + HG * DH].rearrange("p t (h d) -> p t h d", h=HG)
            v.tensor_tensor(out, src[:, :, :, 0:DH],
                            rden[:, :, :].unsqueeze(3).to_broadcast([P, NT, HG, DH]),
                            ALU.mult).then_inc(task_free, 1)

        layer_norm(0)
        normalise(0)
        eng.wait_ge(init_done, 5)
        split_x(0, 0)
        split_x(1, 1)
        for w in range(2):
            low(0, w, w)
            low(1, w, w)
        values(0, TASKS_FIRST.index("V")).then_inc(v_ready, 1)
        for i in range(NMS):
            score_max(i, i)
        maxima(0, TASKS_FIRST.index("mx"), 0)

        def step(b, g, last):
            u = 2 * b + g
            n = 0
            todo = tasks_of(last, g)
            for m in range(NMS):
                scores = 0 if last and g == 1 else SCORES_AT[m]
                if scores:
                    score_max(NMS * (u + 1) + n, n)
                if not last and g == 0 and m == 0:
                    layer_norm(b + 1)
                if not last and g == 0 and m == 1:
                    normalise(b + 1)
                for t in todo:
                    if AT[t] != m:
                        continue
                    no = task_no(b, last, g, t)
                    if t == "V":
                        values(1 - g, no).then_inc(v_ready, 1)
                    elif t[0] == "X":
                        split_x(int(t[1]), 2 * (b + 1) + int(t[1]))
                    elif t in "QK":
                        low("QK".index(t), u + 2, g)
                    elif t[0] == "O":
                        outputs(b, g, int(t[1]), no)
                    elif t == "mx":
                        maxima(u + 1, no, 1 - g)
                if scores == 2:
                    score_max(NMS * (u + 1) + n + 1, n + 1)
                n += scores

        with eng.Fori(0, B - 1) as b:
            link.enter(b, DVE_LINKS)
            step(b, 0, False)
            step(b, 1, False)
            link.leave(B - 1)
        step(B - 1, 0, True)
        step(B - 1, 1, True)

        eng.wait_ge(sp_in, 16)
        link(v.tensor_scalar(race[:, PADS:], spars[:, ::-1], -1.0, None, ALU.mult))
        for _ in range(ROUNDS):
            link(v.max(top8[:, :], race[:, :]))
            link(v.match_replace(race[:, :], top8[:, :], race[:, :], GONE))
        v.tensor_scalar(sel[:, :], race[:, PADS:][:, ::-1], GONE, None,
                        ALU.not_equal).then_inc(sel_ready, 1)
        eng.wait_ge(selT_done, 1)
        v.tensor_copy(selT[:, :, :], bank[0][:, :].rearrange("p (t r) -> p t r", t=NT)).then_inc(selT_ready, 1)
        return link

    def act(eng):
        a = nc.scalar
        a.dma_start(bq[:, :], dram["bq"]).then_inc(w_in, 16)
        a.dma_start(bk[:, :], dram["bk"]).then_inc(w_in, 16)

        def x_out(c, no):
            eng.wait_ge(task_done, no + 1)
            a.activation(xT[:, c, :], misc[:, :], ACT.Copy).then_inc(xT_ready, 1)

        def high(which, w, g, no):
            bias = (bq, bk)[which]
            eng.wait_ge(task_done, no + 1)
            if which == 0 and not (isinstance(w, int) and w == 0):
                for j in range(NPAIR):
                    eng.wait_ge(st_in[j], 16 * 12 * w)
            a.activation(qk_hi[which][:, :], misc[:, :], ACT.Identity,
                         bias=bias[:, g:g + 1]).then_inc(hi_ready, 1)

        def mean_out(par, no):
            eng.wait_ge(task_done, no + 1)
            a.activation(mean_sb[par][:, :], misc[0:HU, :], ACT.Copy).then_inc(mean_ready, 1)

        def o_out(u, gr):
            eng.wait_ge(pT_free, PT_BUFS + NMS * u + NMS // 2 * (gr + 1))
            a.activation(oT[gr][:, :], o_bank[:, :], ACT.Copy).then_inc(oT_ready, 1)

        def exps(u, m):
            n = NMS * u + m
            eng.wait_ge(sT_done, n + 1)
            eng.wait_ge(pT_free, n + 1)
            a.activation(pT[m % PT_BUFS][:, :, :], ps[:, 2 + 2 * (m % 2):4 + 2 * (m % 2), :],
                         ACT.Exp).then_inc(exp_done, 1)

        eng.wait_ge(w_ready, 1)
        x_out(0, 0)
        x_out(1, 1)
        for w in range(2):
            high(0, w, w, TASKS_FIRST.index(f"Q{w}"))
            high(1, w, w, TASKS_FIRST.index(f"K{w}"))
            mean_out(w, TASKS_FIRST.index(f"mean{w}"))

        def step(b, g, last):
            u = 2 * b + g
            todo = tasks_of(last, g)
            for m in range(NMS):
                exps(u, m)
                for t in todo:
                    if AT[t] != m:
                        continue
                    no = task_no(b, last, g, t)
                    if t[0] == "X":
                        x_out(int(t[1]), no)
                    elif t in "QK":
                        high("QK".index(t), u + 2, g, no)
                    elif t == "mean":
                        mean_out(g, no)
                    elif t[0] == "O":
                        o_out(u, int(t[1]))

        with eng.Fori(0, B - 1) as b:
            step(b, 0, False)
            step(b, 1, False)
        step(B - 1, 0, True)
        step(B - 1, 1, True)

    def pe(eng):
        t_ = nc.tensor

        def x_task(c):
            for t in range(NT):
                last = t_.transpose(misc[:, t * P:(t + 1) * P], xn[:, t, c * P:(c + 1) * P], ident[:, :])
            last.then_inc(task_done, 1)

        def qk_task(which, g):
            w = (w_q, w_k)[which]
            n = 0
            for c in range(NC):
                for i, k in PASSES:
                    last = t_.matmul(misc[:, :], w[i][:, c, g * P:(g + 1) * P], xT_parts[k][:, c, :],
                                     start=n == 0, stop=n == NC * len(PASSES) - 1)
                    n += 1
            last.then_inc(task_done, 1)

        def v_task(g):
            for t in range(NT):
                for c in range(NC):
                    last = t_.matmul(misc[:, t * P:(t + 1) * P], xT[:, c, t * P:(t + 1) * P],
                                     w_v[:, c, g * P:(g + 1) * P], start=c == 0, stop=c == NC - 1)
            last.then_inc(task_done, 1)

        def mean_task():
            for n, (i, k) in enumerate(PASSES):
                last = t_.matmul(misc[:, :], kmean_w[i][:, :], (qk_hi[0], qk_lo[0])[k][:, :],
                                 start=n == 0, stop=n == len(PASSES) - 1)
            last.then_inc(task_done, 1)

        def mx_task():
            for t in range(NT):
                last = t_.transpose(misc[0:HU, t * P:(t + 1) * P], mx[:, t, :], ident[:, :])
            last.then_inc(task_done, 1)

        def o_task(gr):
            n = HG * OR
            for t in range(NT):
                last = t_.transpose(misc[:, t * n:(t + 1) * n], oT[gr][0:n, t * P:(t + 1) * P],
                                    ident[0:n, 0:n])
            last.then_inc(task_done, 1)

        def scores(n, i, buf):
            j, qt = divmod(i, NT)
            if not (isinstance(n, int) and n == 0):
                eng.wait_ge(max_done, n)
            for e in range(2):
                last = t_.matmul(bank[e][:, :],
                                 q_st[buf][64 * e:64 * e + 3 * DH, j, qt * P:(qt + 1) * P],
                                 k_st[buf][64 * e:64 * e + 3 * DH, j, :], start=True, stop=True)
            last.then_inc(s_done, 1)

        def scores_T(m, buf):
            j, kt = divmod(m, NT)
            for e in range(2):
                last = t_.matmul(bank[2 + 2 * (m % 2) + e][:, :],
                                 k_st[buf][64 * e:64 * e + 64, j, kt * P:(kt + 1) * P],
                                 q_st[buf][64 * e:64 * e + 64, j, :], start=True, stop=True)
            last.then_inc(sT_done, 1)

        def products(m, g):
            j, kt = divmod(m, NT)
            half = NMS // 2
            for e in range(2):
                h = 2 * j + e
                last = t_.matmul(o_bank[:, :], vz[g][:, kt, h * P:(h + 1) * P], pT[m % PT_BUFS][:, e, :],
                                 start=m % half == 0 and e == 0, stop=m % half == half - 1 and e == 1)
            last.then_inc(pT_free, 1)

        eng.wait_ge(init_done, 5)
        eng.wait_ge(const["ready"], const["count"])
        eng.wait_ge(w_ready, 1)
        eng.wait_ge(stage_free, 3)
        eng.wait_ge(xn_ready, 1)
        x_task(0)
        eng.wait_ge(xT_ready, 1)
        x_task(1)
        eng.wait_ge(xT_ready, 2)
        eng.wait_ge(xT_split, 2)
        for w in range(2):
            if w:
                eng.wait_ge(mean_ready, w)
            qk_task(0, w)
            eng.wait_ge(lo_ready, 2 * w + 1)
            qk_task(1, w)
            eng.wait_ge(kmean_ready, w + 1)
            mean_task()
        eng.wait_ge(mean_ready, 2)
        v_task(0)
        for i in range(NMS):
            if i % NT == 0:
                eng.wait_ge(st_in[i // NT], 16 * 12)
            scores(i, i, 0)
        eng.wait_ge(max_done, NMS)
        eng.wait_ge(v_ready, 1)
        mx_task()
        eng.wait_ge(m_in, 64)
        scores_T(0, 0)

        def step(b, g, last):
            u = 2 * b + g
            n = 0
            todo = tasks_of(last, g)
            for m in range(NMS):
                count = 0 if last and g == 1 else SCORES_AT[m]
                for k in range(count):
                    if k == 1:
                        continue
                    if n % NT == 0:
                        eng.wait_ge(st_in[n // NT], 16 * 12 * (u + 2))
                    scores(NMS * (u + 1) + n, n, 1 - g)
                if m < NMS - 1:
                    eng.wait_ge(exp_done, NMS * u + m + 1)
                    scores_T(m + 1, g)
                elif not (last and g == 1):
                    eng.wait_ge(exp_done, NMS * u + m + 1)
                    eng.wait_ge(m_in, 64 * (u + 2))
                    scores_T(0, 1 - g)
                if m != NMS - 1:
                    for t in todo:
                        if AT[t] == m:
                            task(b, last, g, t)
                eng.wait_ge(exp_done, NMS * u + m + 2)
                if m == 0:
                    eng.wait_ge(v_ready, u + 1)
                if m % (NMS // 2) == 0:
                    eng.wait_ge(oT_ready, 2 * u + m // (NMS // 2) + 1)
                products(m, g)
                if m == NMS - 1:
                    task(b, last, g, "O1")
                if count == 2:
                    if (n + 1) % NT == 0:
                        eng.wait_ge(st_in[(n + 1) // NT], 16 * 12 * (u + 2))
                    scores(NMS * (u + 1) + n + 1, n + 1, 1 - g)
                n += count

        def task(b, last, g, t):
            u = 2 * b + g
            todo = tasks_of(last, g)
            at = todo.index(t)
            prev = todo[at - 1] if at else "O1"
            if prev[0] == "O":
                eng.wait_ge(task_free, 2 * u + (2 if at else 1))
            elif prev == "V":
                eng.wait_ge(v_ready, u + 2)
            elif prev == "X0":
                eng.wait_ge(xT_ready, 2 * (b + 1) + 1)
            elif prev == "X1":
                eng.wait_ge(xT_ready, 2 * (b + 1) + 2)
            elif prev == "Q":
                eng.wait_ge(lo_ready, 2 * (u + 2) + 1)
            elif prev == "K":
                eng.wait_ge(kmean_ready, u + 3)
            elif prev == "mean":
                eng.wait_ge(mean_ready, u + 3)
            elif prev == "mx":
                eng.wait_ge(m_ready, u + 2)
            if t == "V":
                v_task(1 - g)
            elif t[0] == "X":
                if t == "X0":
                    eng.wait_ge(xn_ready, b + 2)
                x_task(int(t[1]))
            elif t in "QK":
                eng.wait_ge(xT_split, 2 * (b + 2))
                qk_task("QK".index(t), g)
            elif t == "mean":
                eng.wait_ge(kmean_ready, u + 3)
                mean_task()
            elif t == "mx":
                eng.wait_ge(max_done, NMS * (u + 2))
                mx_task()
            else:
                gr = int(t[1])
                eng.wait_ge(oT_ready, 2 * u + gr + 2)
                o_task(gr)

        eng.wait_ge(m_ready, 1)
        with eng.Fori(0, B - 1) as b:
            step(b, 0, False)
            step(b, 1, False)
        step(B - 1, 0, True)
        step(B - 1, 1, True)
        eng.wait_ge(sel_ready, 1)
        for t in range(NT):
            last = t_.transpose(bank[0][:, t * P:(t + 1) * P], sel[:, t * P:(t + 1) * P], ident[:, :])
        last.then_inc(selT_done, 1)

    return locals()


def project(nc, dram, sb, ps, sem, const, A):
    xi = [A["x_in"], sb("x_in2", [P, NT, D], F32)]
    om = [A["xn"], sb("xn2", [P, NT, D], F32)]
    hi = [A["xT_hi"], sb("xT_hi2", [P, NC, L], F32R)]
    lo = [A["xT_lo"], sb("xT_lo2", [P, NC, L], F32R)]
    oa, selT, bo_all, w_o, ident = A["oa"], A["selT"], A["bo_all"], A["w_o"], const["ident"]
    x_in, x_biased = sem("p_x_in"), sem("p_x_biased")
    masked, tr_done, hi_ready, lo_ready = sem("p_masked"), sem("p_tr_done"), sem("p_hi"), sem("p_lo")
    prod_done, x1_ready, x1_out = sem("p_prod"), sem("p_x1_ready"), sem("p_x1_out")

    def sp(eng):
        with eng.Fori(0, B // 2) as i:
            eng.wait_ge(x1_out, 32 * (i + 1))
            for p in range(2):
                eng.dma_start(xi[p][:, :, :], dram["x_tiles"][:, bass.ts(2 * i + p, NT), :]).then_inc(x_in, 16)
            for p in range(2):
                eng.wait_ge(x1_ready, 2 * i + p + 1)
                eng.dma_start(dram["x1_tiles"][:, bass.ts(2 * i + p, NT), :], xi[p][:, :, :]).then_inc(x1_out, 16)
        eng.wait_ge(x1_out, 32 + 16 * B)

    def pool(eng):
        with eng.Fori(0, B // 2) as i:
            for p in range(2):
                eng.wait_ge(x_in, 32 * (i + 1))
                nc.gpsimd.tensor_tensor(xi[p][:, :, :], xi[p][:, :, :],
                                        bo_all[:, :].unsqueeze(1).to_broadcast([P, NT, D]),
                                        ALU.add).then_inc(x_biased, 1)

    def dve(eng):
        v = nc.vector
        v.memset(const["tiny"][:, 0:1], 0.0).then_inc(x1_out, 32)
        with eng.Fori(0, B // 2) as i:
            for p in range(2):
                b = 2 * i + p
                v.tensor_tensor(om[p][:, :, :].rearrange("p t (h d) -> p t h d", h=H),
                                oa[:, bass.ts(b, NT), :].rearrange("p t (h d) -> p t h d", h=H),
                                selT[:, :, bass.ts(b, H)].unsqueeze(3).to_broadcast([P, NT, H, DH]),
                                ALU.mult).then_inc(masked, 1)
            for p in range(2):
                b = 2 * i + p
                for c in range(NC):
                    eng.wait_ge(hi_ready, NC * b + c + 1)
                    v.tensor_tensor(lo[p][:, c, :], ps[:, 2 * p + c, :], hi[p][:, c, :].bitcast(F32),
                                    ALU.subtract).then_inc(lo_ready, 1)
            for p in range(2):
                b = 2 * i + p
                eng.wait_ge(x_biased, b + 1)
                eng.wait_ge(prod_done, b + 1)
                for k in range(2):
                    rows = xi[p][:, 2 * k:2 * k + 2, :]
                    last = v.tensor_tensor(rows, ps[:, 4 + 2 * p + k, :].rearrange("p (t c) -> p t c", t=2),
                                           rows, ALU.add)
                last.then_inc(x1_ready, 1)

    def act(eng):
        with eng.Fori(0, B // 2) as i:
            for p in range(2):
                for c in range(NC):
                    eng.wait_ge(tr_done, NC * (2 * i + p) + c + 1)
                    nc.scalar.activation(hi[p][:, c, :], ps[:, 2 * p + c, :], ACT.Copy).then_inc(hi_ready, 1)

    def pe(eng):
        t_ = nc.tensor
        eng.wait_ge(A["selT_ready"], 1)
        with eng.Fori(0, B // 2) as i:
            for p in range(2):
                eng.wait_ge(masked, 2 * i + p + 1)
                for c in range(NC):
                    for t in range(NT):
                        last = t_.transpose(ps[:, 2 * p + c, t * P:(t + 1) * P],
                                            om[p][:, t, c * P:(c + 1) * P], ident[:, :])
                    last.then_inc(tr_done, 1)
            for p in range(2):
                eng.wait_ge(lo_ready, NC * (2 * i + p + 1))
                for t in range(NT):
                    n = 0
                    for c in range(NC):
                        for a, w in PASSES:
                            last = t_.matmul(ps[:, 4 + 2 * p + t // 2, (t % 2) * D:(t % 2 + 1) * D],
                                             (hi, lo)[a][p][:, c, t * P:(t + 1) * P], w_o[w][:, c, :],
                                             start=n == 0, stop=n == NC * len(PASSES) - 1)
                            n += 1
                last.then_inc(prod_done, 1)

    return locals()


PB = L // 8
NBLK = L // PB
T8 = B
NE, TOPK = 16, 4
HID = 1024
NM = HID // P
OFF = 2.0 ** 100
UNDER = -103.0
RMS_EPS = 1e-6
GATE_TEMP = 16.0
NOUT = 9


def steps(name, n):
    return [f"{name}{k}" for k in range(n)]


STREAM0 = ["f0.ln", "f0.T", "f0.rt", "f0.lg", "f0.mk", *steps("f0.m", 8), "f0.end", "z.ln", "z.rms", "z.T",
           *steps("z.o", NOUT), *steps("rec", T8), "og", "o.mean", "o.ln", "o.T", "o.wo", "o.rms", "o.x"]
STREAM1 = ["g.T", *steps("g.m", 8), "g.end", "f1.ln", "f1.T", "f1.rt", "f1.lg", "f1.mk", *steps("f1.m", 8), "f1.end"]
MERGED = ["g.T", "g.m0", "f0.ln", "g.m1", "f0.T", "g.m2", "f0.rt", "f0.lg", "g.m3", "f0.mk", *steps("f0.m", 7),
          "g.m4", "f0.m7", "f0.end", "z.ln", "g.m5", "z.rms", "g.m6", "g.m7", "g.end", "z.T", "f1.ln",
          "z.o0", "z.o1", "z.o2", "z.o3", "f1.T", "z.o4", "z.o5", "f1.rt", "z.o6", "f1.lg", "z.o7", "z.o8", "f1.mk",
          "rec0", "rec1", "f1.m0", "rec2", "f1.m1", "rec3", "rec4", "f1.m2", "rec5", "rec6", "rec7", "f1.m3",
          "f1.m4", "og", "o.mean", "o.ln", "f1.m5", "f1.m6", "o.T", "o.wo", "o.rms", "f1.m7", "f1.end", "o.x"]
assert [n for n in MERGED if n in STREAM0] == STREAM0 and [n for n in MERGED if n not in STREAM0] == STREAM1


def block_part(nc, dram, sb, ps, sem, const):
    ident, minus_half, plus_half = const["ident"], const["minus_half"], const["plus_half"]
    def two(name, shape):
        return [sb(f"{name}{i}", shape, F32R) for i in range(2)]

    w1, w2 = two("w1", [P, NC, HID]), two("w2", [P, NM, D])
    w_gate, w_up, w_down = two("w_gate", [P, NC, HID]), two("w_up", [P, NC, HID]), two("w_down", [P, NM, D])
    w_q, w_k, w_v, w_og, w_o = (two(n, [P, NC, D]) for n in ("wq_b", "wk_b", "wv_b", "wog_b", "wo_b"))
    w_r, w_g1, w_g2 = two("w_r", [P, NC, P]), two("w_g1", [P, NC, P]), two("w_g2", [P, D])
    b1, bg2, s1, s2 = sb("b1", [P, NM], F32), sb("bg2", [P, NC], F32), sb("s1", [P, NC], F32), sb("s2", [P, NC], F32)
    rb, bg1 = sb("rb", [NE, 1], F32), sb("bg1", [NE, 1], F32)
    b2_all, bog_all = sb("b2_all", [P, D], F32), sb("bog_all", [P, D], F32)
    expand = sb("expand", [P, HID], BF16)
    head_sum = sb("head_sum", [P, P], F32)
    x = [sb(f"x{s}", [P, NT, D], F32) for s in range(2)]
    tok = [sb(f"tok{s}", [P, NT, D], F32) for s in range(2)]
    xT = [two(f"xT_b{s}", [P, NC, L]) for s in range(2)]
    hf = [[sb(f"hf{s}{k}", [P, L], F32) for k in range(2)] for s in range(2)]
    h = [[[sb(f"h{s}{k}{a}", [P, L], F32R) for a in range(2)] for k in range(2)] for s in range(2)]
    maskT = [sb(f"maskT{s}", [P, L], BF16) for s in range(2)]
    logT = [hf[s][1][0:NE, :] for s in range(2)]
    lg = [sb(f"lg{s}", [P, NT, TOPK + NE], F32) for s in range(2)]
    lg_out = [sb(f"lg_out{s}", [P, NT, TOPK + NE], F32) for s in range(2)]
    top8 = [sb(f"top8_b{s}", [P, NT, 8], F32) for s in range(2)]
    lmax = [sb(f"lmax{s}", [P, NT], F32) for s in range(2)]
    mask = [sb(f"mask{s}", [P, NT, NE], F32) for s in range(2)]
    stat = [sb(f"stat_b{s}", [P, NT, 6], F32) for s in range(2)]
    mv = [sb(f"mv_b{s}", [P, NT, 2], F32) for s in range(2)]
    ve = [sb(f"ve_b{s}", [P, NT], F32) for s in range(2)]
    rstd = [sb(f"rstd_b{s}", [P, NT], F32) for s in range(2)]
    y = sb("y", [P, NT, D], F32)
    oT = sb("oT_b", [P, NC, L], F32)
    sq_rows = oT[:, :, :].rearrange("p a (b c) -> p (a b) c", c=D)
    gT = two("gT", [P, L])
    mu, var, rs = (sb(n, [P, NT * H], F32) for n in ("mu", "var", "rs"))
    rinv = sb("rinv", [P, NT], F32)
    qT, kT, vT, aT = (sb(n, [P, NC, L], F32) for n in ("qT", "kT", "vT", "aT"))
    og = kT[:, :, :].rearrange("p a (b c) -> p (a b) c", c=D)
    pr = [sb(f"pr{c}", [P, L], F32) for c in range(NC)]
    w = hf[0][1]
    stage = [t[:, :, :].rearrange("p a b -> p (a b)") for t in (qT, vT)]

    def site(name, *kinds):
        return {k: sem(f"{name}_{k}") for k in kinds}

    tr_kinds = ("src", "tr", "hi", "lo")
    ffn_kinds = ("dm", "var", "rstd", "biased", "rt", "lt", "lg", "mk", "mt", "mtb", "up", "relu", "hh", "hl", "dn", "out") + tr_kinds
    F = [site("ffn0", *ffn_kinds), site("ffn1", *ffn_kinds)]
    Z = site("z", "var", "rstd", "ss", "rn", "ghs", "out", "cv", "og", "ogb", "ogs", *tr_kinds)
    R = site("rec", "kd", "pr", "hs", "w")
    O = site("o", "os", "ot", "var", "rs", "wo", *tr_kinds)
    G = site("g", "dm", "pd", "xy", "ss", "rn", "gate", "silu", "up", "hh", "hl", "dn", "out", *tr_kinds)
    ACC = [0, 4]
    RING = [2, 6]
    x_in, x_out = sem("b_x_in"), sem("b_x_out")
    stage_in = [sem(f"b_stage_in{k}") for k in range(2)]
    stage_hi, stage_lo = sem("b_stage_hi"), sem("b_stage_lo")
    small_in, b_init = sem("b_small_in"), sem("b_init")
    b_cleared = sem("b_cleared")
    dve_link = sem("b_dve_link")

    pieces = []
    for name, ws in (("w1", w1), ("w_gate", w_gate), ("w_up", w_up)):
        for c in range(NC):
            pieces.append((dram[name][c * P:(c + 1) * P, :], HID, [t[:, c, :] for t in ws]))
    for name, ws in (("w2", w2), ("w_down", w_down)):
        for k in range(2):
            rows = dram[name][k * NM // 2 * P:(k + 1) * NM // 2 * P, :].rearrange("(m p) n -> p m n", p=P)
            pieces.append((rows, HID, [t[:, k * NM // 2:(k + 1) * NM // 2, :] for t in ws]))
    for name, ws in (("wq", w_q), ("wk", w_k), ("wv", w_v), ("wog", w_og), ("wo", w_o)):
        pieces.append((dram[name].rearrange("(c p) n -> p c n", p=P), NC * D, [t[:, :, :] for t in ws]))
    for name, ws in (("rw", w_r), ("wg1", w_g1)):
        pieces.append((dram[name].rearrange("(c p) n -> p c n", p=P), NC * NE, [t[:, :, 0:NE] for t in ws]))
    pieces.append((dram["wg2"], D, [t[0:NE, :] for t in w_g2]))

    def staged(n):
        src, cols, ws = pieces[n]
        rows = ws[0].shape[0]
        v = stage[n % 2][0:rows, 0:cols]
        if len(ws[0].shape) == 3:
            v = v.rearrange("p (m n) -> p m n", m=ws[0].shape[1])
        return v

    small = [(b1[:, :], "b1"), (bg2[:, :], "bg2"), (s1[:, :], "s1"), (s2[:, :], "s2"), (rb[:, :], "rb"), (bg1[:, :], "bg1")]
    NSMALL = len(small) + 2

    def sp(eng):
        def ld(out, in_, s):
            eng.dma_start(out, in_).then_inc(s, 16)

        eng.wait_ge(*const["a_done"])
        for n, (src, _, _) in enumerate(pieces):
            if n >= 2:
                eng.wait_ge(stage_lo, n - 1)
            ld(staged(n), src, stage_in[n % 2])
            if n == 1:
                for out, name in small:
                    ld(out, dram[name], small_in)
                ld(b2_all[:, :], dram["b2"].partition_broadcast(P), small_in)
                ld(bog_all[:, :], dram["bog"].partition_broadcast(P), small_in)

        def load(i):
            for e in range(2):
                ld(x[0][e * PB:(e + 1) * PB, :, :], dram["x1_blocks"][e, bass.ts(i, PB), :, :], x_in)

        def store(j):
            eng.wait_ge(F[1]["out"], j + 1)
            for e in range(2):
                ld(dram["out_blocks"][e, bass.ts(j, PB), :, :], x[1][e * PB:(e + 1) * PB, :, :], x_out)

        load(0)
        with eng.Fori(1, NBLK) as i:
            eng.wait_ge(G["xy"], i)
            load(i)
            store(i - 1)
        store(NBLK - 1)
        eng.wait_ge(x_out, 32 * NBLK)

    def pool(eng):
        g = nc.gpsimd
        eng.wait_ge(*const["a_done"])
        g.memset(expand[:, :], OFF).then_inc(b_init, 1)
        g.memset(head_sum[:, :], 1.0).then_inc(b_init, 1)
        n = 2
        hs3 = head_sum[:, :].rearrange("p (h d) -> p h d", h=HU)
        for out, base, pattern, mult in (
                (expand[:, :], 0, [[1, HID]], -HID // NE), (expand[:, :], HID // NE - 1, [[-1, HID]], HID // NE),
                (hs3, 0, [[-DH, HU], [0, DH]], 1), (hs3, DH - 1, [[DH, HU], [0, DH]], -1)):
            eng.wait_ge(b_init, n)
            g.affine_select(out=out, in_=out, compare_op=ALU.is_ge, fill=0.0, base=base, pattern=pattern,
                            channel_multiplier=mult).then_inc(b_init, 1)
            n += 1
        for n, (_, _, ws) in enumerate(pieces):
            eng.wait_ge(stage_hi, n + 1)
            g.tensor_tensor(ws[1], staged(n), ws[0].bitcast(F32), ALU.subtract).then_inc(stage_lo, 1)

        def power(src, dst, half, wait, done, i):
            eng.wait_ge(wait, i + 1)
            g.tensor_tensor(dst, src, half, ALU.pow).then_inc(done, 1)

        def std(s, S, i):
            power(ve[s][:, :], rstd[s][:, :], minus_half[:, 0:NT], S["var"], S["rstd"], i)

        def ffn_ln(i, s):
            std(s, F[s], i)
            eng.wait_ge(F[s]["src"], i + 1)
            g.tensor_tensor(x[s][:, :, :], x[s][:, :, :], b2_all[:, :].unsqueeze(1).to_broadcast([P, NT, D]),
                            ALU.add).then_inc(F[s]["biased"], 1)

        def rec(i, t):
            if t == 1:
                eng.wait_ge(Z["cv"], NOUT * (i + 1))
            for c in range(NC):
                eng.wait_ge(R["pr"], 2 * T8 * i + 2 * (t - 1) + c + 1)
                keys = kT[:, c, 0:PB * t].rearrange("p (s n) -> p s n", s=t)
                decay = aT[:, c, PB * t:PB * (t + 1)].unsqueeze(1).to_broadcast([P, t, PB])
                g.tensor_tensor(keys, keys, decay, ALU.mult).then_inc(R["kd"], 1)

        def out_rms(i):
            power(ve[0][:, :], rstd[0][:, :], plus_half[:, 0:NT], G["ss"], G["rn"], i)

        def hand_over(i):
            if not (isinstance(i, int) and i == 0):
                eng.wait_ge(x_out, 32 * i)
            g.tensor_tensor(x[1][:, :, :], x[0][:, :, :], y[:, :, :], ALU.add).then_inc(G["xy"], 1)

        def low_h(i, s, m, S, done):
            eng.wait_ge(S[done], NM * i + m + 1)
            hi, lo = h[s][m % 2]
            g.tensor_tensor(lo[:, :], hf[s][m % 2][:, :], hi[:, :].bitcast(F32), ALU.subtract).then_inc(S["hl"], 1)

        parts = {"f0.ln": lambda i: ffn_ln(i, 0), "f1.ln": lambda j: ffn_ln(j, 1), "z.ln": lambda i: std(0, Z, i),
                 "z.rms": lambda i: power(ve[0][:, :], rstd[0][:, :], plus_half[:, 0:NT], Z["ss"], Z["rn"], i),
                 "o.rms": out_rms, "o.x": hand_over}
        for t in range(T8 - 1):
            parts[f"rec{t}"] = lambda i, t=t: rec(i, t + 1)
        for m in range(NM):
            parts[f"f0.m{m}"] = lambda i, m=m: low_h(i, 0, m, F[0], "relu")
            parts[f"f1.m{m}"] = lambda j, m=m: low_h(j, 1, m, F[1], "relu")
            parts[f"g.m{m}"] = lambda j, m=m: low_h(j, 1, m, G, "hh")
        run(eng, parts)

    def run(eng, parts, link=None, per=0):
        for name in STREAM0:
            if name in parts:
                parts[name](0)
        with eng.Fori(1, NBLK) as i:
            if link:
                link.enter(i - 1, per)
            for name in MERGED:
                if name in parts:
                    parts[name](i if name in STREAM0 else i - 1)
            if link:
                link.leave(NBLK - 1)
        for name in STREAM1:
            if name in parts:
                parts[name](NBLK - 1)

    def dve(eng):
        v = nc.vector
        link = Link(eng, dve_link, const)
        eng.wait_ge(*const["a_done"])
        for t in (*w_r, *w_g1):
            v.memset(t[:, :, :].bitcast(F32), 0.0)
        for t in (*w_g2, *gT):
            v.memset(t[:, :].bitcast(F32), 0.0)
        for s in range(2):
            v.memset(maskT[s][:, :], 0.0)
            last = v.memset(lg[s][:, :, 0:TOPK], BIG)
        last.then_inc(b_cleared, 1)
        eng.wait_ge(small_in, 16 * NSMALL)
        link(v.tensor_scalar(bg2[:, :], bg2[:, :], 1.0 / GATE_TEMP, None, ALU.mult))

        def layer_norm(i, s, out, S):
            for t in range(NT):
                last = v.bn_stats(stat[s][:, t, :], x[s][:, t, :])
            link(last, alone=True)
            for t in range(NT):
                last = v.bn_aggr(mv[s][:, t, :], stat[s][:, t, :])
            link(last)
            v.tensor_scalar(ve[s][:, :], mv[s][:, :, 1], LN_EPS, None, ALU.add).then_inc(S["var"], 1)
            eng.wait_ge(S["rstd"], i + 1)
            for t in range(NT):
                last = v.tensor_scalar(out[:, t, :], x[s][:, t, :], mv[s][:, t, 0:1], rstd[s][:, t:t + 1],
                                       ALU.subtract, ALU.mult)
            return last

        def rms_norm(i, squares, out, S):
            link(v.tensor_tensor(squares, y[:, :, :], y[:, :, :], ALU.mult))
            v.tensor_reduce(ve[0][:, :], squares, AX_X, ALU.add).then_inc(S["ss"], 1)
            eng.wait_ge(S["rn"], i + 1)
            link(v.tensor_scalar(ve[0][:, :], rstd[0][:, :], float(D) ** -0.5, RMS_EPS, ALU.mult, ALU.add))
            link(v.reciprocal(rinv[:, :], ve[0][:, :]))
            for t in range(NT):
                last = v.tensor_scalar(out[:, t, :], y[:, t, :], rinv[:, t:t + 1], None, ALU.mult)
            last.then_inc(S["src"], 1)

        def low(i, s, S, scale=None):
            for c in range(NC):
                eng.wait_ge(S["hi"], NC * i + c + 1)
                v.scalar_tensor_tensor(xT[s][1][:, c, :], ps[:, RING[s] + c, :],
                                       1.0 if scale is None else scale[:, c:c + 1],
                                       xT[s][0][:, c, :].bitcast(F32), ALU.mult, ALU.subtract).then_inc(S["lo"], 1)

        def add_down(i, s, S):
            eng.wait_ge(S["dm"], NM * (i + 1))
            for k in range(2):
                rows = x[s][:, 2 * k:2 * k + 2, :]
                last = v.tensor_tensor(rows, ps[:, ACC[s] + k, :].rearrange("p (t c) -> p t c", t=2), rows, ALU.add)
            return last

        def ffn_ln(i, s):
            if s == 0:
                eng.wait_ge(x_in, 32 * (i + 1))
            layer_norm(i, s, tok[s], F[s]).then_inc(F[s]["src"], 1)

        def choose(i, s):
            S = F[s]
            eng.wait_ge(S["lg"], i + 1)
            logits = ps[:, RING[s] + 1, 0:NT * NE].rearrange("p (t e) -> p t e", t=NT)
            link(v.tensor_reduce(lmax[s][:, :], logits, AX_X, ALU.max))
            link(v.tensor_tensor(lg[s][:, :, TOPK:], logits, lmax[s][:, :].unsqueeze(2).to_broadcast([P, NT, NE]),
                                 ALU.subtract))
            link(v.tensor_scalar(lg[s][:, :, TOPK:], lg[s][:, :, TOPK:], UNDER, None, ALU.max), alone=True)
            for t in range(NT):
                last = v.max(top8[s][:, t, :], lg[s][:, t, :])
            link(last, alone=True)
            for t in range(NT):
                last = v.match_replace(lg_out[s][:, t, :], top8[s][:, t, :], lg[s][:, t, :], GONE)
            link(last)
            v.tensor_scalar(mask[s][:, :, :], lg_out[s][:, :, TOPK:], GONE, 1.0, ALU.is_equal,
                            ALU.subtract).then_inc(S["mk"], 1)

        def f0_end(i):
            eng.wait_ge(F[0]["biased"], i + 1)
            link(add_down(i, 0, F[0]))

        def g_end(j):
            eng.wait_ge(G["xy"], j + 1)
            link(add_down(j, 1, G))

        def f1_end(j):
            eng.wait_ge(F[1]["biased"], j + 1)
            add_down(j, 1, F[1]).then_inc(F[1]["out"], 1)

        def gate_in(i):
            eng.wait_ge(Z["cv"], NOUT * i + 1)
            g_in = hf[0][0][0:NE, :]
            link(v.tensor_copy(gT[0][0:NE, :], g_in))
            v.tensor_tensor(gT[1][0:NE, :], g_in, gT[0][0:NE, :].bitcast(F32), ALU.subtract).then_inc(Z["ghs"], 1)

        def product(i, s):
            t, c = divmod(s, NC)
            if t:
                eng.wait_ge(R["kd"], 2 * (T8 - 1) * i + s - 1)
            if s >= 2:
                eng.wait_ge(R["hs"], 2 * T8 * i + s - 1)
            v.tensor_tensor(pr[c][:, 0:PB * (t + 1)].rearrange("p (s n) -> p s n", n=PB),
                            kT[:, c, 0:PB * (t + 1)].rearrange("p (s n) -> p s n", n=PB),
                            qT[:, c, PB * t:PB * (t + 1)].unsqueeze(1).to_broadcast([P, t + 1, PB]),
                            ALU.mult).then_inc(R["pr"], 1)

        def rec(i, t):
            if t == 0:
                eng.wait_ge(Z["cv"], NOUT * (i + 1))
                product(i, 0)
            for s in (2 * t, 2 * t + 1):
                if s + 1 < 2 * T8:
                    product(i, s + 1)
                c = s % NC
                eng.wait_ge(R["hs"], 2 * T8 * i + s + 1)
                bank = ps[:, RING[0] + c, 0:PB * (t + 1)]
                out = oT[:, c, PB * t:PB * (t + 1)]
                if t == 0:
                    v.tensor_tensor(out, bank, vT[:, c, 0:PB], ALU.mult).then_inc(R["w"], 1)
                    continue
                v.tensor_tensor(w[:, 0:PB * (t + 1)], bank, vT[:, c, 0:PB * (t + 1)], ALU.mult).then_inc(R["w"], 1)
                eng.wait_ge(R["w"], 2 * T8 * i + s + 1)
                last = v.tensor_reduce(out, w[:, 0:PB * (t + 1)].rearrange("p (s n) -> p n s", n=PB), AX_X, ALU.add)
                if s < 2 * T8 - 1:
                    link(last)
                else:
                    last.then_inc(O["os"], 1)

        def og_out(i):
            eng.wait_ge(O["os"], i + 1)
            for k in range(2):
                eng.wait_ge(Z["og"], 2 * i + k + 1)
                last = v.tensor_tensor(og[:, 2 * k:2 * k + 2, :],
                                       ps[:, ACC[0] + k, :].rearrange("p (t c) -> p t c", t=2),
                                       bog_all[:, :].unsqueeze(1).to_broadcast([P, 2, D]), ALU.add)
            last.then_inc(Z["ogb"], 1)

        tokh = tok[0][:, :, :].rearrange("p t (h d) -> p (t h) d", d=DH)

        def o_mean(i):
            for k in range(2):
                eng.wait_ge(O["ot"], 2 * i + k + 1)
                last = v.tensor_reduce(mu[:, 2 * k * H:2 * (k + 1) * H],
                                       ps[:, ACC[0] + k, :].rearrange("p (g d) -> p g d", d=DH), AX_X, ALU.add)
            link(last)
            link(v.tensor_scalar(mu[:, :], mu[:, :], 1.0 / DH, None, ALU.mult))
            for k in range(2):
                part = slice(2 * k * H, 2 * (k + 1) * H)
                last = v.tensor_tensor(tokh[:, part, :], ps[:, ACC[0] + k, :].rearrange("p (g d) -> p g d", d=DH),
                                       mu[:, part].unsqueeze(2).to_broadcast([P, 2 * H, DH]), ALU.subtract)
            link(last)

        def o_ln(i):
            sqh = sq_rows.rearrange("p t (h d) -> p (t h) d", d=DH)
            link(v.tensor_tensor(sqh, tokh, tokh, ALU.mult))
            link(v.tensor_reduce(var[:, :], sqh, AX_X, ALU.add))
            v.tensor_scalar(var[:, :], var[:, :], 1.0 / DH, LN_EPS, ALU.mult, ALU.add).then_inc(O["var"], 1)
            eng.wait_ge(Z["ogs"], i + 1)
            link(v.tensor_tensor(tok[0][:, :, :], tok[0][:, :, :], og, ALU.mult))
            eng.wait_ge(O["rs"], i + 1)
            link(v.reciprocal(rs[:, :], rs[:, :]))
            link(v.scalar_tensor_tensor(mu[:, :], var[:, :], -0.5, rs[:, :], ALU.mult, ALU.mult))
            link(v.tensor_tensor(mu[:, :], mu[:, :], rs[:, :], ALU.mult))
            link(v.scalar_tensor_tensor(rs[:, :], mu[:, :], 1.5, rs[:, :], ALU.add, ALU.mult))
            v.tensor_tensor(tokh, tokh, rs[:, :].unsqueeze(2).to_broadcast([P, NT * H, DH]),
                            ALU.mult).then_inc(O["src"], 1)

        def o_add(i):
            for k in range(2):
                eng.wait_ge(O["wo"], 2 * i + k + 1)
                rows = y[:, 2 * k:2 * k + 2, :]
                last = v.tensor_tensor(rows, ps[:, ACC[0] + k, :].rearrange("p (t c) -> p t c", t=2), rows, ALU.add)
            link(last)

        def o_rms(i):
            if not (isinstance(i, int) and i == 0):
                eng.wait_ge(F[1]["tr"], NC * i)
            rms_norm(i, sq_rows, tok[1], G)

        def gated(j, m):
            eng.wait_ge(G["silu"], NM * j + m + 1)
            eng.wait_ge(G["up"], NM * j + m + 1)
            buf = hf[1][m % 2][:, :]
            v.tensor_tensor(buf, ps[:, RING[1] + 1, :], buf, ALU.mult).then_inc(G["pd"], 1)
            if m >= 2:
                eng.wait_ge(G["dm"], NM * j + m - 1)
            eng.wait_ge(G["pd"], NM * j + m + 1)
            v.tensor_copy(h[1][m % 2][0][:, :], buf).then_inc(G["hh"], 1)

        parts = {"f0.ln": lambda i: ffn_ln(i, 0), "f0.T": lambda i: low(i, 0, F[0]), "f0.lg": lambda i: choose(i, 0),
                 "f0.end": f0_end, "z.ln": lambda i: link(layer_norm(i, 0, y, Z)),
                 "z.rms": lambda i: rms_norm(i, tok[0][:, :, :], tok[0], Z), "z.T": lambda i: low(i, 0, Z, s1),
                 "z.o0": gate_in, "og": og_out, "o.mean": o_mean, "o.ln": o_ln, "o.T": lambda i: low(i, 0, O),
                 "o.wo": o_add, "o.rms": o_rms, "g.T": lambda j: low(j, 1, G, s2),
                 "g.end": g_end, "f1.ln": lambda j: ffn_ln(j, 1),
                 "f1.T": lambda j: low(j, 1, F[1]), "f1.lg": lambda j: choose(j, 1), "f1.end": f1_end}
        for t in range(T8):
            parts[f"rec{t}"] = lambda i, t=t: rec(i, t)
        for m in range(NM):
            parts[f"g.m{m}"] = lambda j, m=m: gated(j, m)
        eng.wait_ge(b_init, 6)
        eng.wait_ge(b_cleared, 1)
        run(eng, parts, link, DVE_LINKS_B)

    def act(eng):
        a = nc.scalar
        eng.wait_ge(*const["a_done"])
        eng.wait_ge(b_cleared, 1)
        for n, (_, _, ws) in enumerate(pieces):
            eng.wait_ge(stage_in[n % 2], 16 * (n // 2 + 1))
            a.activation(ws[0], staged(n), ACT.Copy).then_inc(stage_hi, 1)

        def high(i, s, S, scale=None):
            for c in range(NC):
                eng.wait_ge(S["tr"], NC * i + c + 1)
                out, src = xT[s][0][:, c, :], ps[:, RING[s] + c, :]
                if scale is None:
                    a.activation(out, src, ACT.Copy).then_inc(S["hi"], 1)
                else:
                    a.activation(out, src, ACT.Identity, scale=scale[:, c:c + 1]).then_inc(S["hi"], 1)

        def logits(i, s):
            eng.wait_ge(F[s]["rt"], i + 1)
            a.activation(logT[s], ps[0:NE, RING[s], :], ACT.Identity, bias=rb[:, :]).then_inc(F[s]["lt"], 1)

        def mask_out(i, s):
            eng.wait_ge(F[s]["mt"], i + 1)
            a.activation(maskT[s][0:NE, :], ps[0:NE, RING[s], :], ACT.Copy).then_inc(F[s]["mtb"], 1)

        def relu(i, s, m):
            eng.wait_ge(F[s]["up"], NM * i + m + 1)
            if m >= 2:
                eng.wait_ge(F[s]["hl"], NM * i + m - 1)
            src, bias = ps[:, RING[s] + m % 2, :], b1[:, m:m + 1]
            a.activation(hf[s][m % 2][:, :], src, ACT.Relu, bias=bias)
            if m >= 2:
                eng.wait_ge(F[s]["dm"], NM * i + m - 1)
            a.activation(h[s][m % 2][0][:, :], src, ACT.Relu, bias=bias).then_inc(F[s]["relu"], 1)

        def projection(i, n):
            eng.wait_ge(Z["out"], NOUT * i + n + 1)
            src = ps[:, RING[0] + n % 2, :]
            if n == 0:
                ins = a.activation(hf[0][0][0:NE, :], src[0:NE, :], ACT.Silu, bias=bg1[:, :])
            elif n < 7:
                c, k = divmod(n - 1, 3)
                ins = a.activation((kT, qT, vT)[k][:, c, :], src, ACT.Copy)
            else:
                ins = a.activation(aT[:, n - 7, :], src, ACT.Sigmoid, bias=bg2[:, n - 7:n - 6], scale=1.0 / GATE_TEMP)
            ins.then_inc(Z["cv"], 1)

        def og_silu(i):
            eng.wait_ge(Z["ogb"], i + 1)
            a.activation(og, og, ACT.Silu).then_inc(Z["ogs"], 1)

        def silu(j, m):
            eng.wait_ge(G["gate"], NM * j + m + 1)
            if m >= 2:
                eng.wait_ge(G["hl"], NM * j + m - 1)
            a.activation(hf[1][m % 2][:, :], ps[:, RING[1], :], ACT.Silu).then_inc(G["silu"], 1)

        def deviation(i):
            eng.wait_ge(O["var"], i + 1)
            a.activation(rs[:, :], var[:, :], ACT.Sqrt).then_inc(O["rs"], 1)

        parts = {"z.T": lambda i: high(i, 0, Z, s1), "og": og_silu, "o.ln": deviation, "o.T": lambda i: high(i, 0, O),
                 "g.T": lambda j: high(j, 1, G, s2)}
        for s in range(2):
            parts[f"f{s}.T"] = lambda i, s=s: high(i, s, F[s])
            parts[f"f{s}.rt"] = lambda i, s=s: logits(i, s)
            parts[f"f{s}.mk"] = lambda i, s=s: mask_out(i, s)
            for m in range(NM):
                parts[f"f{s}.m{m}"] = lambda i, s=s, m=m: relu(i, s, m)
        for n in range(NOUT):
            parts[f"z.o{n}"] = lambda i, n=n: projection(i, n)
        for m in range(NM):
            parts[f"g.m{m}"] = lambda j, m=m: silu(j, m)
        eng.wait_ge(b_init, 6)
        eng.wait_ge(small_in, 16 * NSMALL)
        run(eng, parts)

    def pe(eng):
        t_ = nc.tensor

        def transposed(i, s, S):
            eng.wait_ge(S["src"], i + 1)
            for c in range(NC):
                for t in range(NT):
                    last = t_.transpose(ps[:, RING[s] + c, t * P:(t + 1) * P], tok[s][:, t, c * P:(c + 1) * P],
                                        ident[:, :])
                last.then_inc(S["tr"], 1)

        def channels(bank, ws, m, s, close=True):
            n = 0
            for c in range(NC):
                for a, k in PASSES:
                    last = t_.matmul(ps[:, bank, :], ws[a][:, c, m * P:(m + 1) * P], xT[s][k][:, c, :],
                                     start=n == 0, stop=close and n == NC * len(PASSES) - 1)
                    n += 1
            return last

        def rows(ws, done):
            for t in range(NT):
                n = 0
                for c in range(NC):
                    for a, k in PASSES:
                        last = t_.matmul(ps[:, ACC[0] + t // 2, (t % 2) * D:(t % 2 + 1) * D],
                                         xT[0][a][:, c, t * P:(t + 1) * P], ws[k][:, c, :],
                                         start=n == 0, stop=n == NC * len(PASSES) - 1)
                        n += 1
                if t % 2:
                    last.then_inc(done, 1)

        def down(i, s, m, ws, S):
            eng.wait_ge(S["hl"], NM * i + m + 1)
            for t in range(NT):
                for n, (a, k) in enumerate(PASSES):
                    last = t_.matmul(ps[:, ACC[s] + t // 2, (t % 2) * D:(t % 2 + 1) * D],
                                     h[s][m % 2][a][:, t * P:(t + 1) * P], ws[k][:, m, :],
                                     start=m == 0 and n == 0 and t % 2 == 0,
                                     stop=m == NM - 1 and n == len(PASSES) - 1, skip_group_check=True)
            last.then_inc(S["dm"], 1)

        def router(i, s):
            eng.wait_ge(F[s]["lo"], NC * (i + 1))
            channels(RING[s], w_r, 0, s).then_inc(F[s]["rt"], 1)

        def logits(i, s):
            constant_wait(eng, const)
            eng.wait_ge(F[s]["lt"], i + 1)
            for t in range(NT):
                last = t_.transpose(ps[:, RING[s] + 1, t * NE:(t + 1) * NE], logT[s][:, t * P:(t + 1) * P],
                                    ident[0:NE, 0:NE])
            last.then_inc(F[s]["lg"], 1)

        def masks(i, s):
            eng.wait_ge(F[s]["mk"], i + 1)
            for t in range(NT):
                last = t_.transpose(ps[0:NE, RING[s], t * P:(t + 1) * P], mask[s][:, t, :], ident[:, :])
            last.then_inc(F[s]["mt"], 1)

        def ffn(i, s, m):
            if m == 0:
                eng.wait_ge(F[s]["mtb"], i + 1)
            if m >= 2:
                eng.wait_ge(F[s]["relu"], NM * i + m - 1)
            bank = RING[s] + m % 2
            channels(bank, w1, m, s, close=False)
            t_.matmul(ps[:, bank, :], expand[:, m * P:(m + 1) * P], maskT[s][:, :],
                      start=False, stop=True).then_inc(F[s]["up"], 1)
            if m:
                down(i, s, m - 1, w2, F[s])

        outs = [(w_g1, 0)] + [(ws, c) for c in range(NC) for ws in (w_k, w_q, w_v)]

        def projection(i, n):
            if n == 0:
                eng.wait_ge(Z["lo"], NC * (i + 1))
            else:
                if n >= 2:
                    eng.wait_ge(Z["cv"], NOUT * i + n - 1)
            bank = RING[0] + n % 2
            if n < len(outs):
                channels(bank, *outs[n], 0).then_inc(Z["out"], 1)
                return
            eng.wait_ge(Z["ghs"], i + 1)
            c = n - len(outs)
            for k, (a, b) in enumerate(PASSES):
                last = t_.matmul(ps[:, bank, :], w_g2[a][:, c * P:(c + 1) * P], gT[b][:, :],
                                 start=k == 0, stop=k == len(PASSES) - 1)
            last.then_inc(Z["out"], 1)

        def rec(i, t):
            for s in (2 * t, 2 * t + 1):
                c = s % NC
                eng.wait_ge(R["pr"], 2 * T8 * i + s + 1)
                if s >= 2:
                    eng.wait_ge(R["w"], 2 * T8 * i + s - 1)
                t_.matmul(ps[:, RING[0] + c, 0:PB * (t + 1)], head_sum[:, :], pr[c][:, 0:PB * (t + 1)],
                          start=True, stop=True).then_inc(R["hs"], 1)
            if t == T8 - 2:
                rows(w_og, Z["og"])

        def o_back(i):
            eng.wait_ge(O["os"], i + 1)
            eng.wait_ge(Z["ogb"], i + 1)
            for t in range(NT):
                for c in range(NC):
                    at = (t % 2) * D + c * P
                    last = t_.transpose(ps[:, ACC[0] + t // 2, at:at + P], oT[:, c, t * P:(t + 1) * P], ident[:, :])
                if t % 2:
                    last.then_inc(O["ot"], 1)

        def o_wo(i):
            eng.wait_ge(O["lo"], NC * (i + 1))
            rows(w_o, O["wo"])

        def gated(j, m):
            if m == 0:
                eng.wait_ge(G["lo"], NC * (j + 1))
            else:
                eng.wait_ge(G["silu"], NM * j + m)
            channels(RING[1], w_gate, m, 1).then_inc(G["gate"], 1)
            if m:
                eng.wait_ge(G["pd"], NM * j + m)
            channels(RING[1] + 1, w_up, m, 1).then_inc(G["up"], 1)
            if m:
                down(j, 1, m - 1, w_down, G)

        parts = {"z.T": lambda i: transposed(i, 0, Z), "o.mean": o_back, "o.T": lambda i: transposed(i, 0, O),
                 "o.wo": o_wo, "g.T": lambda j: transposed(j, 1, G), "g.end": lambda j: down(j, 1, NM - 1, w_down, G)}
        for s in range(2):
            parts[f"f{s}.T"] = lambda i, s=s: transposed(i, s, F[s])
            parts[f"f{s}.rt"] = lambda i, s=s: router(i, s)
            parts[f"f{s}.lg"] = lambda i, s=s: logits(i, s)
            parts[f"f{s}.mk"] = lambda i, s=s: masks(i, s)
            parts[f"f{s}.end"] = lambda i, s=s: down(i, s, NM - 1, w2, F[s])
            for m in range(NM):
                parts[f"f{s}.m{m}"] = lambda i, s=s, m=m: ffn(i, s, m)
        for n in range(NOUT):
            parts[f"z.o{n}"] = lambda i, n=n: projection(i, n)
        for t in range(T8):
            parts[f"rec{t}"] = lambda i, t=t: rec(i, t)
        for m in range(NM):
            parts[f"g.m{m}"] = lambda j, m=m: gated(j, m)
        eng.wait_ge(b_init, 6)
        eng.wait_ge(b_cleared, 1)
        eng.wait_ge(stage_lo, len(pieces))
        run(eng, parts)

    return locals()


def build(nc, dram):
    ctx = ExitStack()
    with ctx:
        sb = lambda name, shape, dt: ctx.enter_context(nc.sbuf_tensor(name, shape, dt))
        sem = lambda name: ctx.enter_context(nc.semaphore(name))
        ps = ctx.enter_context(nc.psum_tensor("ps", [P, 8, 512], F32))
        ident = sb("ident", [P, P], F32)
        minus_half = sb("minus_half", [P, NT * H], F32)
        plus_half = sb("plus_half", [P, NT], F32)
        const_ready = sem("const_ready")
        tiny = sb("tiny", [P, 2], F32)
        const = {"ident": ident, "minus_half": minus_half, "plus_half": plus_half, "ready": const_ready, "count": 5, "tiny": tiny}
        arena = ExitStack()
        sb_a = lambda name, shape, dt: arena.enter_context(nc.sbuf_tensor(name, shape, dt))
        with arena:
            A = attention(nc, ctx, dram, sb_a, ps, sem, const)
            A2 = project(nc, dram, sb_a, ps, sem, const, A)
        const["a_done"] = (A2["x1_out"], 32 + 16 * B)
        second = lambda name, shape, dt: ctx.enter_context(nc.sbuf_tensor(name, shape, dt))

        BB = block_part(nc, dram, second, ps, sem, const)
        block = ctx.enter_context(nc.Block())

        @block.sync
        def _(eng):
            A["sp"](eng)
            A2["sp"](eng)
            BB["sp"](eng)

        @block.gpsimd
        def _(eng):
            nc.gpsimd.memset(ident[:, :], 0.0).then_inc(const_ready, 1)
            nc.gpsimd.memset(minus_half[:, :], -0.5).then_inc(const_ready, 1)
            nc.gpsimd.memset(plus_half[:, :], 0.5).then_inc(const_ready, 1)
            nc.gpsimd.memset(tiny[:, :], 0.0).then_inc(const_ready, 1)
            eng.wait_ge(const_ready, 4)
            nc.gpsimd.affine_select(out=ident[:, :], in_=ident[:, :], compare_op=ALU.not_equal, fill=1.0,
                                    base=0, pattern=[[-1, P]], channel_multiplier=1).then_inc(const_ready, 1)
            A["pool"](eng)
            A2["pool"](eng)
            BB["pool"](eng)

        @block.vector
        def _(eng):
            eng.wait_ge(const_ready, const["count"])
            A["dve"](eng)
            eng.wait_ge(A["selT_ready"], 1)
            A2["dve"](eng)
            BB["dve"](eng)

        @block.scalar
        def _(eng):
            A["act"](eng)
            A2["act"](eng)
            BB["act"](eng)

        @block.tensor
        def _(eng):
            A["pe"](eng)
            A2["pe"](eng)
            BB["pe"](eng)



_NAMES = {"x": "L0_attn_a_x", "Wq": "L0_attn_a_Wq", "Wk": "L0_attn_a_Wk", "Wv": "L0_attn_a_Wv", "Wo": "L0_attn_a_Wo",
          "bq": "L0_attn_a_bq", "bk": "L0_attn_a_bk", "bv": "L0_attn_a_bv", "bo": "L0_attn_a_bo",
          "w1": "L0_ffn_w1", "w2": "L0_ffn_w2", "rw": "L0_ffn_router_w", "b1": "L0_ffn_b1", "b2": "L0_ffn_b2",
          "rb": "L0_ffn_router_b", "wq": "L0_attn_b_wq", "wk": "L0_attn_b_wk", "wv": "L0_attn_b_wv",
          "wog": "L0_attn_b_wog", "wo": "L0_attn_b_wo", "wg1": "L0_attn_b_wg1", "wg2": "L0_attn_b_wg2",
          "bg1": "L0_attn_b_bg1", "bg2": "L0_attn_b_bg2", "bog": "L0_attn_b_bog", "s1": "L0_attn_b_scale1",
          "s2": "L0_attn_b_scale2", "w_gate": "L0_attn_b_w_gate", "w_up": "L0_attn_b_w_up", "w_down": "L0_attn_b_w_down"}
_TRANSPOSED = ("w1", "w2", "rw", "wq", "wk", "wv", "wog", "wo", "wg1", "wg2", "w_gate", "w_up", "w_down")
_COLUMNS = ("bq", "bk", "b1", "bg2", "s1", "s2")
_ONE_COLUMN = ("rb", "bg1")


def kernel(**inputs):
    import numpy as _np
    import concourse.bacc as _bacc
    from concourse import mybir as _mybir
    from concourse.bass_utils import run_bass_kernel_spmd as _run

    nc = _bacc.Bacc("TRN2", target_bir_lowering=False, num_devices=1)
    arrays, dram = {}, {}
    for key, name in _NAMES.items():
        a = _np.asarray(inputs[name])
        if key in _TRANSPOSED:
            a = a.T
        elif key in _COLUMNS:
            a = a.reshape(-1, P).T
        elif key in _ONE_COLUMN:
            a = a.reshape(-1, 1)
        a = _np.ascontiguousarray(a)
        arrays[f"in_{key}_dram"] = a
        dram[key] = nc.dram_tensor(f"in_{key}_dram", a.shape, _mybir.dt.from_np(a.dtype), kind="ExternalInput").ap()
    out = nc.dram_tensor("out_dram", (B, L, D), F32, kind="ExternalOutput").ap()
    x1 = nc.dram_tensor("x1_dram", (B, L, D), F32).ap()
    dram["spars"] = nc.dram_tensor("spars_dram", (B * H, L), F32).ap()
    dram["x_tiles"] = dram["x"].rearrange("b (t p) c -> p (b t) c", p=P)
    dram["x1_tiles"] = x1.rearrange("b (t p) c -> p (b t) c", p=P)
    dram["x1_blocks"] = x1.rearrange("(t e) l c -> e l t c", e=2)
    dram["out_blocks"] = out.rearrange("(t e) l c -> e l t c", e=2)
    build(nc, dram)
    r = _run(nc, [arrays], core_ids=[0])
    return r.results[0]["out_dram"]
```

```python
from contextlib import ExitStack

import concourse.bass as bass
from concourse import mybir

ALU = mybir.AluOpType
ACT = mybir.ActivationFunctionType
AX_X = mybir.AxisListType.X
F32 = mybir.dt.float32
F32R = mybir.dt.float32r
BF16 = mybir.dt.bfloat16

P = 128
B, L, D = 8, 512, 256
H, DH = 16, 16
NC = D // P
NT = L // P
HU = P // DH
NPAIR = HU // 2
NMS = NPAIR * NT
HG = 4
OR = DH + 1
KEEP = max(1, min(L, int(0.6 * L)))
DROP = L - KEEP
ROUNDS = -(-DROP // 8)
PADS = ROUNDS * 8 - DROP
BIG = 3.0e38
GONE = -3.2e38
LN_EPS = 1e-5
QS = 0.25
PASSES = ((0, 0), (0, 1), (1, 0))
VZ_STRIDE = 1160
PT_BUFS = 4
DVE_LINKS = 18
DVE_LINKS_B = 50

TASKS = [["V", "X0", "X1", "Q", "K", "O0", "mean", "mx", "O1"],
         ["V", "Q", "K", "O0", "mean", "mx", "O1"]]
TASKS_FIRST = ["X0", "X1", "Q0", "K0", "mean0", "V", "Q1", "K1", "mean1", "mx"]
AT = {"V": 1, "X0": 3, "X1": 4, "Q": 6, "K": 7, "O0": 8, "mean": 9, "mx": 12, "O1": 15}
SCORES_AT = ["ac", "c", "b"] * 4 + [""] * 4
assert sum(map(len, SCORES_AT)) == NMS


def tasks_of(b_last, g):
    if not b_last:
        return TASKS[g]
    return [t for t in TASKS[g] if t in (("V", "O0", "mx", "O1") if g == 0 else ("O0", "O1"))]


def per_batch(kinds):
    return sum(t in kinds for g in (0, 1) for t in TASKS[g])


def constant_wait(eng, const):
    eng.wait_ge(const["ready"], const["count"])


class Link:

    def __init__(self, eng, sem, const):
        self.eng, self.sem, self.const, self.base, self.n = eng, sem, const, 0, 0

    def __call__(self, ins, alone=False):
        ins.then_inc(self.sem, 1)
        self.n += 1
        self.eng.wait_ge(self.sem, self.base + self.n)
        if alone:
            tiny = self.const["tiny"]
            self.eng.tensor_copy(tiny[:, 1:2], tiny[:, 0:1])

    def enter(self, i, per):
        self.start, self.per = self.n + self.base, per
        self.base, self.n = self.start + per * i, 0

    def leave(self, times):
        assert self.n == self.per, (self.n, self.per)
        self.base, self.n = self.start + self.per * times, 0


def attention(nc, ctx, dram, sb, ps, sem, const):
    xT = sb("xT", [P, NC, L], F32)
    q_st = [sb(f"q_st{i}", [P, NPAIR, L], F32R) for i in range(2)]
    k_st = [sb(f"k_st{i}", [P, NPAIR, L], F32R) for i in range(2)]
    qk_hi = [sb(n, [P, L], F32R) for n in ("q_hi", "k_hi")]
    qk_lo = [sb(n, [P, L], F32R) for n in ("q_lo", "k_lo")]

    def parts_of(w):
        return (first[0:2], first[2:4]) if isinstance(w, int) and w == 1 else (qk_hi, qk_lo)

    vz = [sb(f"vz{i}", [P, NT, VZ_STRIDE], F32) for i in range(2)]
    pT = [sb(f"pT{i}", [P, 2, L], F32) for i in range(PT_BUFS)]
    oT = [sb(f"oT{i}", [P, L], F32) for i in range(2)]
    mean_sb = [sb(f"mean{i}", [HU, L], F32) for i in range(2)]
    m_hi = sb("m_hi", [HU, L], F32R)
    m_lo = sb("m_lo", [HU, L], F32R)
    sp_u = sb("sp_u", [HU, L], F32)
    w_q = [sb(f"wq_a{i}", [P, NC, D], F32R) for i in range(2)]
    w_k = [sb(f"wk_a{i}", [P, NC, D], F32R) for i in range(2)]
    w_v = sb("wv_a", [P, NC, D], F32)
    x_in = sb("x_in", [P, NT, D], F32)
    with ExitStack() as own:
        own.enter_context(nc.sbuf_tensor("oa_first", [P, 2 * NT, D], F32))
        first = [own.enter_context(nc.sbuf_tensor(f"first{n}", [P, L], F32R)) for n in range(4)]
    oa = sb("oa", [P, B * NT, D], F32)
    xn = sb("xn", [P, NT, D], F32)
    xT_hi = sb("xT_hi", [P, NC, L], F32R)
    xT_lo = sb("xT_lo", [P, NC, L], F32R)
    xT_parts = (xT_hi, xT_lo)
    mx = sb("mx", [P, NT, HU], F32)
    ksum = sb("ksum", [P, 2], F32)
    kmean = sb("kmean", [P, HU], F32)
    kmean_w = [sb(f"kmean_w{i}", [P, P], F32R) for i in range(2)]
    spars = sb("spars", [P, L], F32)
    race = sb("race", [P, PADS + L], F32)
    top8 = sb("top8", [P, 8], F32)
    sel = sb("sel", [P, L], F32)
    selT = sb("selT", [P, NT, P], F32)
    rden = sb("rden", [P, NT, HG], F32)
    stat = sb("stat", [P, NT, 6], F32)
    mv = sb("mv", [P, NT, 2], F32)
    ve = sb("ve", [P, NT], F32)
    rstd = sb("rstd", [P, NT], F32)
    stage = [oa[:, NC * n:NC * (n + 1), :] for n in range(3)]
    w_o = [sb(f"wo_a{i}", [P, NC, D], F32R) for i in range(2)]
    bq = sb("bq", [P, NC], F32)
    bk = sb("bk", [P, NC], F32)
    bkL = sb("bkL", [P, NC], F32)
    bv_all = sb("bv_all", [P, D], F32)
    bo_all = sb("bo_all", [P, D], F32)
    head_of = sb("head_of", [P, HU], F32)
    ident, minus_half = const["ident"], const["minus_half"]

    bank = [ps[:, k, :] for k in range(8)]
    o_bank, misc = bank[6], bank[7]

    w_in, w_ready = sem("w_in"), sem("w_ready")
    stage_in = [sem(f"stage_in{n}") for n in range(3)]
    x_loaded, x_next, xn_ready = sem("x_loaded"), sem("x_next"), sem("xn_ready")
    var_ready, rstd_ready = sem("var_ready"), sem("rstd_ready")
    xT_ready, xT_split = sem("xT_ready"), sem("xT_split")
    hi_ready, lo_ready = sem("hi_ready"), sem("lo_ready")
    st_in = [sem(f"st_in{j}") for j in range(NPAIR)]
    st_first = [sem(f"st_first{j}") for j in range(NPAIR)]
    kmean_ready, mean_ready = sem("kmean_ready"), sem("mean_ready")
    v_ready = sem("v_ready")
    s_done, max_done = sem("s_done"), sem("max_done")
    sT_done, exp_done, pT_free = sem("sT_done"), sem("exp_done"), sem("pT_free")
    oT_ready = sem("oT_ready")
    task_done, task_free = sem("task_done"), sem("task_free")
    m_ready, m_in, sp_in = sem("m_ready"), sem("m_in"), sem("sp_in")
    sp_out = sem("sp_out")
    sel_ready, selT_done, selT_ready = sem("sel_ready"), sem("selT_done"), sem("selT_ready")
    pool_init, dve_init = sem("pool_init"), sem("dve_init")
    dve_link = sem("dve_link")
    NPRO = len(TASKS_FIRST)
    NTASK = sum(map(len, TASKS))

    def task_no(b, last, g, kind):
        names = [(g_, t) for g_ in (0, 1) for t in tasks_of(last, g_)]
        return NPRO + NTASK * b + names.index((g, kind))

    def sp(eng):
        ld = lambda out, in_, s: eng.dma_start(out, in_).then_inc(s, 16)
        ld(x_in[:, :, :], dram["x"][0].rearrange("(t p) c -> p t c", p=P), x_loaded)
        for n, name in enumerate(("Wq", "Wk", "Wo")):
            ld(stage[n], dram[name].rearrange("(c p) n -> p c n", p=P), stage_in[n])
        ld(w_v[:, :, :], dram["Wv"].rearrange("(c p) n -> p c n", p=P), w_in)
        ld(bv_all[:, :], dram["bv"].partition_broadcast(P), w_in)
        ld(bo_all[:, :], dram["bo"].partition_broadcast(P), w_in)

        def stack(w, pairs, buf):
            hi, lo = parts_of(w)
            done = st_first if isinstance(w, int) and w == 0 else st_in
            for j in pairs:
                for parts, dst in (((hi[0], hi[0], lo[0]), q_st[buf]),
                                   ((hi[1], lo[1], hi[1]), k_st[buf])):
                    for r, src in enumerate(parts):
                        for e in range(2):
                            ld(dst[64 * e + DH * r:64 * e + DH * r + DH, j, :].bitcast(F32),
                               src[(2 * j + e) * DH:(2 * j + e + 1) * DH, :].bitcast(F32), done[j])

        def m_rows(w, buf):
            eng.wait_ge(m_ready, w + 1)
            for e in range(2):
                for r, src in enumerate((m_hi, m_lo)):
                    at = 64 * e + 3 * DH + r
                    ld(q_st[buf][at:at + 1, :, :].bitcast(F32), src[e::2, :].bitcast(F32), m_in)
            ld(dram["spars"][bass.ds(w * HU, HU), :], sp_u[:, :], sp_out)

        eng.wait_ge(dve_init, 2)
        for w in range(2):
            if w:
                eng.wait_ge(pool_init, 8)
            eng.wait_ge(lo_ready, 2 * w + 2)
            stack(w, range(NPAIR // 2 if w else NPAIR), w)
        m_rows(0, 0)
        stack(1, range(NPAIR // 2, NPAIR), 1)

        def step(b, g, last):
            u = 2 * b + g
            if not last:
                eng.wait_ge(lo_ready, 2 * (u + 2) + 2)
                eng.wait_ge(sT_done, NMS * u + NMS // 2)
                stack(u + 2, range(NPAIR // 2), g)
            if not (last and g == 1):
                m_rows(u + 1, 1 - g)
            if not last:
                eng.wait_ge(sT_done, NMS * u + NMS)
                stack(u + 2, range(NPAIR // 2, NPAIR), g)

        with eng.Fori(0, B - 1) as b:
            step(b, 0, False)
            step(b, 1, False)
        step(B - 1, 0, True)
        eng.wait_ge(sp_out, 16 * 2 * B)
        ld(spars[:, :], dram["spars"][:, :], sp_in)
        step(B - 1, 1, True)

    def pool(eng):
        g = nc.gpsimd
        g.memset(head_of[:, :], 1.0).then_inc(pool_init, 1)
        eng.wait_ge(pool_init, 1)
        g.affine_select(out=head_of[:, :], in_=head_of[:, :], compare_op=ALU.is_ge, fill=0.0,
                        base=0, pattern=[[-DH, HU]], channel_multiplier=1).then_inc(pool_init, 1)
        eng.wait_ge(pool_init, 2)
        g.affine_select(out=head_of[:, :], in_=head_of[:, :], compare_op=ALU.is_ge, fill=0.0,
                        base=DH - 1, pattern=[[DH, HU]], channel_multiplier=-1).then_inc(pool_init, 1)
        def power(i):
            eng.wait_ge(var_ready, i + 1)
            g.tensor_tensor(rstd[:, :], ve[:, :], minus_half[:, 0:NT], ALU.pow).then_inc(rstd_ready, 1)

        power(0)
        for buf in range(2):
            g.memset(vz[buf][:, :, :], 0.0).then_inc(pool_init, 1)
        eng.wait_ge(pool_init, 5)
        for buf in range(2):
            for gr in range(HU // HG):
                at = gr * HG * P + DH
                ones = vz[buf][:, :, at:at + HG * (P + OR)].rearrange("p t (h c) -> p t h c", c=P + OR)
                last = g.memset(ones[:, :, :, 0:1], 1.0)
        last.then_inc(pool_init, 1)
        g.memset(q_st[1][:, :, :].bitcast(F32), 0.0).then_inc(pool_init, 1)
        g.memset(k_st[1][:, :, :].bitcast(F32), 1.0).then_inc(pool_init, 1)
        with eng.Fori(0, B - 1) as b:
            eng.wait_ge(xn_ready, b + 1)
            g.dma_start(x_in[:, :, :], dram["x_tiles"][:, bass.ts(b + 1, NT), :]).then_inc(x_next, 16)
            power(b + 1)

    def dve(eng):
        v = nc.vector
        link = Link(eng, dve_link, const)
        def layer_norm(i):
            if isinstance(i, int):
                eng.wait_ge(x_loaded, 16)
            else:
                eng.wait_ge(x_next, 16 * i)
            for t in range(NT):
                last = v.bn_stats(stat[:, t, :], x_in[:, t, :])
            link(last, alone=True)
            for t in range(NT):
                last = v.bn_aggr(mv[:, t, :], stat[:, t, :])
            link(last)
            v.tensor_scalar(ve[:, :], mv[:, :, 1], LN_EPS, None, ALU.add).then_inc(var_ready, 1)

        def normalise(i):
            eng.wait_ge(rstd_ready, i + 1)
            for t in range(NT):
                last = v.tensor_scalar(xn[:, t, :], x_in[:, t, :], mv[:, t, 0:1], rstd[:, t:t + 1],
                                       ALU.subtract, ALU.mult)
            last.then_inc(xn_ready, 1)

        def split_x(no, i):
            c = no
            eng.wait_ge(xT_ready, i + 1)
            link(v.tensor_copy(xT_hi[:, c, :], xT[:, c, :]))
            v.tensor_tensor(xT_lo[:, c, :], xT[:, c, :], xT_hi[:, c, :].bitcast(F32),
                            ALU.subtract).then_inc(xT_split, 1)

        def low(which, w, g):
            bias = (bq, bk)[which]
            eng.wait_ge(hi_ready, 2 * w + which + 1)
            hi, lo = parts_of(w)
            v.scalar_tensor_tensor(lo[which][:, :], misc[:, :], bias[:, g:g + 1],
                                   hi[which][:, :].bitcast(F32), ALU.add,
                                   ALU.subtract).then_inc(lo_ready, 1)
            if which == 0:
                return
            link(v.tensor_reduce(ksum[:, 0:1], misc[:, :], AX_X, ALU.add))
            link(v.tensor_tensor(ksum[:, 1:2], ksum[:, 0:1], bkL[:, g:g + 1], ALU.add))
            link(v.tensor_scalar(kmean[:, :], head_of[:, :], ksum[:, 1:2], 1.0 / L, ALU.mult, ALU.mult))
            link(v.tensor_copy(kmean_w[0][:, 0:HU], kmean[:, :]))
            v.tensor_tensor(kmean_w[1][:, 0:HU], kmean[:, :], kmean_w[0][:, 0:HU].bitcast(F32),
                            ALU.subtract).then_inc(kmean_ready, 1)

        def values(g, no):
            eng.wait_ge(task_done, no + 1)
            for gr in range(HU // HG):
                at = gr * HG * P
                out = vz[g][:, :, at:at + HG * (P + OR)].rearrange(
                    "p t (h c) -> p t h c", c=P + OR)[:, :, :, 0:DH]
                cols = slice(gr * HG * DH, (gr + 1) * HG * DH)
                src = misc[:, :].rearrange("p (t c) -> p t c", t=NT)[:, :, cols].rearrange(
                    "p t (h d) -> p t h d", d=DH)
                bias = bv_all[:, g * P:(g + 1) * P][:, cols].rearrange("p (h d) -> p h d", d=DH)
                last = v.tensor_tensor(out, src, bias.unsqueeze(1).to_broadcast([P, NT, HG, DH]), ALU.add)
            return last

        def score_max(n, i):
            j, qt = divmod(i, NT)
            eng.wait_ge(s_done, n + 1)
            v.tensor_reduce(mx[:, qt, 2 * j:2 * j + 2], ps[:, 0:2, :], AX_X, ALU.max).then_inc(max_done, 1)

        def maxima(w, no, par):
            eng.wait_ge(task_done, no + 1)
            if not (isinstance(w, int) and w == 0):
                eng.wait_ge(m_in, 64 * w)
                eng.wait_ge(sp_out, 16 * w)
            link(v.tensor_scalar(m_hi[:, :], misc[0:HU, :], -1.0, None, ALU.mult))
            v.scalar_tensor_tensor(m_lo[:, :], misc[0:HU, :], -1.0, m_hi[:, :].bitcast(F32),
                                   ALU.mult, ALU.subtract)
            eng.wait_ge(mean_ready, w + 1)
            v.tensor_tensor(sp_u[:, :], misc[0:HU, :], mean_sb[par][:, :],
                            ALU.subtract).then_inc(m_ready, 1)

        def outputs(b, g, gr, no):
            eng.wait_ge(task_done, no + 1)
            src = misc[:, 0:NT * HG * OR].rearrange("p (t h c) -> p t h c", t=NT, h=HG)
            link(v.reciprocal(rden[:, :, :], src[:, :, :, DH]))
            at = g * P + gr * HG * DH
            out = oa[:, bass.ts(b, NT), at:at + HG * DH].rearrange("p t (h d) -> p t h d", h=HG)
            v.tensor_tensor(out, src[:, :, :, 0:DH],
                            rden[:, :, :].unsqueeze(3).to_broadcast([P, NT, HG, DH]),
                            ALU.mult).then_inc(task_free, 1)

        def split_weight(n, w, scale):
            eng.wait_ge(stage_in[n], 16)
            link(v.tensor_scalar(w[0][:, :, :], stage[n], scale, None, ALU.mult))
            return v.scalar_tensor_tensor(w[1][:, :, :], stage[n], scale, w[0][:, :, :].bitcast(F32),
                                          ALU.mult, ALU.subtract)

        layer_norm(0)
        v.memset(k_st[0][:, :, :].bitcast(F32), 1.0).then_inc(dve_init, 1)
        normalise(0)
        split_weight(0, w_q, QS)
        eng.wait_ge(w_in, 16 * 5)
        v.tensor_scalar(bkL[:, :], bk[:, :], float(L), None, ALU.mult)
        v.tensor_scalar(bq[:, :], bq[:, :], QS, None, ALU.mult).then_inc(w_ready, 1)
        split_x(0, 0)
        split_x(1, 1)
        split_weight(1, w_k, 1.0).then_inc(w_ready, 1)
        v.memset(q_st[0][:, :, :].bitcast(F32), 0.0).then_inc(dve_init, 1)
        for t in kmean_w:
            v.memset(t[:, :].bitcast(F32), 0.0)
        eng.wait_ge(pool_init, 3)
        low(0, 0, 0)
        low(1, 0, 0)
        v.memset(rden[:, :, :], 1.0).then_inc(pT_free, PT_BUFS)
        v.memset(mean_sb[1][:, :], 0.0).then_inc(exp_done, 1)
        v.memset(m_hi[:, :].bitcast(F32), 0.0).then_inc(oT_ready, 1)
        v.memset(sp_u[:, :], 0.0).then_inc(task_free, 1)
        v.memset(race[:, 0:PADS], BIG)
        eng.wait_ge(pool_init, 6)
        values(0, TASKS_FIRST.index("V")).then_inc(v_ready, 1)
        low(0, 1, 1)
        low(1, 1, 1)
        for i in range(NMS):
            score_max(i, i)
        split_weight(2, w_o, 1.0)
        maxima(0, TASKS_FIRST.index("mx"), 0)

        def step(b, g, last):
            u = 2 * b + g
            n = 0
            todo = tasks_of(last, g)
            for m in range(NMS):
                scores = 0 if last and g == 1 else len(SCORES_AT[m])
                if last and g == 1 and m in (0, AT["O0"] + 1):
                    choose(range(ROUNDS)[:ROUNDS // 2] if m == 0 else range(ROUNDS)[ROUNDS // 2:])
                if scores:
                    score_max(NMS * (u + 1) + n, n)
                if not last and g == 0 and m == 0:
                    layer_norm(b + 1)
                if not last and g == 0 and m == 1:
                    normalise(b + 1)
                for t in todo:
                    if AT[t] != m:
                        continue
                    no = task_no(b, last, g, t)
                    if t == "V":
                        values(1 - g, no).then_inc(v_ready, 1)
                    elif t[0] == "X":
                        split_x(int(t[1]), 2 * (b + 1) + int(t[1]))
                    elif t in "QK":
                        low("QK".index(t), u + 2, g)
                    elif t[0] == "O":
                        outputs(b, g, int(t[1]), no)
                    elif t == "mx":
                        maxima(u + 1, no, 1 - g)
                if scores == 2:
                    score_max(NMS * (u + 1) + n + 1, n + 1)
                n += scores

        def choose(rounds):
            if rounds[0] == 0:
                eng.wait_ge(sp_in, 16)
                link(v.tensor_scalar(race[:, PADS:], spars[:, ::-1], -1.0, None, ALU.mult))
            for _ in rounds:
                link(v.max(top8[:, :], race[:, :]))
                link(v.match_replace(race[:, :], top8[:, :], race[:, :], GONE))
            if rounds[-1] == ROUNDS - 1:
                v.tensor_scalar(sel[:, :], race[:, PADS:][:, ::-1], GONE, None,
                                ALU.not_equal).then_inc(sel_ready, 1)

        with eng.Fori(0, B - 1) as b:
            link.enter(b, DVE_LINKS)
            step(b, 0, False)
            step(b, 1, False)
            link.leave(B - 1)
        step(B - 1, 0, True)
        step(B - 1, 1, True)

        eng.wait_ge(selT_done, 1)
        v.tensor_copy(selT[:, :, :], bank[0][:, :].rearrange("p (t r) -> p t r", t=NT)).then_inc(selT_ready, 1)
        return link

    def act(eng):
        a = nc.scalar
        a.dma_start(bq[:, :], dram["bq"]).then_inc(w_in, 16)
        a.dma_start(bk[:, :], dram["bk"]).then_inc(w_in, 16)

        def x_out(c, no):
            eng.wait_ge(task_done, no + 1)
            a.activation(xT[:, c, :], misc[:, :], ACT.Copy).then_inc(xT_ready, 1)

        def high(which, w, g, no):
            bias = (bq, bk)[which]
            eng.wait_ge(task_done, no + 1)
            if which == 0 and not isinstance(w, int):
                for j in range(NPAIR):
                    eng.wait_ge(st_in[j], 16 * 12 * (w - 1))
            a.activation(parts_of(w)[0][which][:, :], misc[:, :], ACT.Identity,
                         bias=bias[:, g:g + 1]).then_inc(hi_ready, 1)

        def mean_out(par, no):
            eng.wait_ge(task_done, no + 1)
            a.activation(mean_sb[par][:, :], misc[0:HU, :], ACT.Copy).then_inc(mean_ready, 1)

        def o_out(u, gr):
            eng.wait_ge(pT_free, PT_BUFS + NMS * u + NMS // 2 * (gr + 1))
            a.activation(oT[gr][:, :], o_bank[:, :], ACT.Copy).then_inc(oT_ready, 1)

        def exps(u, m):
            n = NMS * u + m
            eng.wait_ge(sT_done, n + 1)
            eng.wait_ge(pT_free, n + 1)
            a.activation(pT[m % PT_BUFS][:, :, :], ps[:, 2 + 2 * (m % 2):4 + 2 * (m % 2), :],
                         ACT.Exp).then_inc(exp_done, 1)

        x_out(0, 0)
        x_out(1, 1)
        eng.wait_ge(w_ready, 1)
        for w in range(2):
            high(0, w, w, TASKS_FIRST.index(f"Q{w}"))
            high(1, w, w, TASKS_FIRST.index(f"K{w}"))
            mean_out(w, TASKS_FIRST.index(f"mean{w}"))

        def step(b, g, last):
            u = 2 * b + g
            todo = tasks_of(last, g)
            for m in range(NMS):
                exps(u, m)
                for t in todo:
                    if AT[t] != m:
                        continue
                    no = task_no(b, last, g, t)
                    if t[0] == "X":
                        x_out(int(t[1]), no)
                    elif t in "QK":
                        high("QK".index(t), u + 2, g, no)
                    elif t == "mean":
                        mean_out(g, no)
                    elif t[0] == "O":
                        o_out(u, int(t[1]))

        with eng.Fori(0, B - 1) as b:
            step(b, 0, False)
            step(b, 1, False)
        step(B - 1, 0, True)
        step(B - 1, 1, True)

    def pe(eng):
        t_ = nc.tensor

        def x_task(c):
            for t in range(NT):
                last = t_.transpose(misc[:, t * P:(t + 1) * P], xn[:, t, c * P:(c + 1) * P], ident[:, :])
            last.then_inc(task_done, 1)

        def qk_task(which, g):
            w = (w_q, w_k)[which]
            n = 0
            for c in range(NC):
                for i, k in PASSES:
                    last = t_.matmul(misc[:, :], w[i][:, c, g * P:(g + 1) * P], xT_parts[k][:, c, :],
                                     start=n == 0, stop=n == NC * len(PASSES) - 1)
                    n += 1
            last.then_inc(task_done, 1)

        def v_task(g):
            for t in range(NT):
                for c in range(NC):
                    last = t_.matmul(misc[:, t * P:(t + 1) * P], xT[:, c, t * P:(t + 1) * P],
                                     w_v[:, c, g * P:(g + 1) * P], start=c == 0, stop=c == NC - 1)
            last.then_inc(task_done, 1)

        def mean_task(w):
            for n, (i, k) in enumerate(PASSES):
                last = t_.matmul(misc[:, :], kmean_w[i][:, :], parts_of(w)[k][0][:, :],
                                 start=n == 0, stop=n == len(PASSES) - 1)
            last.then_inc(task_done, 1)

        def mx_task():
            for t in range(NT):
                last = t_.transpose(misc[0:HU, t * P:(t + 1) * P], mx[:, t, :], ident[:, :])
            last.then_inc(task_done, 1)

        def o_task(gr):
            n = HG * OR
            for t in range(NT):
                last = t_.transpose(misc[:, t * n:(t + 1) * n], oT[gr][0:n, t * P:(t + 1) * P],
                                    ident[0:n, 0:n])
            last.then_inc(task_done, 1)

        def scores(n, i, buf):
            j, qt = divmod(i, NT)
            if not (isinstance(n, int) and n == 0):
                eng.wait_ge(max_done, n)
            for e in range(2):
                last = t_.matmul(bank[e][:, :],
                                 q_st[buf][64 * e:64 * e + 3 * DH, j, qt * P:(qt + 1) * P],
                                 k_st[buf][64 * e:64 * e + 3 * DH, j, :], start=True, stop=True)
            last.then_inc(s_done, 1)

        def scores_T(m, buf):
            j, kt = divmod(m, NT)
            for e in range(2):
                last = t_.matmul(bank[2 + 2 * (m % 2) + e][:, :],
                                 k_st[buf][64 * e:64 * e + 64, j, kt * P:(kt + 1) * P],
                                 q_st[buf][64 * e:64 * e + 64, j, :], start=True, stop=True)
            last.then_inc(sT_done, 1)

        def product(m, g, e):
            j, kt = divmod(m, NT)
            half = NMS // 2
            h = 2 * j + e
            ins = t_.matmul(o_bank[:, :], vz[g][:, kt, h * P:(h + 1) * P], pT[m % PT_BUFS][:, e, :],
                            start=m % half == 0 and e == 0, stop=m % half == half - 1 and e == 1)
            if e:
                ins.then_inc(pT_free, 1)

        eng.wait_ge(const["ready"], const["count"])
        eng.wait_ge(xn_ready, 1)
        x_task(0)
        eng.wait_ge(xT_ready, 1)
        x_task(1)
        eng.wait_ge(xT_ready, 2)
        eng.wait_ge(w_ready, 1)
        eng.wait_ge(xT_split, 2)
        qk_task(0, 0)
        eng.wait_ge(w_ready, 2)
        eng.wait_ge(lo_ready, 1)
        qk_task(1, 0)
        eng.wait_ge(kmean_ready, 1)
        mean_task(0)
        eng.wait_ge(mean_ready, 1)
        v_task(0)
        eng.wait_ge(v_ready, 1)
        qk_task(0, 1)
        eng.wait_ge(lo_ready, 3)
        qk_task(1, 1)
        eng.wait_ge(kmean_ready, 2)
        mean_task(1)
        for i in range(NMS):
            if i % NT == 0:
                eng.wait_ge(st_first[i // NT], 16 * 12)
            scores(i, i, 0)
        eng.wait_ge(mean_ready, 2)
        eng.wait_ge(max_done, NMS)
        mx_task()
        eng.wait_ge(m_in, 64)
        scores_T(0, 0)

        def step(b, g, last):
            u = 2 * b + g
            n = 0
            todo = tasks_of(last, g)
            for m in range(NMS):
                at = "" if last and g == 1 else SCORES_AT[m]
                n = next_scores(u, g, n, "a" in at)
                if m < NMS - 1:
                    eng.wait_ge(exp_done, NMS * u + m + 1)
                    scores_T(m + 1, g)
                elif not (last and g == 1):
                    eng.wait_ge(exp_done, NMS * u + m + 1)
                    eng.wait_ge(m_in, 64 * (u + 2))
                    scores_T(0, 1 - g)
                if m != NMS - 1:
                    for t in todo:
                        if AT[t] == m:
                            task(b, last, g, t)
                eng.wait_ge(exp_done, NMS * u + m + 2)
                if m == 0:
                    eng.wait_ge(v_ready, u + 1)
                if m % (NMS // 2) == 0:
                    eng.wait_ge(oT_ready, 2 * u + m // (NMS // 2) + 1)
                n = next_scores(u, g, n, "b" in at)
                product(m, g, 0)
                n = next_scores(u, g, n, "c" in at)
                product(m, g, 1)
                if m == NMS - 1:
                    task(b, last, g, "O1")

        def next_scores(u, g, n, now):
            if not now:
                return n
            if n % NT == 0:
                eng.wait_ge(st_in[n // NT], 16 * 12 * (u + 1))
            scores(NMS * (u + 1) + n, n, 1 - g)
            return n + 1

        def task(b, last, g, t):
            u = 2 * b + g
            todo = tasks_of(last, g)
            at = todo.index(t)
            prev = todo[at - 1] if at else "O1"
            if prev[0] == "O":
                eng.wait_ge(task_free, 2 * u + (2 if at else 1))
            elif prev == "V":
                eng.wait_ge(v_ready, u + 2)
            elif prev == "X0":
                eng.wait_ge(xT_ready, 2 * (b + 1) + 1)
            elif prev == "X1":
                eng.wait_ge(xT_ready, 2 * (b + 1) + 2)
            elif prev == "Q":
                eng.wait_ge(lo_ready, 2 * (u + 2) + 1)
            elif prev == "K":
                eng.wait_ge(kmean_ready, u + 3)
            elif prev == "mean":
                eng.wait_ge(mean_ready, u + 3)
            elif prev == "mx":
                eng.wait_ge(m_ready, u + 2)
            if t == "V":
                v_task(1 - g)
            elif t[0] == "X":
                if t == "X0":
                    eng.wait_ge(xn_ready, b + 2)
                x_task(int(t[1]))
            elif t in "QK":
                eng.wait_ge(xT_split, 2 * (b + 2))
                qk_task("QK".index(t), g)
            elif t == "mean":
                eng.wait_ge(kmean_ready, u + 3)
                mean_task(u + 2)
            elif t == "mx":
                eng.wait_ge(max_done, NMS * (u + 2))
                mx_task()
            else:
                gr = int(t[1])
                eng.wait_ge(oT_ready, 2 * u + gr + 2)
                o_task(gr)

        eng.wait_ge(m_ready, 1)
        with eng.Fori(0, B - 1) as b:
            step(b, 0, False)
            step(b, 1, False)
        step(B - 1, 0, True)
        step(B - 1, 1, True)
        eng.wait_ge(sel_ready, 1)
        for t in range(NT):
            last = t_.transpose(bank[0][:, t * P:(t + 1) * P], sel[:, t * P:(t + 1) * P], ident[:, :])
        last.then_inc(selT_done, 1)

    return locals()


def project(nc, dram, sb, ps, sem, const, A):
    xi = [A["x_in"], sb("x_in2", [P, NT, D], F32)]
    om = [A["xn"], sb("xn2", [P, NT, D], F32)]
    hi = [A["xT_hi"], sb("xT_hi2", [P, NC, L], F32R)]
    lo = [A["xT_lo"], sb("xT_lo2", [P, NC, L], F32R)]
    oa, selT, bo_all, w_o, ident = A["oa"], A["selT"], A["bo_all"], A["w_o"], const["ident"]
    x_in, x_biased = sem("p_x_in"), sem("p_x_biased")
    masked, tr_done, hi_ready, lo_ready = sem("p_masked"), sem("p_tr_done"), sem("p_hi"), sem("p_lo")
    prod_done, x1_ready, x1_out = sem("p_prod"), sem("p_x1_ready"), sem("p_x1_out")

    def sp(eng):
        with eng.Fori(0, B // 2) as i:
            eng.wait_ge(x1_out, 32 * (i + 1))
            for p in range(2):
                eng.dma_start(xi[p][:, :, :], dram["x_tiles"][:, bass.ts(2 * i + p, NT), :]).then_inc(x_in, 16)
            for p in range(2):
                eng.wait_ge(x1_ready, 2 * i + p + 1)
                eng.dma_start(dram["x1_tiles"][:, bass.ts(2 * i + p, NT), :], xi[p][:, :, :]).then_inc(x1_out, 16)
        eng.wait_ge(x1_out, 32 + 16 * B)

    def dve(eng):
        v = nc.vector
        v.memset(const["tiny"][:, 0:1], 0.0).then_inc(x1_out, 32)
        with eng.Fori(0, B // 2) as i:
            for p in range(2):
                b = 2 * i + p
                v.tensor_tensor(om[p][:, :, :].rearrange("p t (h d) -> p t h d", h=H),
                                oa[:, bass.ts(b, NT), :].rearrange("p t (h d) -> p t h d", h=H),
                                selT[:, :, bass.ts(b, H)].unsqueeze(3).to_broadcast([P, NT, H, DH]),
                                ALU.mult).then_inc(masked, 1)
            for p in range(2):
                b = 2 * i + p
                for c in range(NC):
                    eng.wait_ge(tr_done, NC * b + c + 1)
                    v.tensor_copy(hi[p][:, c, :], ps[:, 2 * p + c, :]).then_inc(hi_ready, 1)
                    eng.wait_ge(hi_ready, NC * b + c + 1)
                    v.tensor_tensor(lo[p][:, c, :], ps[:, 2 * p + c, :], hi[p][:, c, :].bitcast(F32),
                                    ALU.subtract).then_inc(lo_ready, 1)
            for p in range(2):
                b = 2 * i + p
                eng.wait_ge(x_in, 32 * (i + 1))
                v.tensor_tensor(xi[p][:, :, :], xi[p][:, :, :],
                                bo_all[:, :].unsqueeze(1).to_broadcast([P, NT, D]), ALU.add).then_inc(x_biased, 1)
                eng.wait_ge(x_biased, b + 1)
                eng.wait_ge(prod_done, b + 1)
                for k in range(2):
                    rows = xi[p][:, 2 * k:2 * k + 2, :]
                    last = v.tensor_tensor(rows, ps[:, 4 + 2 * p + k, :].rearrange("p (t c) -> p t c", t=2),
                                           rows, ALU.add)
                last.then_inc(x1_ready, 1)

    def pe(eng):
        t_ = nc.tensor
        eng.wait_ge(A["selT_ready"], 1)
        with eng.Fori(0, B // 2) as i:
            for p in range(2):
                eng.wait_ge(masked, 2 * i + p + 1)
                for c in range(NC):
                    for t in range(NT):
                        last = t_.transpose(ps[:, 2 * p + c, t * P:(t + 1) * P],
                                            om[p][:, t, c * P:(c + 1) * P], ident[:, :])
                    last.then_inc(tr_done, 1)
            for p in range(2):
                eng.wait_ge(lo_ready, NC * (2 * i + p + 1))
                for t in range(NT):
                    n = 0
                    for c in range(NC):
                        for a, w in PASSES:
                            last = t_.matmul(ps[:, 4 + 2 * p + t // 2, (t % 2) * D:(t % 2 + 1) * D],
                                             (hi, lo)[a][p][:, c, t * P:(t + 1) * P], w_o[w][:, c, :],
                                             start=n == 0, stop=n == NC * len(PASSES) - 1)
                            n += 1
                last.then_inc(prod_done, 1)

    return locals()


PB = L // 8
NBLK = L // PB
T8 = B
NE, TOPK = 16, 4
HID = 1024
NM = HID // P
OFF = 2.0 ** 100
UNDER = -103.0
RMS_EPS = 1e-6
GATE_TEMP = 16.0
NOUT = 9


def steps(name, n):
    return [f"{name}{k}" for k in range(n)]


STREAM0 = ["f0.ln", "f0.T", "f0.rt", "f0.lg", "f0.mk", *steps("f0.m", 8), "f0.end", "z.ln", "z.rms", "z.T",
           *steps("z.o", NOUT), *steps("rec", T8), "og", "o.mean", "o.ln", "o.T", "o.wo", "o.rms", "o.x"]
STREAM1 = ["g.T", *steps("g.m", 8), "g.end", "f1.ln", "f1.T", "f1.rt", "f1.lg", "f1.mk", *steps("f1.m", 8), "f1.end"]
MERGED = ["g.T", "g.m0", "f0.ln", "g.m1", "f0.T", "g.m2", "f0.rt", "f0.lg", "g.m3", "f0.mk", "f0.m0", "f0.m1",
          "f0.m2", "f0.m3", "f0.m4", "f0.m5", "f0.m6", "f0.m7", "f0.end", "g.m4", "z.ln", "g.m5", "g.m6",
          "z.rms", "g.m7", "z.T", "g.end", "f1.ln", "z.o0", "z.o1", "z.o2", "z.o3", "z.o4", "f1.T", "z.o5",
          "z.o6", "f1.rt", "f1.lg", "z.o7", "z.o8", "f1.mk", "rec0", "rec1", "f1.m0", "rec2", "f1.m1", "rec3",
          "rec4", "f1.m2", "rec5", "f1.m3", "rec6", "rec7", "og", "o.mean", "f1.m4", "o.ln", "f1.m5", "o.T",
          "f1.m6", "o.wo", "f1.m7", "o.rms", "f1.end", "o.x"]
assert [n for n in MERGED if n in STREAM0] == STREAM0 and [n for n in MERGED if n not in STREAM0] == STREAM1


def block_part(nc, dram, sb, ps, sem, const):
    ident, minus_half, plus_half = const["ident"], const["minus_half"], const["plus_half"]
    def two(name, shape):
        return [sb(f"{name}{i}", shape, F32R) for i in range(2)]

    w1, w2 = two("w1", [P, NC, HID]), two("w2", [P, NM, D])
    w_gate, w_up, w_down = two("w_gate", [P, NC, HID]), two("w_up", [P, NC, HID]), two("w_down", [P, NM, D])
    w_q, w_k, w_v, w_og, w_o = (two(n, [P, NC, D]) for n in ("wq_b", "wk_b", "wv_b", "wog_b", "wo_b"))
    w_r, w_g1, w_g2 = two("w_r", [P, NC, P]), two("w_g1", [P, NC, P]), two("w_g2", [P, D])
    qT, kT, vT = (sb(n, [P, NC, L], F32) for n in ("qT", "kT", "vT"))
    b1, bg2, s1, s2 = sb("b1", [P, NM], F32), sb("bg2", [P, NC], F32), sb("s1", [P, NC], F32), sb("s2", [P, NC], F32)
    rb, bg1 = sb("rb", [NE, 1], F32), sb("bg1", [NE, 1], F32)
    b2_all, bog_all = sb("b2_all", [P, D], F32), sb("bog_all", [P, D], F32)
    head_sum = sb("head_sum", [P, P], F32)
    expand = sb("expand", [P, HID], BF16)
    x = [sb(f"x{s}", [P, NT, D], F32) for s in range(2)]
    tok = [sb(f"tok{s}", [P, NT, D], F32) for s in range(2)]
    xT = [two(f"xT_b{s}", [P, NC, L]) for s in range(2)]
    hf = [[sb(f"hf{s}{k}", [P, L], F32) for k in range(2)] for s in range(2)]
    h = [[[sb(f"h{s}{k}{a}", [P, L], F32R) for a in range(2)] for k in range(2)] for s in range(2)]
    maskT = [sb(f"maskT{s}", [P, L], BF16) for s in range(2)]
    logT = [hf[s][1][0:NE, :] for s in range(2)]
    lg = [sb(f"lg{s}", [P, NT, TOPK + NE], F32) for s in range(2)]
    lg_out = [sb(f"lg_out{s}", [P, NT, TOPK + NE], F32) for s in range(2)]
    top8 = [sb(f"top8_b{s}", [P, NT, 8], F32) for s in range(2)]
    lmax = [sb(f"lmax{s}", [P, NT], F32) for s in range(2)]
    mask = [sb(f"mask{s}", [P, NT, NE], F32) for s in range(2)]
    stat = [sb(f"stat_b{s}", [P, NT, 6], F32) for s in range(2)]
    mv = [sb(f"mv_b{s}", [P, NT, 2], F32) for s in range(2)]
    ve = [sb(f"ve_b{s}", [P, NT], F32) for s in range(2)]
    rstd = [sb(f"rstd_b{s}", [P, NT], F32) for s in range(2)]
    y = sb("y", [P, NT, D], F32)
    oT = sb("oT_b", [P, NC, L], F32)
    sq_rows = oT[:, :, :].rearrange("p a (b c) -> p (a b) c", c=D)
    gT = two("gT", [P, L])
    mu, var, rs = (sb(n, [P, NT * H], F32) for n in ("mu", "var", "rs"))
    rinv = sb("rinv", [P, NT], F32)
    aT = sb("aT", [P, NC, L], F32)
    og = kT[:, :, :].rearrange("p a (b c) -> p (a b) c", c=D)
    pr = [sb(f"pr{c}", [P, L], F32) for c in range(NC)]
    w = hf[0][1]
    stage = [t[:, :, :].rearrange("p a b -> p (a b)") for t in (qT, vT, kT)]

    def site(name, *kinds):
        return {k: sem(f"{name}_{k}") for k in kinds}

    tr_kinds = ("src", "tr", "hi", "lo")
    ffn_kinds = ("dm", "var", "rstd", "biased", "rt", "lt", "lg", "mk", "mt", "mtb", "up", "relu", "hh", "hl", "dn", "out") + tr_kinds
    F = [site("ffn0", *ffn_kinds), site("ffn1", *ffn_kinds)]
    Z = site("z", "var", "rstd", "ss", "rn", "ghs", "out", "cv", "og", "ogb", "ogs", *tr_kinds)
    R = site("rec", "kd", "pr", "hs", "w")
    O = site("o", "os", "ot", "var", "rs", "wo", *tr_kinds)
    G = site("g", "dm", "pd", "xy", "ss", "rn", "gate", "silu", "up", "hh", "hl", "dn", "out", *tr_kinds)
    ACC = [0, 4]
    RING = [2, 6]
    x_in, x_out = sem("b_x_in"), sem("b_x_out")
    stage_in = [sem(f"b_stage_in{k}") for k in range(len(stage))]
    w_cleared = sem("b_w_cleared")
    stage_hi, stage_lo = sem("b_stage_hi"), sem("b_stage_lo")
    small_in, b_init = sem("b_small_in"), sem("b_init")
    b_cleared = sem("b_cleared")
    dve_link = sem("b_dve_link")

    pieces = []
    for name, ws in (("w1", w1), ("w_gate", w_gate), ("w_up", w_up)):
        for c in range(NC):
            pieces.append((dram[name][c * P:(c + 1) * P, :], HID, [t[:, c, :] for t in ws]))
    for name, ws in (("w2", w2), ("w_down", w_down)):
        for k in range(2):
            rows = dram[name][k * NM // 2 * P:(k + 1) * NM // 2 * P, :].rearrange("(m p) n -> p m n", p=P)
            pieces.append((rows, HID, [t[:, k * NM // 2:(k + 1) * NM // 2, :] for t in ws]))
    for name, ws in (("wq", w_q), ("wk", w_k), ("wv", w_v), ("wog", w_og), ("wo", w_o)):
        pieces.append((dram[name].rearrange("(c p) n -> p c n", p=P), NC * D, [t[:, :, :] for t in ws]))
    for name, ws in (("rw", w_r), ("wg1", w_g1)):
        pieces.append((dram[name].rearrange("(c p) n -> p c n", p=P), NC * NE, [t[:, :, 0:NE] for t in ws]))
    pieces.append((dram["wg2"], D, [t[0:NE, :] for t in w_g2]))

    def staged(n):
        src, cols, ws = pieces[n]
        rows = ws[0].shape[0]
        v = stage[n % len(stage)][0:rows, 0:cols]
        if len(ws[0].shape) == 3:
            v = v.rearrange("p (m n) -> p m n", m=ws[0].shape[1])
        return v

    small = [(t[:, :], dram[name]) for name, t in (("b1", b1), ("bg2", bg2), ("s1", s1), ("s2", s2), ("rb", rb), ("bg1", bg1))]
    small += [(t[:, :], dram[name].partition_broadcast(P)) for name, t in (("b2", b2_all), ("bog", bog_all))]
    NSMALL = len(small)

    def weights_act(eng):
        def fetch(n):
            eng.dma_start(staged(n), pieces[n][0]).then_inc(stage_in[n % len(stage)], 16)

        eng.wait_ge(*const["units_done"])
        for n in range(len(stage)):
            fetch(n)
        for out, in_ in small:
            eng.dma_start(out, in_).then_inc(small_in, 16)
        eng.wait_ge(w_cleared, 1)
        for n, (_, _, ws) in enumerate(pieces):
            eng.wait_ge(stage_in[n % len(stage)], 16 * (n // len(stage) + 1))
            nc.scalar.activation(ws[0], staged(n), ACT.Copy).then_inc(stage_hi, 1)
            if n and n - 1 + len(stage) < len(pieces):
                eng.wait_ge(stage_lo, n)
                fetch(n - 1 + len(stage))

    def weights_pool(eng):
        g = nc.gpsimd
        eng.wait_ge(*const["units_done"])
        for t in (*w_r, *w_g1):
            g.memset(t[:, :, :].bitcast(F32), 0.0)
        for t in w_g2:
            last = g.memset(t[:, :].bitcast(F32), 0.0)
        last.then_inc(w_cleared, 1)
        for n, (_, _, ws) in enumerate(pieces):
            eng.wait_ge(stage_hi, n + 1)
            g.tensor_tensor(ws[1], staged(n), ws[0].bitcast(F32), ALU.subtract).then_inc(stage_lo, 1)

    def sp(eng):
        def ld(out, in_, s):
            eng.dma_start(out, in_).then_inc(s, 16)

        eng.wait_ge(*const["a_done"])

        def load(i):
            for e in range(2):
                ld(x[0][e * PB:(e + 1) * PB, :, :], dram["x1_blocks"][e, bass.ts(i, PB), :, :], x_in)

        def store(j):
            eng.wait_ge(F[1]["out"], j + 1)
            for e in range(2):
                ld(dram["out_blocks"][e, bass.ts(j, PB), :, :], tok[0][e * PB:(e + 1) * PB, :, :], x_out)

        load(0)
        with eng.Fori(1, NBLK) as i:
            eng.wait_ge(G["xy"], i)
            load(i)
            store(i - 1)
        store(NBLK - 1)
        eng.wait_ge(x_out, 32 * (NBLK + 1))

    def pool(eng):
        g = nc.gpsimd
        eng.wait_ge(*const["a_done"])
        g.memset(expand[:, :], OFF).then_inc(b_init, 1)
        g.memset(head_sum[:, :], 1.0).then_inc(b_init, 1)
        n = 2
        hs3 = head_sum[:, :].rearrange("p (h d) -> p h d", h=HU)
        for out, base, pattern, mult in (
                (expand[:, :], 0, [[1, HID]], -HID // NE), (expand[:, :], HID // NE - 1, [[-1, HID]], HID // NE),
                (hs3, 0, [[-DH, HU], [0, DH]], 1), (hs3, DH - 1, [[DH, HU], [0, DH]], -1)):
            eng.wait_ge(b_init, n)
            g.affine_select(out=out, in_=out, compare_op=ALU.is_ge, fill=0.0, base=base, pattern=pattern,
                            channel_multiplier=mult).then_inc(b_init, 1)
            n += 1
        def power(src, dst, half, wait, done, i):
            eng.wait_ge(wait, i + 1)
            g.tensor_tensor(dst, src, half, ALU.pow).then_inc(done, 1)

        def std(s, S, i):
            power(ve[s][:, :], rstd[s][:, :], minus_half[:, 0:NT], S["var"], S["rstd"], i)

        def ffn_ln(i, s):
            std(s, F[s], i)
            eng.wait_ge(F[s]["src"], i + 1)
            g.tensor_tensor(x[s][:, :, :], x[s][:, :, :], b2_all[:, :].unsqueeze(1).to_broadcast([P, NT, D]),
                            ALU.add).then_inc(F[s]["biased"], 1)

        def rec(i, t):
            if t == 1:
                eng.wait_ge(Z["cv"], NOUT * (i + 1))
            for c in range(NC):
                eng.wait_ge(R["pr"], 2 * T8 * i + 2 * (t - 1) + c + 1)
                keys = kT[:, c, 0:PB * t].rearrange("p (s n) -> p s n", s=t)
                decay = aT[:, c, PB * t:PB * (t + 1)].unsqueeze(1).to_broadcast([P, t, PB])
                g.tensor_tensor(keys, keys, decay, ALU.mult).then_inc(R["kd"], 1)

        def out_rms(i):
            power(ve[0][:, :], rstd[0][:, :], plus_half[:, 0:NT], G["ss"], G["rn"], i)

        def hand_over(i):
            if not (isinstance(i, int) and i == 0):
                eng.wait_ge(F[1]["out"], i)
            g.tensor_tensor(x[1][:, :, :], x[0][:, :, :], y[:, :, :], ALU.add).then_inc(G["xy"], 1)

        def low_h(i, s, m, S, done):
            eng.wait_ge(S[done], NM * i + m + 1)
            hi, lo = h[s][m % 2]
            g.tensor_tensor(lo[:, :], hf[s][m % 2][:, :], hi[:, :].bitcast(F32), ALU.subtract).then_inc(S["hl"], 1)

        parts = {"f0.ln": lambda i: ffn_ln(i, 0), "f1.ln": lambda j: ffn_ln(j, 1), "z.ln": lambda i: std(0, Z, i),
                 "z.rms": lambda i: power(ve[0][:, :], rstd[0][:, :], plus_half[:, 0:NT], Z["ss"], Z["rn"], i),
                 "o.rms": out_rms, "o.x": hand_over}
        for t in range(T8 - 1):
            parts[f"rec{t}"] = lambda i, t=t: rec(i, t + 1)
        for m in range(NM):
            parts[f"f0.m{m}"] = lambda i, m=m: low_h(i, 0, m, F[0], "relu")
            parts[f"f1.m{m}"] = lambda j, m=m: low_h(j, 1, m, F[1], "relu")
            parts[f"g.m{m}"] = lambda j, m=m: low_h(j, 1, m, G, "hh")
        run(eng, parts)

    def run(eng, parts, link=None, per=0):
        for name in STREAM0:
            if name in parts:
                parts[name](0)
        with eng.Fori(1, NBLK) as i:
            if link:
                link.enter(i - 1, per)
            for name in MERGED:
                if name in parts:
                    parts[name](i if name in STREAM0 else i - 1)
            if link:
                link.leave(NBLK - 1)
        for name in STREAM1:
            if name in parts:
                parts[name](NBLK - 1)

    def dve(eng):
        v = nc.vector
        link = Link(eng, dve_link, const)
        eng.wait_ge(*const["a_done"])
        for t in gT:
            v.memset(t[:, :].bitcast(F32), 0.0)
        for s in range(2):
            v.memset(maskT[s][:, :], 0.0)
            last = v.memset(lg[s][:, :, 0:TOPK], BIG)
        last.then_inc(b_cleared, 1)
        v.memset(const["tiny"][:, 0:1], 0.0).then_inc(x_out, 32)
        eng.wait_ge(small_in, 16 * NSMALL)
        link(v.tensor_scalar(bg2[:, :], bg2[:, :], 1.0 / GATE_TEMP, None, ALU.mult))

        def layer_norm(i, s, out, S):
            for t in range(NT):
                last = v.bn_stats(stat[s][:, t, :], x[s][:, t, :])
            link(last, alone=True)
            for t in range(NT):
                last = v.bn_aggr(mv[s][:, t, :], stat[s][:, t, :])
            link(last)
            v.tensor_scalar(ve[s][:, :], mv[s][:, :, 1], LN_EPS, None, ALU.add).then_inc(S["var"], 1)
            eng.wait_ge(S["rstd"], i + 1)
            for t in range(NT):
                last = v.tensor_scalar(out[:, t, :], x[s][:, t, :], mv[s][:, t, 0:1], rstd[s][:, t:t + 1],
                                       ALU.subtract, ALU.mult)
            return last

        def rms_norm(i, squares, out, S):
            link(v.tensor_tensor(squares, y[:, :, :], y[:, :, :], ALU.mult))
            v.tensor_reduce(ve[0][:, :], squares, AX_X, ALU.add).then_inc(S["ss"], 1)
            eng.wait_ge(S["rn"], i + 1)
            link(v.tensor_scalar(ve[0][:, :], rstd[0][:, :], float(D) ** -0.5, RMS_EPS, ALU.mult, ALU.add))
            link(v.reciprocal(rinv[:, :], ve[0][:, :]))
            for t in range(NT):
                last = v.tensor_scalar(out[:, t, :], y[:, t, :], rinv[:, t:t + 1], None, ALU.mult)
            last.then_inc(S["src"], 1)

        def low(i, s, S, scale=None):
            for c in range(NC):
                eng.wait_ge(S["hi"], NC * i + c + 1)
                v.scalar_tensor_tensor(xT[s][1][:, c, :], ps[:, RING[s] + c, :],
                                       1.0 if scale is None else scale[:, c:c + 1],
                                       xT[s][0][:, c, :].bitcast(F32), ALU.mult, ALU.subtract).then_inc(S["lo"], 1)

        def add_down(i, s, S, out=None):
            out = out or x[s]
            eng.wait_ge(S["dm"], NM * (i + 1))
            for k in range(2):
                rows = x[s][:, 2 * k:2 * k + 2, :]
                last = v.tensor_tensor(out[:, 2 * k:2 * k + 2, :],
                                       ps[:, ACC[s] + k, :].rearrange("p (t c) -> p t c", t=2), rows, ALU.add)
            return last

        def ffn_ln(i, s):
            if s == 0:
                eng.wait_ge(x_in, 32 * (i + 1))
                if not isinstance(i, int):
                    eng.wait_ge(x_out, 32 * i)
            layer_norm(i, s, tok[s], F[s]).then_inc(F[s]["src"], 1)

        def choose(i, s):
            S = F[s]
            eng.wait_ge(S["lg"], i + 1)
            logits = ps[:, RING[s] + 1, 0:NT * NE].rearrange("p (t e) -> p t e", t=NT)
            link(v.tensor_reduce(lmax[s][:, :], logits, AX_X, ALU.max))
            link(v.tensor_tensor(lg[s][:, :, TOPK:], logits, lmax[s][:, :].unsqueeze(2).to_broadcast([P, NT, NE]),
                                 ALU.subtract))
            link(v.tensor_scalar(lg[s][:, :, TOPK:], lg[s][:, :, TOPK:], UNDER, None, ALU.max), alone=True)
            for t in range(NT):
                last = v.max(top8[s][:, t, :], lg[s][:, t, :])
            link(last, alone=True)
            for t in range(NT):
                last = v.match_replace(lg_out[s][:, t, :], top8[s][:, t, :], lg[s][:, t, :], GONE)
            link(last)
            v.tensor_scalar(mask[s][:, :, :], lg_out[s][:, :, TOPK:], GONE, 1.0, ALU.is_equal,
                            ALU.subtract).then_inc(S["mk"], 1)

        def f0_end(i):
            eng.wait_ge(F[0]["biased"], i + 1)
            link(add_down(i, 0, F[0]))

        def g_end(j):
            eng.wait_ge(G["xy"], j + 1)
            link(add_down(j, 1, G))

        def f1_end(j):
            eng.wait_ge(F[1]["biased"], j + 1)
            if isinstance(j, int):
                eng.wait_ge(x_out, 32 * (j + 1))
            add_down(j, 1, F[1], tok[0]).then_inc(F[1]["out"], 1)

        def gate_in(i):
            eng.wait_ge(Z["cv"], NOUT * i + 1)
            g_in = hf[0][0][0:NE, :]
            link(v.tensor_copy(gT[0][0:NE, :], g_in))
            v.tensor_tensor(gT[1][0:NE, :], g_in, gT[0][0:NE, :].bitcast(F32), ALU.subtract).then_inc(Z["ghs"], 1)

        def product(i, s):
            t, c = divmod(s, NC)
            if t:
                eng.wait_ge(R["kd"], 2 * (T8 - 1) * i + s - 1)
            if s >= 2:
                eng.wait_ge(R["hs"], 2 * T8 * i + s - 1)
            v.tensor_tensor(pr[c][:, 0:PB * (t + 1)].rearrange("p (s n) -> p s n", n=PB),
                            kT[:, c, 0:PB * (t + 1)].rearrange("p (s n) -> p s n", n=PB),
                            qT[:, c, PB * t:PB * (t + 1)].unsqueeze(1).to_broadcast([P, t + 1, PB]),
                            ALU.mult).then_inc(R["pr"], 1)

        def rec(i, t):
            if t == 0:
                eng.wait_ge(Z["cv"], NOUT * (i + 1))
                product(i, 0)
            for s in (2 * t, 2 * t + 1):
                if s + 1 < 2 * T8:
                    product(i, s + 1)
                c = s % NC
                eng.wait_ge(R["hs"], 2 * T8 * i + s + 1)
                bank = ps[:, RING[0] + c, 0:PB * (t + 1)]
                out = oT[:, c, PB * t:PB * (t + 1)]
                if t == 0:
                    v.tensor_tensor(out, bank, vT[:, c, 0:PB], ALU.mult).then_inc(R["w"], 1)
                    continue
                v.tensor_tensor(w[:, 0:PB * (t + 1)], bank, vT[:, c, 0:PB * (t + 1)], ALU.mult).then_inc(R["w"], 1)
                eng.wait_ge(R["w"], 2 * T8 * i + s + 1)
                last = v.tensor_reduce(out, w[:, 0:PB * (t + 1)].rearrange("p (s n) -> p n s", n=PB), AX_X, ALU.add)
                if s < 2 * T8 - 1:
                    link(last)
                else:
                    last.then_inc(O["os"], 1)

        def og_out(i):
            eng.wait_ge(O["os"], i + 1)
            for k in range(2):
                eng.wait_ge(Z["og"], 2 * i + k + 1)
                last = v.tensor_tensor(og[:, 2 * k:2 * k + 2, :],
                                       ps[:, ACC[0] + k, :].rearrange("p (t c) -> p t c", t=2),
                                       bog_all[:, :].unsqueeze(1).to_broadcast([P, 2, D]), ALU.add)
            last.then_inc(Z["ogb"], 1)

        tokh = tok[0][:, :, :].rearrange("p t (h d) -> p (t h) d", d=DH)

        def o_mean(i):
            for k in range(2):
                eng.wait_ge(O["ot"], 2 * i + k + 1)
                last = v.tensor_reduce(mu[:, 2 * k * H:2 * (k + 1) * H],
                                       ps[:, RING[0] + k, :].rearrange("p (g d) -> p g d", d=DH), AX_X, ALU.add)
            link(last)
            link(v.tensor_scalar(mu[:, :], mu[:, :], 1.0 / DH, None, ALU.mult))
            for k in range(2):
                part = slice(2 * k * H, 2 * (k + 1) * H)
                last = v.tensor_tensor(tokh[:, part, :], ps[:, RING[0] + k, :].rearrange("p (g d) -> p g d", d=DH),
                                       mu[:, part].unsqueeze(2).to_broadcast([P, 2 * H, DH]), ALU.subtract)
            link(last)

        def o_ln(i):
            sqh = sq_rows.rearrange("p t (h d) -> p (t h) d", d=DH)
            link(v.tensor_tensor(sqh, tokh, tokh, ALU.mult))
            link(v.tensor_reduce(var[:, :], sqh, AX_X, ALU.add))
            v.tensor_scalar(var[:, :], var[:, :], 1.0 / DH, LN_EPS, ALU.mult, ALU.add).then_inc(O["var"], 1)
            eng.wait_ge(Z["ogs"], i + 1)
            link(v.tensor_tensor(tok[0][:, :, :], tok[0][:, :, :], og, ALU.mult))
            eng.wait_ge(O["rs"], i + 1)
            link(v.reciprocal(rs[:, :], rs[:, :]))
            link(v.scalar_tensor_tensor(mu[:, :], var[:, :], -0.5, rs[:, :], ALU.mult, ALU.mult))
            link(v.tensor_tensor(mu[:, :], mu[:, :], rs[:, :], ALU.mult))
            link(v.scalar_tensor_tensor(rs[:, :], mu[:, :], 1.5, rs[:, :], ALU.add, ALU.mult))
            v.tensor_tensor(tokh, tokh, rs[:, :].unsqueeze(2).to_broadcast([P, NT * H, DH]),
                            ALU.mult).then_inc(O["src"], 1)

        def o_add(i):
            for k in range(2):
                eng.wait_ge(O["wo"], 2 * i + k + 1)
                rows = y[:, 2 * k:2 * k + 2, :]
                last = v.tensor_tensor(rows, ps[:, ACC[0] + k, :].rearrange("p (t c) -> p t c", t=2), rows, ALU.add)
            link(last)

        def o_rms(i):
            if not (isinstance(i, int) and i == 0):
                eng.wait_ge(F[1]["tr"], NC * i)
            rms_norm(i, sq_rows, tok[1], G)

        def gated(j, m):
            eng.wait_ge(G["silu"], NM * j + m + 1)
            eng.wait_ge(G["up"], NM * j + m + 1)
            buf = hf[1][m % 2][:, :]
            v.tensor_tensor(buf, ps[:, RING[1] + 1, :], buf, ALU.mult).then_inc(G["pd"], 1)
            if m >= 2:
                eng.wait_ge(G["dm"], NM * j + m - 1)
            eng.wait_ge(G["pd"], NM * j + m + 1)
            v.tensor_copy(h[1][m % 2][0][:, :], buf).then_inc(G["hh"], 1)

        parts = {"f0.ln": lambda i: ffn_ln(i, 0), "f0.T": lambda i: low(i, 0, F[0]), "f0.lg": lambda i: choose(i, 0),
                 "f0.end": f0_end, "z.ln": lambda i: link(layer_norm(i, 0, y, Z)),
                 "z.rms": lambda i: rms_norm(i, tok[0][:, :, :], tok[0], Z), "z.T": lambda i: low(i, 0, Z, s1),
                 "z.o0": gate_in, "og": og_out, "o.mean": o_mean, "o.ln": o_ln, "o.T": lambda i: low(i, 0, O),
                 "o.wo": o_add, "o.rms": o_rms, "g.T": lambda j: low(j, 1, G, s2),
                 "g.end": g_end, "f1.ln": lambda j: ffn_ln(j, 1),
                 "f1.T": lambda j: low(j, 1, F[1]), "f1.lg": lambda j: choose(j, 1), "f1.end": f1_end}
        for t in range(T8):
            parts[f"rec{t}"] = lambda i, t=t: rec(i, t)
        for m in range(NM):
            parts[f"g.m{m}"] = lambda j, m=m: gated(j, m)
        eng.wait_ge(b_init, 6)
        eng.wait_ge(b_cleared, 1)
        run(eng, parts, link, DVE_LINKS_B)

    def act(eng):
        a = nc.scalar
        eng.wait_ge(*const["a_done"])
        eng.wait_ge(b_cleared, 1)

        def high(i, s, S, scale=None):
            for c in range(NC):
                eng.wait_ge(S["tr"], NC * i + c + 1)
                out, src = xT[s][0][:, c, :], ps[:, RING[s] + c, :]
                if scale is None:
                    a.activation(out, src, ACT.Copy).then_inc(S["hi"], 1)
                else:
                    a.activation(out, src, ACT.Identity, scale=scale[:, c:c + 1]).then_inc(S["hi"], 1)

        def logits(i, s):
            eng.wait_ge(F[s]["rt"], i + 1)
            a.activation(logT[s], ps[0:NE, RING[s], :], ACT.Identity, bias=rb[:, :]).then_inc(F[s]["lt"], 1)

        def mask_out(i, s):
            eng.wait_ge(F[s]["mt"], i + 1)
            a.activation(maskT[s][0:NE, :], ps[0:NE, RING[s], :], ACT.Copy).then_inc(F[s]["mtb"], 1)

        def relu(i, s, m):
            eng.wait_ge(F[s]["up"], NM * i + m + 1)
            if m >= 2:
                eng.wait_ge(F[s]["hl"], NM * i + m - 1)
            src, bias = ps[:, RING[s] + m % 2, :], b1[:, m:m + 1]
            a.activation(hf[s][m % 2][:, :], src, ACT.Relu, bias=bias)
            if m >= 2:
                eng.wait_ge(F[s]["dm"], NM * i + m - 1)
            a.activation(h[s][m % 2][0][:, :], src, ACT.Relu, bias=bias).then_inc(F[s]["relu"], 1)

        def projection(i, n):
            eng.wait_ge(Z["out"], NOUT * i + n + 1)
            src = ps[:, RING[0] + n % 2, :]
            if n == 0:
                ins = a.activation(hf[0][0][0:NE, :], src[0:NE, :], ACT.Silu, bias=bg1[:, :])
            elif n < 7:
                c, k = divmod(n - 1, 3)
                ins = a.activation((kT, qT, vT)[k][:, c, :], src, ACT.Copy)
            else:
                ins = a.activation(aT[:, n - 7, :], src, ACT.Sigmoid, bias=bg2[:, n - 7:n - 6], scale=1.0 / GATE_TEMP)
            ins.then_inc(Z["cv"], 1)

        def og_silu(i):
            eng.wait_ge(Z["ogb"], i + 1)
            a.activation(og, og, ACT.Silu).then_inc(Z["ogs"], 1)

        def silu(j, m):
            eng.wait_ge(G["gate"], NM * j + m + 1)
            if m >= 2:
                eng.wait_ge(G["hl"], NM * j + m - 1)
            a.activation(hf[1][m % 2][:, :], ps[:, RING[1], :], ACT.Silu).then_inc(G["silu"], 1)

        def deviation(i):
            eng.wait_ge(O["var"], i + 1)
            a.activation(rs[:, :], var[:, :], ACT.Sqrt).then_inc(O["rs"], 1)

        parts = {"z.T": lambda i: high(i, 0, Z, s1), "og": og_silu, "o.ln": deviation, "o.T": lambda i: high(i, 0, O),
                 "g.T": lambda j: high(j, 1, G, s2)}
        for s in range(2):
            parts[f"f{s}.T"] = lambda i, s=s: high(i, s, F[s])
            parts[f"f{s}.rt"] = lambda i, s=s: logits(i, s)
            parts[f"f{s}.mk"] = lambda i, s=s: mask_out(i, s)
            for m in range(NM):
                parts[f"f{s}.m{m}"] = lambda i, s=s, m=m: relu(i, s, m)
        for n in range(NOUT):
            parts[f"z.o{n}"] = lambda i, n=n: projection(i, n)
        for m in range(NM):
            parts[f"g.m{m}"] = lambda j, m=m: silu(j, m)
        eng.wait_ge(b_init, 6)
        eng.wait_ge(small_in, 16 * NSMALL)
        run(eng, parts)

    def pe(eng):
        t_ = nc.tensor

        def transposed(i, s, S):
            eng.wait_ge(S["src"], i + 1)
            for c in range(NC):
                for t in range(NT):
                    last = t_.transpose(ps[:, RING[s] + c, t * P:(t + 1) * P], tok[s][:, t, c * P:(c + 1) * P],
                                        ident[:, :])
                last.then_inc(S["tr"], 1)

        def channels(bank, ws, m, s, close=True):
            n = 0
            for c in range(NC):
                for a, k in PASSES:
                    last = t_.matmul(ps[:, bank, :], ws[a][:, c, m * P:(m + 1) * P], xT[s][k][:, c, :],
                                     start=n == 0, stop=close and n == NC * len(PASSES) - 1)
                    n += 1
            return last

        def rows(ws, done):
            for t in range(NT):
                n = 0
                for c in range(NC):
                    for a, k in PASSES:
                        last = t_.matmul(ps[:, ACC[0] + t // 2, (t % 2) * D:(t % 2 + 1) * D],
                                         xT[0][a][:, c, t * P:(t + 1) * P], ws[k][:, c, :],
                                         start=n == 0, stop=n == NC * len(PASSES) - 1)
                        n += 1
                if t % 2:
                    last.then_inc(done, 1)

        def down(i, s, m, ws, S):
            eng.wait_ge(S["hl"], NM * i + m + 1)
            for t in range(NT):
                for n, (a, k) in enumerate(PASSES):
                    last = t_.matmul(ps[:, ACC[s] + t // 2, (t % 2) * D:(t % 2 + 1) * D],
                                     h[s][m % 2][a][:, t * P:(t + 1) * P], ws[k][:, m, :],
                                     start=m == 0 and n == 0 and t % 2 == 0,
                                     stop=m == NM - 1 and n == len(PASSES) - 1, skip_group_check=True)
            last.then_inc(S["dm"], 1)

        def router(i, s):
            eng.wait_ge(F[s]["lo"], NC * (i + 1))
            channels(RING[s], w_r, 0, s).then_inc(F[s]["rt"], 1)

        def logits(i, s):
            constant_wait(eng, const)
            eng.wait_ge(F[s]["lt"], i + 1)
            for t in range(NT):
                last = t_.transpose(ps[:, RING[s] + 1, t * NE:(t + 1) * NE], logT[s][:, t * P:(t + 1) * P],
                                    ident[0:NE, 0:NE])
            last.then_inc(F[s]["lg"], 1)

        def masks(i, s):
            eng.wait_ge(F[s]["mk"], i + 1)
            for t in range(NT):
                last = t_.transpose(ps[0:NE, RING[s], t * P:(t + 1) * P], mask[s][:, t, :], ident[:, :])
            last.then_inc(F[s]["mt"], 1)

        def ffn(i, s, m):
            if m == 0:
                eng.wait_ge(F[s]["mtb"], i + 1)
            if m >= 2:
                eng.wait_ge(F[s]["relu"], NM * i + m - 1)
            bank = RING[s] + m % 2
            channels(bank, w1, m, s, close=False)
            t_.matmul(ps[:, bank, :], expand[:, m * P:(m + 1) * P], maskT[s][:, :],
                      start=False, stop=True).then_inc(F[s]["up"], 1)
            if m:
                down(i, s, m - 1, w2, F[s])

        outs = [(w_g1, 0)] + [(ws, c) for c in range(NC) for ws in (w_k, w_q, w_v)]

        def projection(i, n):
            if n == 0:
                eng.wait_ge(Z["lo"], NC * (i + 1))
            else:
                if n >= 2:
                    eng.wait_ge(Z["cv"], NOUT * i + n - 1)
            bank = RING[0] + n % 2
            if n < len(outs):
                channels(bank, *outs[n], 0).then_inc(Z["out"], 1)
                return
            eng.wait_ge(Z["ghs"], i + 1)
            c = n - len(outs)
            for k, (a, b) in enumerate(PASSES):
                last = t_.matmul(ps[:, bank, :], w_g2[a][:, c * P:(c + 1) * P], gT[b][:, :],
                                 start=k == 0, stop=k == len(PASSES) - 1)
            last.then_inc(Z["out"], 1)

        def rec(i, t):
            for s in (2 * t, 2 * t + 1):
                c = s % NC
                eng.wait_ge(R["pr"], 2 * T8 * i + s + 1)
                if s >= 2:
                    eng.wait_ge(R["w"], 2 * T8 * i + s - 1)
                t_.matmul(ps[:, RING[0] + c, 0:PB * (t + 1)], head_sum[:, :], pr[c][:, 0:PB * (t + 1)],
                          start=True, stop=True).then_inc(R["hs"], 1)
            if t == T8 - 2:
                rows(w_og, Z["og"])

        def o_back(i):
            eng.wait_ge(O["os"], i + 1)
            for t in range(NT):
                for c in range(NC):
                    at = (t % 2) * D + c * P
                    last = t_.transpose(ps[:, RING[0] + t // 2, at:at + P], oT[:, c, t * P:(t + 1) * P], ident[:, :])
                if t % 2:
                    last.then_inc(O["ot"], 1)

        def o_wo(i):
            eng.wait_ge(O["lo"], NC * (i + 1))
            rows(w_o, O["wo"])

        def gated(j, m):
            if m == 0:
                eng.wait_ge(G["lo"], NC * (j + 1))
            else:
                eng.wait_ge(G["silu"], NM * j + m)
            channels(RING[1], w_gate, m, 1).then_inc(G["gate"], 1)
            if m:
                eng.wait_ge(G["pd"], NM * j + m)
            channels(RING[1] + 1, w_up, m, 1).then_inc(G["up"], 1)
            if m:
                down(j, 1, m - 1, w_down, G)

        parts = {"z.T": lambda i: transposed(i, 0, Z), "o.mean": o_back, "o.T": lambda i: transposed(i, 0, O),
                 "o.wo": o_wo, "g.T": lambda j: transposed(j, 1, G), "g.end": lambda j: down(j, 1, NM - 1, w_down, G)}
        for s in range(2):
            parts[f"f{s}.T"] = lambda i, s=s: transposed(i, s, F[s])
            parts[f"f{s}.rt"] = lambda i, s=s: router(i, s)
            parts[f"f{s}.lg"] = lambda i, s=s: logits(i, s)
            parts[f"f{s}.mk"] = lambda i, s=s: masks(i, s)
            parts[f"f{s}.end"] = lambda i, s=s: down(i, s, NM - 1, w2, F[s])
            for m in range(NM):
                parts[f"f{s}.m{m}"] = lambda i, s=s, m=m: ffn(i, s, m)
        for n in range(NOUT):
            parts[f"z.o{n}"] = lambda i, n=n: projection(i, n)
        for t in range(T8):
            parts[f"rec{t}"] = lambda i, t=t: rec(i, t)
        for m in range(NM):
            parts[f"g.m{m}"] = lambda j, m=m: gated(j, m)
        eng.wait_ge(b_init, 6)
        eng.wait_ge(b_cleared, 1)
        eng.wait_ge(stage_lo, len(pieces))
        run(eng, parts)

    return locals()


def build(nc, dram):
    ctx = ExitStack()
    with ctx:
        sb = lambda name, shape, dt: ctx.enter_context(nc.sbuf_tensor(name, shape, dt))
        sem = lambda name: ctx.enter_context(nc.semaphore(name))
        ps = ctx.enter_context(nc.psum_tensor("ps", [P, 8, 512], F32))
        ident = sb("ident", [P, P], F32)
        minus_half = sb("minus_half", [P, NT * H], F32)
        plus_half = sb("plus_half", [P, NT], F32)
        const_ready = sem("const_ready")
        tiny = sb("tiny", [P, 2], F32)
        const = {"ident": ident, "minus_half": minus_half, "plus_half": plus_half, "ready": const_ready, "count": 5, "tiny": tiny}
        arena = ExitStack()
        sb_a = lambda name, shape, dt: arena.enter_context(nc.sbuf_tensor(name, shape, dt))
        with arena:
            A = attention(nc, ctx, dram, sb_a, ps, sem, const)
            A2 = project(nc, dram, sb_a, ps, sem, const, A)
        const["units_done"] = (A["task_free"], 1 + 2 * 2 * B)
        const["a_done"] = (A2["x1_out"], 32 + 16 * B)
        second = lambda name, shape, dt: ctx.enter_context(nc.sbuf_tensor(name, shape, dt))

        BB = block_part(nc, dram, second, ps, sem, const)
        block = ctx.enter_context(nc.Block())

        @block.sync
        def _(eng):
            A["sp"](eng)
            A2["sp"](eng)
            BB["sp"](eng)

        @block.gpsimd
        def _(eng):
            nc.gpsimd.memset(ident[:, :], 0.0).then_inc(const_ready, 1)
            nc.gpsimd.memset(minus_half[:, :], -0.5).then_inc(const_ready, 1)
            nc.gpsimd.memset(plus_half[:, :], 0.5).then_inc(const_ready, 1)
            nc.gpsimd.memset(tiny[:, :], 0.0).then_inc(const_ready, 1)
            eng.wait_ge(const_ready, 4)
            nc.gpsimd.affine_select(out=ident[:, :], in_=ident[:, :], compare_op=ALU.not_equal, fill=1.0,
                                    base=0, pattern=[[-1, P]], channel_multiplier=1).then_inc(const_ready, 1)
            A["pool"](eng)
            BB["weights_pool"](eng)
            BB["pool"](eng)

        @block.vector
        def _(eng):
            eng.wait_ge(const_ready, const["count"])
            A["dve"](eng)
            eng.wait_ge(A["selT_ready"], 1)
            A2["dve"](eng)
            BB["dve"](eng)

        @block.scalar
        def _(eng):
            A["act"](eng)
            BB["weights_act"](eng)
            BB["act"](eng)

        @block.tensor
        def _(eng):
            A["pe"](eng)
            A2["pe"](eng)
            BB["pe"](eng)



_NAMES = {"x": "L0_attn_a_x", "Wq": "L0_attn_a_Wq", "Wk": "L0_attn_a_Wk", "Wv": "L0_attn_a_Wv", "Wo": "L0_attn_a_Wo",
          "bq": "L0_attn_a_bq", "bk": "L0_attn_a_bk", "bv": "L0_attn_a_bv", "bo": "L0_attn_a_bo",
          "w1": "L0_ffn_w1", "w2": "L0_ffn_w2", "rw": "L0_ffn_router_w", "b1": "L0_ffn_b1", "b2": "L0_ffn_b2",
          "rb": "L0_ffn_router_b", "wq": "L0_attn_b_wq", "wk": "L0_attn_b_wk", "wv": "L0_attn_b_wv",
          "wog": "L0_attn_b_wog", "wo": "L0_attn_b_wo", "wg1": "L0_attn_b_wg1", "wg2": "L0_attn_b_wg2",
          "bg1": "L0_attn_b_bg1", "bg2": "L0_attn_b_bg2", "bog": "L0_attn_b_bog", "s1": "L0_attn_b_scale1",
          "s2": "L0_attn_b_scale2", "w_gate": "L0_attn_b_w_gate", "w_up": "L0_attn_b_w_up", "w_down": "L0_attn_b_w_down"}
_TRANSPOSED = ("w1", "w2", "rw", "wq", "wk", "wv", "wog", "wo", "wg1", "wg2", "w_gate", "w_up", "w_down")
_COLUMNS = ("bq", "bk", "b1", "bg2", "s1", "s2")
_ONE_COLUMN = ("rb", "bg1")


def kernel(**inputs):
    import numpy as _np
    import concourse.bacc as _bacc
    from concourse import mybir as _mybir
    from concourse.bass_utils import run_bass_kernel_spmd as _run

    nc = _bacc.Bacc("TRN2", target_bir_lowering=False, num_devices=1)
    arrays, dram = {}, {}
    for key, name in _NAMES.items():
        a = _np.asarray(inputs[name])
        if key in _TRANSPOSED:
            a = a.T
        elif key in _COLUMNS:
            a = a.reshape(-1, P).T
        elif key in _ONE_COLUMN:
            a = a.reshape(-1, 1)
        a = _np.ascontiguousarray(a)
        arrays[f"in_{key}_dram"] = a
        dram[key] = nc.dram_tensor(f"in_{key}_dram", a.shape, _mybir.dt.from_np(a.dtype), kind="ExternalInput").ap()
    out = nc.dram_tensor("out_dram", (B, L, D), F32, kind="ExternalOutput").ap()
    x1 = nc.dram_tensor("x1_dram", (B, L, D), F32).ap()
    dram["spars"] = nc.dram_tensor("spars_dram", (B * H, L), F32).ap()
    dram["x_tiles"] = dram["x"].rearrange("b (t p) c -> p (b t) c", p=P)
    dram["x1_tiles"] = x1.rearrange("b (t p) c -> p (b t) c", p=P)
    dram["x1_blocks"] = x1.rearrange("(t e) l c -> e l t c", e=2)
    dram["out_blocks"] = out.rearrange("(t e) l c -> e l t c", e=2)
    build(nc, dram)
    r = _run(nc, [arrays], core_ids=[0])
    return r.results[0]["out_dram"]
```
